# Optimizing a Trainium2 kernel written in Bass

```python
import numpy as np
import jax
import jax.numpy as jnp

def _softmax(x, axis=-1):
    return jax.nn.softmax(x, axis=axis)

def _gelu(x):
    return jax.nn.gelu(x, approximate=True)

def _silu(x):
    return jax.nn.silu(x)

def _sigmoid(x):
    return jax.nn.sigmoid(x)

def _layernorm(x, axis=-1, eps=1e-05):
    m = jnp.mean(x, axis=axis, keepdims=True)
    v = jnp.var(x, axis=axis, keepdims=True)
    return (x - m) / jnp.sqrt(v + eps)

def _scatter_add(tgt, idx, src, axis=0):
    return tgt.at[idx].add(src)

def _segment_sum(src, seg, n):
    return jax.ops.segment_sum(src, seg, n)
kernel_name = 'mk_cond_resid_d4_seqx_r2_ed1a04'

def setup_inputs(seed: int=0):
    np.random.seed(seed)
    _w = jnp.asarray

    def _rec_inputs():
        import jax
        import jax.numpy as jnp
        _rk = jax.random.key(seed)
        x = -0.0003929 + 0.9999 * jax.random.normal(jax.random.fold_in(_rk, 1), (2, 2048, 512), jnp.float32)
        _lenS = 2048 - jax.random.randint(jax.random.fold_in(_rk, 7), (2,), 0, max(1, 2048 // 4) + 1, jnp.int32)
        _lenS2 = 2048 - jax.random.randint(jax.random.fold_in(_rk, 8), (2,), 0, max(1, 2048 // 4) + 1, jnp.int32)
        itok_B_0_2 = jax.random.randint(jax.random.fold_in(_rk, 11), (2,), 0, 3, jnp.int32)
        condB_zX = jax.random.uniform(jax.random.fold_in(_rk, 12), (2,), jnp.float32, 0.0, 0.983423)
        condB_zY = jax.random.uniform(jax.random.fold_in(_rk, 13), (2,), jnp.float32, 0.0, 0.979075)
        condB_zR = jax.random.uniform(jax.random.fold_in(_rk, 14), (2,), jnp.float32, 0.0, 0.9968)
        itok_B_0_6 = jax.random.randint(jax.random.fold_in(_rk, 15), (2,), 0, 7, jnp.int32)
        condB_tauraws = -5.74692 + 0.777674 * jax.random.normal(jax.random.fold_in(_rk, 16), (2,), jnp.float32)
        cond_256 = -0.000235209 + 0.019331 * jax.random.normal(jax.random.fold_in(_rk, 17), (2, 128), jnp.float32)
        condB_bn2 = jnp.zeros((2,), jnp.float32)
        cond_1024 = -4.10585e-05 + 0.0199478 * jax.random.normal(jax.random.fold_in(_rk, 19), (2, 512), jnp.float32)
        return (x, itok_B_0_2, condB_zX, condB_zY, condB_zR, itok_B_0_6, condB_tauraws, cond_256, condB_bn2, cond_1024)
    x, itok_B_0_2, condB_zX, condB_zY, condB_zR, itok_B_0_6, condB_tauraws, cond_256, condB_bn2, cond_1024 = _rec_inputs()

    def _L0_cond_setup():
        import jax, jax.numpy as jnp
        import numpy as np
        NEG_INF = -1e+30
        key = jax.random.key(seed)
        k1, k2, k3, k4, k5 = jax.random.split(key, 5)
        B, S, D, A = (16, 512, 512, 128)
        hidden = jax.random.normal(k1, (B, S, D), dtype=jnp.float32)
        W1 = jax.random.normal(k2, (D, A), dtype=jnp.float32) / np.sqrt(D)
        b1 = jax.random.normal(k3, (A,), dtype=jnp.float32) * 0.01
        v = jax.random.normal(k4, (A,), dtype=jnp.float32) / np.sqrt(A)
        prompt_type_ids = jax.random.randint(k5, (B,), 0, 3, dtype=jnp.int32)
        return {'hidden': hidden, 'W1': W1, 'b1': b1, 'v': v, 'prompt_type_ids': prompt_type_ids}
    _L0_cond_all = _L0_cond_setup()
    _L0_cond_in = {k: v for k, v in _L0_cond_all.items() if k in ('W1', 'b1', 'v')}
    del _L0_cond_all

    def _L1_cond_setup():
        import jax, jax.numpy as jnp
        import numpy as np
        key = jax.random.key(seed)
        k1, k2, k3, k4 = jax.random.split(key, 4)
        B, H, W = (64, 512, 512)
        return {'y': jax.random.uniform(k1, (B, H, W), dtype=jnp.float32), 'zX': jax.random.uniform(k2, (B, 1), dtype=jnp.float32), 'zY': jax.random.uniform(k3, (B, 1), dtype=jnp.float32), 'zR': jax.random.uniform(k4, (B, 1), dtype=jnp.float32), 'dx': 1, 'dy': 1}
    _L1_cond_all = _L1_cond_setup()
    _L1_cond_in = {k: v for k, v in _L1_cond_all.items() if k in ()}
    del _L1_cond_all

    def _L2_cond_setup():
        import jax, jax.numpy as jnp
        import numpy as np
        N_PROFILES = 8
        HIDDEN = 512
        BOTTLENECK = 128
        EPS = 1e-05
        key = jax.random.key(seed)
        ks = jax.random.split(key, 8)
        B, S, H, K, P = (16, 1024, HIDDEN, BOTTLENECK, N_PROFILES)
        down_w = jax.random.normal(ks[0], (P, H, K), dtype=jnp.float32) * (1.0 / np.sqrt(H))
        down_b = jax.random.normal(ks[1], (P, K), dtype=jnp.float32) * 0.01
        up_w = jax.random.normal(ks[2], (P, K, H), dtype=jnp.float32) * (1.0 / np.sqrt(K))
        up_b = jax.random.normal(ks[3], (P, H), dtype=jnp.float32) * 0.01
        ln_g = jnp.ones((P, H), dtype=jnp.float32)
        ln_b = jnp.zeros((P, H), dtype=jnp.float32)
        hidden = jax.random.normal(ks[4], (B, S, H), dtype=jnp.float32)
        profile_ids = jax.random.randint(ks[5], (B,), 0, P)
        return {'hidden': hidden, 'profile_ids': profile_ids, 'down_w': down_w, 'down_b': down_b, 'up_w': up_w, 'up_b': up_b, 'ln_g': ln_g, 'ln_b': ln_b}
    _L2_cond_all = _L2_cond_setup()
    _L2_cond_in = {k: v for k, v in _L2_cond_all.items() if k in ('down_w', 'down_b', 'up_w', 'up_b', 'ln_g', 'ln_b')}
    del _L2_cond_all

    def _L3_cond_setup():
        import jax, jax.numpy as jnp
        import numpy as np
        import math
        B, T, E, D = (4, 1024, 512, 4)

        def _tau_init(t):
            a = 0.1 ** (1.0 / max(t - 1, 1))
            tt = -math.log(max(a, 1e-10))
            return math.log(math.exp(tt) - 1 + 1e-10)

        def causal_ema(b, tau_raw):
            alpha = jnp.exp(-jax.nn.softplus(tau_raw)).astype(b.dtype)

            def step(h, bt):
                h = alpha * h + bt
                return (h, h)
            h0 = jnp.zeros((b.shape[0], b.shape[2]), b.dtype)
            _, hs = jax.lax.scan(step, h0, jnp.swapaxes(b, 0, 1))
            return jnp.swapaxes(hs, 0, 1)
        key = jax.random.key(seed)
        ks = jax.random.split(key, 10)
        s = 0.02
        return {'x': jax.random.normal(ks[0], (B, T, E), jnp.float32), 'tau_ctx': jnp.float32(_tau_init(max(T // 2, 4))), 'tau_raws': jnp.array([_tau_init(max(T // 2 ** i, 2)) for i in range(D)], jnp.float32), 'Wg': jax.random.normal(ks[1], (E, 2 * E), jnp.float32) * s, 'bg': jnp.full((E,), -0.5, jnp.float32), 'Wn1': jax.random.normal(ks[2], (E // 4, E), jnp.float32) * s, 'bn1': jnp.zeros((E // 4,), jnp.float32), 'Wn2': jax.random.normal(ks[3], (D, E // 4), jnp.float32) * s, 'bn2': jnp.zeros((D,), jnp.float32), 'blend': jax.random.normal(ks[4], (D, E), jnp.float32) * s, 'Wsoma': jax.random.normal(ks[5], (E, E), jnp.float32) * s, 'bsoma': jnp.zeros((E,), jnp.float32), 'Wtemp': jax.random.normal(ks[6], (E, E), jnp.float32) * s, 'btemp': jnp.zeros((E,), jnp.float32), 'Wout': jax.random.normal(ks[7], (E, E), jnp.float32) * s, 'gamma': jnp.ones((E,), jnp.float32), 'beta': jnp.zeros((E,), jnp.float32)}
    _L3_cond_all = _L3_cond_setup()
    _L3_cond_in = {k: v for k, v in _L3_cond_all.items() if k in ('tau_ctx', 'Wg', 'bg', 'Wn1', 'bn1', 'Wsoma', 'bsoma', 'Wtemp', 'btemp', 'Wout', 'gamma', 'beta')}
    del _L3_cond_all
    return {'x': x, 'itok_B_0_2': itok_B_0_2, 'condB_zX': condB_zX, 'condB_zY': condB_zY, 'condB_zR': condB_zR, 'itok_B_0_6': itok_B_0_6, 'condB_tauraws': condB_tauraws, 'cond_256': cond_256, 'condB_bn2': condB_bn2, 'cond_1024': cond_1024, 'L0_cond_W1': _L0_cond_in['W1'], 'L0_cond_b1': _L0_cond_in['b1'], 'L0_cond_v': _L0_cond_in['v'], 'L2_cond_down_w': _L2_cond_in['down_w'], 'L2_cond_down_b': _L2_cond_in['down_b'], 'L2_cond_up_w': _L2_cond_in['up_w'], 'L2_cond_up_b': _L2_cond_in['up_b'], 'L2_cond_ln_g': _L2_cond_in['ln_g'], 'L2_cond_ln_b': _L2_cond_in['ln_b'], 'L3_cond_tau_ctx': _L3_cond_in['tau_ctx'], 'L3_cond_Wg': _L3_cond_in['Wg'], 'L3_cond_bg': _L3_cond_in['bg'], 'L3_cond_Wn1': _L3_cond_in['Wn1'], 'L3_cond_bn1': _L3_cond_in['bn1'], 'L3_cond_Wsoma': _L3_cond_in['Wsoma'], 'L3_cond_bsoma': _L3_cond_in['bsoma'], 'L3_cond_Wtemp': _L3_cond_in['Wtemp'], 'L3_cond_btemp': _L3_cond_in['btemp'], 'L3_cond_Wout': _L3_cond_in['Wout'], 'L3_cond_gamma': _L3_cond_in['gamma'], 'L3_cond_beta': _L3_cond_in['beta']}

def reference(x, itok_B_0_2, condB_zX, condB_zY, condB_zR, itok_B_0_6, condB_tauraws, cond_256, condB_bn2, cond_1024, L0_cond_W1, L0_cond_b1, L0_cond_v, L2_cond_down_w, L2_cond_down_b, L2_cond_up_w, L2_cond_up_b, L2_cond_ln_g, L2_cond_ln_b, L3_cond_tau_ctx, L3_cond_Wg, L3_cond_bg, L3_cond_Wn1, L3_cond_bn1, L3_cond_Wsoma, L3_cond_bsoma, L3_cond_Wtemp, L3_cond_btemp, L3_cond_Wout, L3_cond_gamma, L3_cond_beta):
    import jax
    import jax.numpy as jnp

    def _L0_cond_ref(hidden, W1, b1, v, prompt_type_ids):
        import jax, jax.numpy as jnp
        import numpy as np
        NEG_INF = -1e+30
        B, S, D = hidden.shape
        attn_in = jnp.tanh(jnp.einsum('bsd,da->bsa', hidden, W1) + b1)
        scores = jnp.einsum('bsa,a->bs', attn_in, v)
        idx = jnp.arange(S)
        j = idx[:, None]
        l = idx[None, :]
        prefix_m = l <= j
        postfix_m = l >= j
        cloze_m = l != j
        pt = prompt_type_ids[:, None, None]
        mask = jnp.where(pt == 0, prefix_m[None], jnp.where(pt == 1, postfix_m[None], cloze_m[None]))
        masked_scores = jnp.where(mask, scores[:, None, :], NEG_INF)
        p = jax.nn.softmax(masked_scores, axis=-1)
        cnt = jnp.sum(mask, axis=-1).astype(hidden.dtype)
        pooled = jnp.einsum('bjl,bld->bjd', p, hidden) / cnt[..., None]
        return pooled

    def _L1_cond_ref(y, zX, zY, zR, dx, dy):
        import jax, jax.numpy as jnp
        import numpy as np
        yp_x = jnp.pad(y, ((0, 0), (0, 0), (1, 1)), mode='reflect')
        lap_x = (yp_x[:, :, :-2] - 2.0 * y + yp_x[:, :, 2:]) / (dx * dx)
        yp_y = jnp.pad(y, ((0, 0), (1, 1), (0, 0)), mode='reflect')
        lap_y = (yp_y[:, :-2, :] - 2.0 * y + yp_y[:, 2:, :]) / (dy * dy)
        du_dt = zX[:, :, None] * lap_x + zY[:, :, None] * lap_y + zR[:, :, None] * y * (1.0 - y)
        return du_dt

    def _L2_cond_ref(hidden, profile_ids, down_w, down_b, up_w, up_b, ln_g, ln_b):
        import jax, jax.numpy as jnp
        import numpy as np
        N_PROFILES = 8
        HIDDEN = 512
        BOTTLENECK = 128
        EPS = 1e-05
        Wd = down_w[profile_ids]
        bd = down_b[profile_ids][:, None]
        Wu = up_w[profile_ids]
        bu = up_b[profile_ids][:, None]
        g = ln_g[profile_ids][:, None]
        b = ln_b[profile_ids][:, None]
        z = jax.nn.relu(jnp.einsum('bsh,bhk->bsk', hidden, Wd) + bd)
        y = hidden + jnp.einsum('bsk,bkh->bsh', z, Wu) + bu
        mu = jnp.mean(y, axis=-1, keepdims=True)
        var = jnp.mean(jnp.square(y - mu), axis=-1, keepdims=True)
        return (y - mu) * jax.lax.rsqrt(var + EPS) * g + b

    def _L3_cond_ref(x, tau_ctx, tau_raws, Wg, bg, Wn1, bn1, Wn2, bn2, blend, Wsoma, bsoma, Wtemp, btemp, Wout, gamma, beta):
        import jax, jax.numpy as jnp
        import numpy as np
        import math
        B, T, E, D = (4, 1024, 512, 4)

        def _tau_init(t):
            a = 0.1 ** (1.0 / max(t - 1, 1))
            tt = -math.log(max(a, 1e-10))
            return math.log(math.exp(tt) - 1 + 1e-10)

        def causal_ema(b, tau_raw):
            alpha = jnp.exp(-jax.nn.softplus(tau_raw)).astype(b.dtype)

            def step(h, bt):
                h = alpha * h + bt
                return (h, h)
            h0 = jnp.zeros((b.shape[0], b.shape[2]), b.dtype)
            _, hs = jax.lax.scan(step, h0, jnp.swapaxes(b, 0, 1))
            return jnp.swapaxes(hs, 0, 1)
        ctx = causal_ema(x, tau_ctx)
        gate_in = jnp.concatenate([x, ctx], axis=-1)
        wg = jax.nn.sigmoid(jnp.einsum('btc,ec->bte', gate_in, Wg) + bg)
        gated = x * wg
        h1 = jax.nn.gelu(jnp.einsum('btc,hc->bth', x, Wn1) + bn1, approximate=False)
        mod = 0.5 + jax.nn.sigmoid(jnp.einsum('bth,dh->btd', h1, Wn2) + bn2)
        traces = jax.vmap(lambda tau, m: causal_ema(gated * m[..., None], tau))(tau_raws, jnp.moveaxis(mod, -1, 0))
        blend_w = jax.nn.softmax(blend, axis=0)
        temporal = jnp.einsum('dbtc,dc->btc', traces, blend_w)
        gate = jax.nn.sigmoid(jnp.einsum('btc,ec->bte', temporal, Wtemp) + btemp)
        soma = jax.nn.gelu(jnp.einsum('btc,ec->bte', x, Wsoma) + bsoma, approximate=False)
        out = jnp.einsum('btc,ec->bte', soma * gate, Wout)
        mu = out.mean(-1, keepdims=True)
        var = out.var(-1, keepdims=True)
        return (out - mu) / jnp.sqrt(var + 1e-05) * gamma + beta
    x = x + _L0_cond_ref(x, L0_cond_W1, L0_cond_b1, L0_cond_v, itok_B_0_2)
    x = x + _L1_cond_ref(x, condB_zX[:, None], condB_zY[:, None], condB_zR[:, None], 1, 1)
    x = x + _L2_cond_ref(x, itok_B_0_6, L2_cond_down_w, L2_cond_down_b, L2_cond_up_w, L2_cond_up_b, L2_cond_ln_g, L2_cond_ln_b)
    x = x + _L3_cond_ref(x, L3_cond_tau_ctx, condB_tauraws, L3_cond_Wg, L3_cond_bg, L3_cond_Wn1, L3_cond_bn1, cond_256, condB_bn2, cond_1024, L3_cond_Wsoma, L3_cond_bsoma, L3_cond_Wtemp, L3_cond_btemp, L3_cond_Wout, L3_cond_gamma, L3_cond_beta)
    return x

_drawn_inputs = setup_inputs


def setup_inputs(seed=0):
    import zlib

    import numpy as np

    out = dict(_drawn_inputs(seed))
    spreads = {'condB_bn2': (0.0, 2.0),
     'L2_cond_ln_g': (1.0, 0.2),
     'L2_cond_ln_b': (0.0, 0.1),
     'L3_cond_bg': (-0.5, 0.6),
     'L3_cond_bn1': (0.0, 2.0),
     'L3_cond_bsoma': (0.0, 0.1),
     'L3_cond_btemp': (0.0, 2.0),
     'L3_cond_gamma': (1.0, 0.2),
     'L3_cond_beta': (0.0, 0.1)}
    factors = {'condB_tauraws': 8.0,
     'cond_256': 4.781,
     'cond_1024': 21.748,
     'L0_cond_W1': 8.0,
     'L0_cond_b1': 200.0,
     'L0_cond_v': 8.0,
     'L2_cond_down_b': 3.479,
     'L3_cond_Wn1': 4.716}
    for name, (base, spread) in spreads.items():
        noise = np.random.default_rng([zlib.crc32(name.encode()), seed]).standard_normal(out[name].shape)
        drawn = base * np.exp(spread * noise) if base else spread * noise
        out[name] = jnp.asarray(drawn.astype(out[name].dtype))
    for name, factor in factors.items():
        out[name] = (out[name] * factor).astype(out[name].dtype)
    return out
```

```python
from contextlib import ExitStack

import concourse.bass as bass
from concourse import mybir

F32 = mybir.dt.float32
F32R = mybir.dt.float32r
I32 = mybir.dt.int32
ALU = mybir.AluOpType
ACT = mybir.ActivationFunctionType
AX = mybir.AxisListType

P = 128
B, T, E = 2, 2048, 512
A = 128
KE = E // P
NT = T // P
GT = 4
GN = GT * P
NG = NT // GT
GROUPS = B * NG
LAST = GROUPS - 1
NEG = -1e30
EPS = 1e-5

N_PARAMS = 16 * 19
POOL_CONST = 17
BLEND_SHIFTED = 6
SETUP_V = 49
S_WLOG, S_BLOG, S_PROB, S_GSUM, STAT = 3, 9, 10, 18, 22
START = 1
Q_CHAIN = 2 + 4 * NG
NBR = [0, 5, 9, 13, 18]


def build_program(nc, x, xT, ptype, zx, zy, zr, profile, tau_raws, wn2, bn2, blend, w1, b1, v,
                  down_w, down_b, up_w, up_b, ln_g, ln_b, tau_ctx, wg, bg, wn1, bn1, wsoma, bsoma,
                  wtemp, btemp, wout, gamma, beta, out):
    ctx = ExitStack()
    with ctx:
        def sb(name, shape, dt=F32, stack=ctx):
            return stack.enter_context(nc.sbuf_tensor(name, shape, dt))

        def sem(name):
            return ctx.enter_context(nc.semaphore(name))

        x2_dram = nc.dram_tensor("x2_scratch", (B * T, E), F32, kind="Internal").ap()

        ident = sb("ident", [P, P])
        consts = sb("consts", [P, 4])
        taus = sb("taus", [P, 3])
        alpha = sb("alpha", [P, 3])
        blend_sb = sb("blend_sb", [P, 2, KE])
        blend_w = sb("blend_w", [P, 2, KE])
        blend_t = sb("blend_t", [P, 3, KE])
        bias_g = sb("bias_g", [P, KE])
        bias_soma = sb("bias_soma", [P, KE])
        bias_temp = sb("bias_temp", [P, KE])
        bias_n1 = sb("bias_n1", [P, 1])
        bias_n2 = sb("bias_n2", [P, 2])
        cols_all = sb("cols_all", [P, B, 1 + KE])
        cols = sb("cols", [P, 1 + KE])
        ids = sb("ids", [1, B], I32)
        wn2_rep = sb("wn2_rep", [P, 2, P])
        wn2_col = sb("wn2_col", [P, 2])
        gamma_row = sb("gamma_row", [P, E])
        ln_g_row = sb("ln_g_row", [P, B, E])
        shift_row = sb("shift_row", [P, B, E])
        bu_hl = sb("bu_hl", [2, B, E], F32R)
        ones2 = sb("ones2", [2, P], F32R)
        wg_h = sb("wg_h", [P, 2 * KE, E], F32R)
        wg_l = sb("wg_l", [P, 2 * KE, E], F32R)
        wn1_h = sb("wn1_h", [P, KE, A], F32R)
        wn1_l = sb("wn1_l", [P, KE, A], F32R)
        ws_h = sb("ws_h", [P, KE, E], F32R)
        ws_l = sb("ws_l", [P, KE, E], F32R)
        wt_h = sb("wt_h", [P, KE, E], F32R)
        wt_l = sb("wt_l", [P, KE, E], F32R)
        wo_h = sb("wo_h", [P, KE, E], F32R)
        wo_l = sb("wo_l", [P, KE, E], F32R)

        bank = [ctx.enter_context(nc.psum_tensor(f"bank{i}", [P, 512], F32)) for i in range(8)]

        params_in = sem("params_in")

        NEG_HALF, HALF, EPSILON, ONE = (consts[:, i:i + 1] for i in range(4))

        def f32(t):
            return t.bitcast(F32)

        s1 = ExitStack()
        with s1:
            def sb1(name, shape, dt=F32):
                return sb(name, shape, dt, s1)

            xb = sb1("xb", [P, NT, E])
            xt = sb1("xt", [P, 2, KE, GN])
            w1_sb = sb1("w1_sb", [P, KE, A])
            b1_sb = sb1("b1_sb", [P, 1])
            v_sb = sb1("v_sb", [P, 1])
            v_rep = sb1("v_rep", [P, P])
            ones = sb1("ones", [P, P])
            hid = sb1("hid", [P, 2, GN])
            s_row = sb1("s_row", [P, NT, P])
            prob = sb1("prob", [P, NT, P])
            probT = sb1("probT", [P, 2, GT, P])
            bmax = sb1("bmax", [P, NT])
            imax = sb1("imax", [P, NT])
            omax = sb1("omax", [P, NT])
            rmax = sb1("rmax", [P, NT])
            wlog = sb1("wlog", [P, NT])
            wcol = sb1("wcol", [P, NT])
            blog = sb1("blog", [P, NT, NT])
            bexp = sb1("bexp", [P, NT, 32])
            bwz = sb1("bwz", [P, NT, NT])
            bwT = sb1("bwT", [P, GT, P])
            zin = sb1("zin", [P, NT])
            zout = sb1("zout", [P, NT])
            zblk = sb1("zblk", [P, NT])
            rnorm = sb1("rnorm", [P, NT])
            gT = sb1("gT", [P, KE, GT, 32])
            g4 = sb1("g4", [P, E])
            upb = sb1("upb", [P, GT, E])
            dnb = sb1("dnb", [P, GT, E])
            dbuf = s_row[:].rearrange("p (g c) l -> p g (c l)", g=GT)
            qbuf = xt
            stage = dnb
            beta_row = g4
            bu_f = upb[0:1, 0:B]
            bu_l = upb[0:1, 0:B].bitcast(F32R)
            bu_h = upb[0:1, B:2 * B].bitcast(F32R)
            flat_prob = prob[:].rearrange("p c l -> p (c l)")
            hidden_m = flat_prob[:, 0:3 * P].rearrange("p (m l) -> p m l", m=3)
            hidden_b = flat_prob[:, 3 * P:9 * P].rearrange("p (m c d) -> p m c d", m=3, c=NT)
            counts = flat_prob[:, 9 * P:9 * P + 3 * NT].rearrange("p (m c) -> p m c", m=3)
            typ_i = sb1("typ_i", [P, B], I32)
            typ = sb1("typ", [P, B])
            sel = sb1("sel", [P, 3, B])
            coef_b = sb1("coef_b", [P, 5])
            coef = sb1("coef", [P, 5, B])
            tmask = sb1("tmask", [P, B, P])
            bmask = sb1("bmask", [P, B, NT, NT])
            cnt = sb1("cnt", [P, B, NT])

            ids_in = sem("ids_in")
            rows_in = sem("rows_in")
            x_in = [sem(f"x_in{j}") for j in range(NG)]
            xt_in = [sem(f"xt_in{i}") for i in range(2)]
            w_in = sem("w_in")
            w_split = sem("w_split")
            bu_out = sem("bu_out")
            pool_const = sem("pool_const")
            setup_v = sem("setup_v")
            setup_a = sem("setup_a")
            hid_mm = sem("hid_mm")
            hid_act = sem("hid_act")
            score_mm = sem("score_mm")
            score_cp = sem("score_cp")
            stat = sem("stat")
            wcol_act = sem("wcol_act")
            bexp_act = sem("bexp_act")
            prob_act = sem("prob_act")
            gsum_mm = sem("gsum_mm")
            bwT_mm = sem("bwT_mm")
            bwT_cp = sem("bwT_cp")
            g4_mm = sem("g4_mm")
            g4_cp = sem("g4_cp")
            probT_mm = sem("probT_mm")
            probT_cp = sem("probT_cp")
            pool_mm = sem("pool_mm")
            x1_done = sem("x1_done")
            nbr_in = sem("nbr_in")
            nbr_sum = sem("nbr_sum")
            d_act = sem("d_act")
            d_mul = sem("d_mul")
            q_chain = sem("q_chain")
            x2_done = sem("x2_done")
            x2_out = [sem(f"x2_out{i}") for i in range(2)]

            col = lambda a: a.rearrange("(k p) -> p k", p=P)
            row = lambda a, n: a.rearrange("(o n) -> o n", o=1).broadcast_to([n, a.shape[0]])
            n_params = [0]

            with nc.Block() as block:

                def store_x2(sp, b, j):
                    dst = x2_dram.rearrange("(u c p) e -> p u c e", p=P, c=GT)
                    u = NG * b + j
                    sp.wait_ge(x2_done, START + NG * b + j + 1)
                    sp.dma_start(dst[:, bass.ds(u, 1)].rearrange("p u c e -> p (u c) e"),
                                 qbuf[:, j % 2]).then_inc(x2_out[j % 2], 16)

                def stencil_coef(act, b, j):
                    act.wait_ge(x1_done, START + NT * b + GT * (j + 1))
                    act.wait_ge(x2_done, START + NG * b + j)
                    act.activation(dbuf, xb[:, GT * j:GT * j + GT], ACT.Identity,
                                   bias=coef_b[:, 4:5], scale=coef_b[:, 3:4])\
                       .then_inc(d_act, 1)

                @block.sync
                def _(sp):
                    sp.sem_inc(x2_out[0], START)
                    sp.sem_inc(x2_out[1], START)
                    def load(dst, src):
                        sp.dma_start(dst, src).then_inc(params_in, 16)
                        n_params[0] += 16

                    with nc.allow_non_contiguous_dma(reason="small parameters"):
                        sp.dma_start(ids[:], profile.rearrange("(o n) -> o n", o=1)).then_inc(ids_in, 16)
                        load(w1_sb[:], w1.rearrange("(k p) a -> p k a", p=P))
                        load(b1_sb[:], col(b1))
                        load(v_sb[:], col(v))
                        load(typ_i[:], row(ptype, P))
                        load(coef[:, 0], row(zx, P))
                        load(coef[:, 1], row(zy, P))
                        load(coef[:, 2], row(zr, P))
                        load(taus[:, 0:1], row(tau_ctx, P))
                        load(taus[:, 1:3], row(tau_raws, P))
                        load(wn2_col[:], wn2.rearrange("d p -> p d"))
                        load(bias_n2[:], row(bn2, P))
                        for d in range(2):
                            load(blend_sb[:, d], col(blend[d]))
                        load(bias_g[:], col(bg))
                        load(bias_soma[:], col(bsoma))
                        load(bias_temp[:], col(btemp))
                        load(bias_n1[:], col(bn1))
                        load(gamma_row[:], row(gamma, P))
                        load(beta_row[:], row(beta, P))
                        sp.wait_ge(ids_in, 16)
                        for b in range(B):
                            pid = sp.value_load(ids[0:1, b:b + 1], min_val=0, max_val=7)
                            one = bass.ds(pid, 1)
                            for dst, src in (
                                (cols_all[:, b, 0:1], down_b[one, :].rearrange("o p -> p o")),
                                (cols_all[:, b, 1:], ln_b[one, :].rearrange("o (k p) -> p (o k)", p=P)),
                                (bu_f[:, b], up_b[one, :]),
                                (ln_g_row[:, b], ln_g[one, :].broadcast_to([P, E])),
                                (shift_row[:, b], ln_b[one, :].broadcast_to([P, E])),
                            ):
                                sp.dma_start(dst, src).then_inc(rows_in, 16)

                    with sp.Fori(0, B) as b:
                        xT_b = xT[bass.ds(b, 1)].rearrange("o (k p) t -> p (o k) t", p=P)
                        x_b = x[bass.ds(b, 1)].rearrange("o (c p) e -> p (o c) e", p=P)
                        for j in range(2):
                            sp.wait_ge(x2_out[j], START + 16 * NG // 2 * b)
                        for j in range(2):
                            sp.dma_start(xt[:, j], xT_b[:, :, GN * j:GN * j + GN]).then_inc(xt_in[j], 16)
                        sp.wait_ge(x2_done, START + NG * b)
                        for j in range(NG):
                            sp.dma_start(xb[:, GT * j:GT * j + GT], x_b[:, GT * j:GT * j + GT])\
                              .then_inc(x_in[j], 16)
                        for j in range(2, NG):
                            sp.wait_ge(hid_mm, NG * b + j - 1)
                            sp.dma_start(xt[:, j % 2], xT_b[:, :, GN * j:GN * j + GN])\
                              .then_inc(xt_in[j % 2], 16)
                        sp.wait_ge(bu_out, 32)
                        sp.wait_ge(w_split, 12)
                        for j in range(NG):
                            c0 = GT * j
                            if j > 0:
                                store_x2(sp, b, j - 1)
                            tiles = NT * b + min(NT, c0 + GT + 1)
                            groups = NG * b + j
                            sp.wait_ge(x1_done, START + tiles)
                            sp.wait_ge(nbr_sum, START + groups)
                            sp.dma_start(upb[1:P], xb[0:P - 1, c0:c0 + GT]).then_inc(nbr_in, 16)
                            sp.dma_start(dnb[0:P - 1], xb[1:P, c0:c0 + GT]).then_inc(nbr_in, 16)
                            if j == 0:
                                sp.dma_start(upb[0:1, 0], xb[1:2, 0]).then_inc(nbr_in, 16)
                                sp.dma_start(upb[0:1, 1:GT], xb[P - 1:P, 0:GT - 1]).then_inc(nbr_in, 16)
                            else:
                                sp.dma_start(upb[0:1], xb[P - 1:P, c0 - 1:c0 + GT - 1]).then_inc(nbr_in, 16)
                            if j == NG - 1:
                                sp.dma_start(dnb[P - 1:P, GT - 1], xb[P - 2:P - 1, NT - 1]).then_inc(nbr_in, 16)
                                sp.dma_start(dnb[P - 1:P, 0:GT - 1], xb[0:1, c0 + 1:NT]).then_inc(nbr_in, 16)
                            else:
                                sp.dma_start(dnb[P - 1:P], xb[0:1, c0 + 1:c0 + GT + 1]).then_inc(nbr_in, 16)
                        store_x2(sp, b, NG - 1)
                    for i in range(2):
                        sp.wait_ge(x2_out[i], START + 16 * B * NG // 2)
                        sp.wait_ge(xt_in[i], 16 * B * NG // 2)

                @block.gpsimd
                def _(po):
                    po.sem_inc(nbr_sum, START)
                    n = [0]

                    def step(ins):
                        n[0] += 1
                        ins.then_inc(pool_const, 1)

                    step(po.memset(ident[:], 0.0))
                    step(po.memset(hidden_m, 0.0))
                    step(po.memset(hidden_b, 0.0))
                    po.wait_ge(pool_const, 3)
                    diag = dict(compare_op=ALU.not_equal, fill=1.0)
                    step(po.affine_select(out=ident[:], in_=ident[:], base=0, pattern=[[-1, P]],
                                          channel_multiplier=1, **diag))
                    step(po.affine_select(out=hidden_m[:, 0], in_=hidden_m[:, 0], compare_op=ALU.is_ge,
                                          fill=1.0, base=0, pattern=[[-1, P]], channel_multiplier=1))
                    step(po.affine_select(out=hidden_m[:, 1], in_=hidden_m[:, 1], compare_op=ALU.is_ge,
                                          fill=1.0, base=0, pattern=[[1, P]], channel_multiplier=-1))
                    step(po.affine_select(out=hidden_m[:, 2], in_=hidden_m[:, 2], base=0,
                                          pattern=[[-1, P]], channel_multiplier=1, **diag))
                    step(po.affine_select(out=hidden_b[:, 0], in_=hidden_b[:, 0], compare_op=ALU.is_gt,
                                          fill=1.0, base=0, pattern=[[1, NT], [-1, NT]], channel_multiplier=0))
                    step(po.affine_select(out=hidden_b[:, 1], in_=hidden_b[:, 1], compare_op=ALU.is_gt,
                                          fill=1.0, base=0, pattern=[[-1, NT], [1, NT]], channel_multiplier=0))
                    step(po.affine_select(out=hidden_b[:, 2], in_=hidden_b[:, 2], base=0,
                                          pattern=[[1, NT], [-1, NT]], channel_multiplier=0, **diag))
                    step(po.iota(counts[:, 0], pattern=[[P, NT]], base=1, channel_multiplier=1,
                                 allow_small_or_imprecise_dtypes=True))
                    step(po.iota(counts[:, 1], pattern=[[-P, NT]], base=T, channel_multiplier=-1,
                                 allow_small_or_imprecise_dtypes=True))
                    step(po.memset(counts[:, 2], float(T - 1)))
                    for i, value in enumerate((-0.5, 0.5, EPS, 1.0)):
                        step(po.memset(consts[:, i:i + 1], value))
                    assert n[0] == POOL_CONST
                    pieces = [
                        (stage[:], wg[0:E].rearrange("(k p) n -> p k n", p=P), wg_h[:, 0:KE], wg_l[:, 0:KE]),
                        (stage[:], wg[E:2 * E].rearrange("(k p) n -> p k n", p=P), wg_h[:, KE:], wg_l[:, KE:]),
                        (stage[:, :, 0:A], wn1.rearrange("(k p) n -> p k n", p=P), wn1_h[:], wn1_l[:]),
                        (stage[:], wsoma.rearrange("(k p) n -> p k n", p=P), ws_h[:], ws_l[:]),
                        (stage[:], wtemp.rearrange("(k p) n -> p k n", p=P), wt_h[:], wt_l[:]),
                        (stage[:], wout.rearrange("(k p) n -> p k n", p=P), wo_h[:], wo_l[:]),
                    ]
                    for i, (st, src, hi, lo) in enumerate(pieces):
                        if i:
                            po.wait_ge(w_split, 2 * i)
                        po.dma_start(st, src).then_inc(w_in, 16)
                        po.wait_ge(w_in, 16 * (i + 1))
                        po.tensor_copy(hi, st).then_inc(w_split, 1)
                        po.wait_ge(w_split, 2 * i + 1)
                        po.tensor_tensor(lo, st, f32(hi), ALU.subtract).then_inc(w_split, 1)
                    po.wait_ge(setup_v, SETUP_V)
                    po.dma_start(bu_hl[0:1], bu_h).then_inc(bu_out, 16)
                    po.dma_start(bu_hl[1:2], bu_l).then_inc(bu_out, 16)

                    with po.Fori(0, B) as b:
                        for j in range(NG):
                            po.wait_ge(d_act, NG * b + j + 1)
                            po.tensor_tensor(dbuf, dbuf, xb[:, GT * j:GT * j + GT], ALU.mult)\
                              .then_inc(d_mul, 1)
                            po.wait_ge(nbr_in, 16 * (NBR[NG] * b + NBR[j + 1]))
                            po.tensor_tensor(upb[:], upb[:], dnb[:], ALU.add).then_inc(nbr_sum, 1)
                    po.wait_ge(bu_out, 32)

                @block.scalar
                def _(act):
                    act.wait_ge(params_in, N_PARAMS)
                    act.activation(alpha[:], taus[:], ACT.Exp).then_inc(setup_a, 1)
                    act.wait_ge(setup_v, BLEND_SHIFTED)
                    act.activation(blend_w[:], blend_t[:, 0:2], ACT.Exp).then_inc(setup_a, 1)
                    with act.Fori(0, B) as b:
                        for j in range(NG):
                            act.wait_ge(hid_mm, NG * b + j + 1)
                            if j >= 2:
                                act.wait_ge(score_mm, NG * b + j - 1)
                            act.activation(hid[:, j % 2], bank[j % 2][:], ACT.Tanh, bias=b1_sb[:])\
                               .then_inc(hid_act, 1)
                        act.wait_ge(stat, STAT * b + S_WLOG)
                        act.activation(wcol[:], wlog[:], ACT.Exp).then_inc(wcol_act, 1)
                        act.wait_ge(stat, STAT * b + S_BLOG)
                        act.activation(bexp[:, :, 0:NT], blog[:], ACT.Exp).then_inc(bexp_act, 1)
                        for j in range(NG):
                            act.wait_ge(stat, STAT * b + S_PROB + j)
                            p = prob[:, GT * j:GT * j + GT]
                            act.activation(p, p, ACT.Exp).then_inc(prob_act, 1)
                        act.wait_ge(bwT_mm, b + 1)
                        act.activation(bwT[:].rearrange("p g q -> p (g q)"), bank[4][:], ACT.Copy)\
                           .then_inc(bwT_cp, 1)
                        act.wait_ge(g4_mm, b + 1)
                        act.activation(g4[:], bank[5][:], ACT.Copy).then_inc(g4_cp, 1)
                        for j in range(NG):
                            act.wait_ge(probT_mm, NG * b + j + 1)
                            if j >= 2:
                                act.wait_ge(pool_mm, NT * b + GT * (j - 1))
                            act.activation(probT[:, j % 2].rearrange("p g q -> p (g q)"), bank[j % 2][:],
                                           ACT.Copy).then_inc(probT_cp, 1)
                            if j > 0:
                                stencil_coef(act, b, j - 1)
                        stencil_coef(act, b, NG - 1)

                @block.tensor
                def _(pe):
                    pe.wait_ge(params_in, N_PARAMS)
                    pe.wait_ge(setup_v, SETUP_V)
                    pe.wait_ge(pool_const, POOL_CONST)
                    with pe.Fori(0, B) as b:
                        def hidden(j):
                            pe.wait_ge(xt_in[j % 2], 16 * (2 * b + j // 2 + 1))
                            if j >= 2:
                                pe.wait_ge(hid_act, NG * b + j - 1)
                            for k in range(KE):
                                last = pe.matmul(bank[j % 2][:], w1_sb[:, k], xt[:, j % 2, k],
                                                 start=(k == 0), stop=(k == KE - 1))
                            last.then_inc(hid_mm, 1)

                        def scores(j):
                            pe.wait_ge(hid_act, NG * b + j + 1)
                            if j >= 2:
                                pe.wait_ge(score_cp, NG * b + j - 1)
                            pe.matmul(bank[2 + j % 2][:], v_rep[:], hid[:, j % 2], start=True, stop=True)
                            for i in range(GT):
                                c = GT * j + i
                                last = pe.matmul(bank[6][:, c:c + 1], hid[:, j % 2, P * i:P * i + P],
                                                 v_sb[:], start=True, stop=True)
                            last.then_inc(score_mm, 1)

                        pe.wait_ge(x1_done, START + NT * b)
                        hidden(0)
                        for j in range(1, NG):
                            hidden(j)
                            scores(j - 1)
                        scores(NG - 1)
                        pe.wait_ge(wcol_act, b + 1)
                        for j in range(NG):
                            pe.wait_ge(x_in[j], 16 * (b + 1))
                        pe.matmul(bank[7][:, 0:NT], ones[:], wcol[:], start=True, stop=True)
                        for c in range(NT):
                            for k in range(KE):
                                at = 64 + NT * k + c
                                last = pe.matmul(bank[7][:, at:at + 1], xb[:, c, P * k:P * k + P],
                                                 wcol[:, c:c + 1], start=True, stop=True)
                        last.then_inc(gsum_mm, 1)
                        pe.wait_ge(bexp_act, b + 1)
                        for u in range(GT):
                            last = pe.transpose(bank[4][:, P * u:P * u + P],
                                                bexp[:, GT * u:GT * u + GT].rearrange("p c d -> p (c d)"),
                                                ident[:])
                        last.then_inc(bwT_mm, 1)
                        pe.wait_ge(stat, STAT * b + S_GSUM)
                        for k in range(KE):
                            last = pe.transpose(bank[5][:, P * k:P * k + P],
                                                gT[:, k].rearrange("p r d -> p (r d)"), ident[:])
                        last.then_inc(g4_mm, 1)

                        def transposed(j):
                            pe.wait_ge(prob_act, NG * b + j + 1)
                            if j >= 2:
                                pe.wait_ge(probT_cp, NG * b + j - 1)
                            for i in range(GT):
                                last = pe.transpose(bank[j % 2][:, P * i:P * i + P], prob[:, GT * j + i],
                                                    ident[:])
                            last.then_inc(probT_mm, 1)

                        def pooled(j):
                            pe.wait_ge(probT_cp, NG * b + j + 1)
                            for i in range(GT):
                                c = GT * j + i
                                if c >= 4:
                                    pe.wait_ge(x1_done, START + NT * b + c - 3)
                                acc = bank[2 + c % 4][:]
                                pe.matmul(acc, probT[:, j % 2, i], xb[:, c], start=True, stop=False)
                                q = 32 * i
                                pe.matmul(acc, bwT[q:q + 32, j], g4[q:q + 32], start=False, stop=True)\
                                  .then_inc(pool_mm, 1)

                        transposed(0)
                        transposed(1)
                        pe.wait_ge(bwT_cp, b + 1)
                        pe.wait_ge(g4_cp, b + 1)
                        for j in range(NG):
                            pooled(j)
                            if j + 2 < NG:
                                transposed(j + 2)

                @block.vector
                def _(ve):
                    ve.sem_inc(x1_done, START)
                    ve.sem_inc(x2_done, START)
                    n = [0]

                    def step(ins):
                        n[0] += 1
                        ins.then_inc(setup_v, 1)

                    def settle():
                        ve.wait_ge(setup_v, n[0])

                    step(ve.memset(bexp[:], 0.0))
                    step(ve.memset(gT[:], 0.0))
                    step(ve.memset(ones[:], 1.0))
                    ve.wait_ge(params_in, N_PARAMS)
                    step(ve.tensor_tensor(blend_t[:, 2], blend_sb[:, 0], blend_sb[:, 1], ALU.max))
                    settle()
                    for d in range(2):
                        step(ve.tensor_tensor(blend_t[:, d], blend_sb[:, d], blend_t[:, 2], ALU.subtract))
                    assert n[0] == BLEND_SHIFTED
                    step(ve.tensor_copy(typ[:], typ_i[:]))
                    step(ve.tensor_copy(v_rep[:], v_sb[:].broadcast_to([P, P])))
                    for d in range(2):
                        step(ve.tensor_copy(wn2_rep[:, d], wn2_col[:, d:d + 1].broadcast_to([P, P])))
                    step(ve.tensor_copy(ones2[:], ones[0:2, :]))
                    step(ve.tensor_scalar(coef[:, 3], coef[:, 2], -1.0, None, ALU.mult))
                    step(ve.tensor_tensor(coef[:, 4], coef[:, 0], coef[:, 1], ALU.add))
                    settle()
                    step(ve.tensor_scalar(coef[:, 4], coef[:, 4], -2.0, 1.0, ALU.mult, ALU.add))
                    settle()
                    step(ve.tensor_tensor(coef[:, 4], coef[:, 4], coef[:, 2], ALU.add))
                    step(ve.tensor_scalar(sel[:, 0], typ[:], 0.0, None, ALU.is_equal))
                    step(ve.tensor_scalar(sel[:, 1], typ[:], 1.0, None, ALU.is_equal))
                    settle()
                    step(ve.tensor_tensor(sel[:, 2], sel[:, 0], sel[:, 1], ALU.add))
                    settle()
                    step(ve.tensor_scalar(sel[:, 2], sel[:, 2], -1.0, 1.0, ALU.mult, ALU.add))
                    settle()
                    ve.wait_ge(pool_const, POOL_CONST)
                    for b in range(B):
                        for dst, src in ((tmask[:, b], lambda m: hidden_m[:, m]),
                                         (bmask[:, b], lambda m: hidden_b[:, m]),
                                         (cnt[:, b], lambda m: counts[:, m])):
                            step(ve.tensor_scalar(dst, src(0), sel[:, 0, b:b + 1], None, ALU.mult))
                            settle()
                            step(ve.scalar_tensor_tensor(dst, src(1), sel[:, 1, b:b + 1], dst,
                                                         ALU.mult, ALU.add))
                            settle()
                            step(ve.scalar_tensor_tensor(dst, src(2), sel[:, 2, b:b + 1], dst,
                                                         ALU.mult, ALU.add))
                            settle()
                    step(ve.tensor_scalar(tmask[:], tmask[:], NEG, None, ALU.mult))
                    step(ve.tensor_scalar(bmask[:], bmask[:], NEG, None, ALU.mult))
                    ve.wait_ge(setup_a, 1)
                    step(ve.tensor_scalar(alpha[:], alpha[:], 1.0, None, ALU.add))
                    settle()
                    step(ve.reciprocal(alpha[:], alpha[:]))
                    ve.wait_ge(setup_a, 2)
                    step(ve.tensor_tensor(blend_t[:, 2], blend_w[:, 0], blend_w[:, 1], ALU.add))
                    settle()
                    step(ve.reciprocal(blend_t[:, 2], blend_t[:, 2]))
                    settle()
                    for d in range(2):
                        step(ve.tensor_tensor(blend_w[:, d], blend_w[:, d], blend_t[:, 2], ALU.mult))
                    ve.wait_ge(rows_in, 16 * 5 * B)
                    step(ve.tensor_copy(bu_h, bu_f))
                    settle()
                    step(ve.tensor_tensor(bu_l, bu_f, f32(bu_h), ALU.subtract))
                    for b in range(B):
                        step(ve.tensor_tensor(shift_row[:, b], shift_row[:, b], beta_row[:], ALU.add))
                    settle()
                    assert n[0] == SETUP_V, n[0]

                    with ve.Fori(0, B) as b:
                        m = [0]

                        def link(ins, wait=True):
                            m[0] += 1
                            ins.then_inc(stat, 1)
                            if wait:
                                ve.wait_ge(stat, STAT * b + m[0])

                        one = bass.ds(b, 1)
                        ve.wait_ge(x2_done, START + NG * b)
                        link(ve.tensor_scalar(coef_b[:], coef[:, :, one].rearrange("p m o -> p (m o)"), 1.0,
                                              None, ALU.mult), False)
                        for j in range(NG):
                            ve.wait_ge(score_mm, NG * b + j + 1)
                            ve.tensor_copy(s_row[:, GT * j:GT * j + GT].rearrange("p c l -> p (c l)"),
                                           bank[2 + j % 2][:]).then_inc(score_cp, 1)
                        ve.wait_ge(score_cp, NG * (b + 1))
                        link(ve.tensor_reduce(bmax[:], s_row[:], AX.X, ALU.max))
                        link(ve.tensor_tensor(wlog[:], bank[6][:, 0:NT], bmax[:], ALU.subtract), False)
                        assert m[0] == S_WLOG
                        link(ve.tensor_tensor(prob[:], s_row[:], tmask[:, one].broadcast_to([P, NT, P]),
                                              ALU.add))
                        link(ve.tensor_reduce(imax[:], prob[:], AX.X, ALU.max), False)
                        link(ve.tensor_tensor(
                            blog[:], bmask[:, one].rearrange("p o c d -> p (o c) d"),
                            bmax[:].rearrange("p (o c) -> p o c", o=1).broadcast_to([P, NT, NT]), ALU.add))
                        link(ve.tensor_reduce(omax[:], blog[:], AX.X, ALU.max))
                        link(ve.tensor_tensor(rmax[:], imax[:], omax[:], ALU.max))
                        link(ve.tensor_tensor(
                            blog[:], blog[:],
                            rmax[:].rearrange("p (c o) -> p c o", o=1).broadcast_to([P, NT, NT]),
                            ALU.subtract), False)
                        assert m[0] == S_BLOG
                        for j in range(NG):
                            g = slice(GT * j, GT * j + GT)
                            link(ve.tensor_tensor(
                                prob[:, g], prob[:, g],
                                rmax[:, g].rearrange("p (c o) -> p c o", o=1).broadcast_to([P, GT, P]),
                                ALU.subtract), False)
                            assert m[0] == S_PROB + j
                        ve.wait_ge(gsum_mm, b + 1)
                        link(ve.tensor_copy(zblk[:], bank[7][:, 0:NT]), False)
                        for r in range(GT):
                            link(ve.tensor_copy(gT[:, :, r, 0:NT],
                                                bank[7][:, 64:64 + KE * NT].rearrange("p (k c) -> p k c", k=KE)),
                                 False)
                        assert m[0] == S_GSUM
                        ve.wait_ge(bexp_act, b + 1)
                        ve.wait_ge(stat, STAT * b + m[0])
                        link(ve.tensor_tensor(
                            bwz[:], bexp[:, :, 0:NT],
                            zblk[:].rearrange("p (o c) -> p o c", o=1).broadcast_to([P, NT, NT]), ALU.mult))
                        link(ve.tensor_reduce(zout[:], bwz[:], AX.X, ALU.add), False)
                        ve.wait_ge(prob_act, NG * (b + 1))
                        link(ve.tensor_reduce(zin[:], prob[:], AX.X, ALU.add))
                        link(ve.tensor_tensor(zin[:], zin[:], zout[:], ALU.add))
                        assert m[0] == STAT, m[0]
                        ve.tensor_tensor(rnorm[:], zin[:], cnt[:, one].rearrange("p o c -> p (o c)"),
                                         ALU.mult).then_inc(q_chain, 1)
                        ve.wait_ge(q_chain, Q_CHAIN * b + 1)
                        ve.reciprocal(rnorm[:], rnorm[:]).then_inc(q_chain, 1)
                        ve.wait_ge(q_chain, Q_CHAIN * b + 2)

                        def stencil(j):
                            xg = xb[:, GT * j:GT * j + GT]
                            q = qbuf[:, j % 2]
                            if j >= 2:
                                ve.wait_ge(x2_out[j % 2], START + 16 * (2 * b + j // 2))
                            else:
                                ve.wait_ge(x2_out[j % 2], START + 16 * 2 * b)
                            ve.wait_ge(x1_done, START + NT * b + GT * (j + 1))
                            ve.tensor_tensor(q[:, :, 1:E - 1], xg[:, :, 0:E - 2], xg[:, :, 2:E],
                                             ALU.add).then_inc(q_chain, 1)
                            ve.tensor_scalar(q[:, :, 0:1], xg[:, :, 1:2], 2.0, None, ALU.mult)\
                              .then_inc(q_chain, 1)
                            ve.tensor_scalar(q[:, :, E - 1:E], xg[:, :, E - 2:E - 1], 2.0, None,
                                             ALU.mult).then_inc(q_chain, 1)
                            ve.wait_ge(d_mul, NG * b + j + 1)
                            ve.wait_ge(nbr_sum, START + NG * b + j + 1)
                            flat = lambda a: a.rearrange("p c e -> p (c e)")
                            ve.scalar_tensor_tensor(flat(dbuf), flat(upb[:]), coef_b[:, 1:2],
                                                    flat(dbuf), ALU.mult, ALU.add).then_inc(q_chain, 1)
                            ve.wait_ge(q_chain, Q_CHAIN * b + 2 + 4 * (j + 1))
                            ve.scalar_tensor_tensor(flat(q), flat(q), coef_b[:, 0:1], flat(dbuf),
                                                    ALU.mult, ALU.add).then_inc(x2_done, 1)

                        for c in range(NT):
                            ve.wait_ge(pool_mm, NT * b + c + 1)
                            ve.scalar_tensor_tensor(xb[:, c], bank[2 + c % 4][:], rnorm[:, c:c + 1],
                                                    xb[:, c], ALU.mult, ALU.add).then_inc(x1_done, 1)
                            if c % GT == 1 and c > GT:
                                stencil(c // GT - 1)
                        stencil(NG - 1)
                    ve.wait_ge(rows_in, 16 * 5 * B)

        dw_f = sb("dw_f", [P, KE, A])
        uw_f = sb("uw_f", [P, E])
        dw_h = sb("dw_h", [P, KE, A], F32R)
        dw_l = sb("dw_l", [P, KE, A], F32R)
        uw_h = sb("uw_h", [P, E], F32R)
        uw_l = sb("uw_l", [P, E], F32R)
        xa = sb("xa", [P, GT, E])
        res = sb("res", [P, GT, E])
        ph = sb("ph", [P, KE, GN], F32R)
        pl = sb("pl", [P, KE, GN], F32R)
        xh = sb("xh", [P, KE, GN], F32R)
        xl = sb("xl", [P, KE, GN], F32R)
        th = sb("th", [P, KE, GN], F32R)
        tl = sb("tl", [P, KE, GN], F32R)
        narrow = sb("narrow", [P, GN])
        zh = sb("zh", [P, GN], F32R)
        zl = sb("zl", [P, GN], F32R)
        wide = sb("wide", [P, 2, GN])
        wgb = sb("wgb", [P, 2, GN])
        tr = sb("tr", [P, 2, 2, GN])
        soma = sb("soma", [P, KE, GN])
        carry = sb("carry", [P, KE, 3])
        keep = sb("keep", [P, GROUPS])
        st_a = sb("st_a", [P, GT, 6])
        mv_a = sb("mv_a", [P, GT, 2])
        rs_a = sb("rs_a", [P, GT])
        st_o = sb("st_o", [P, GT, 6])
        mv_o = sb("mv_o", [P, GT, 2])
        rs_o = sb("rs_o", [P, GT])

        x2_in = sem("x2_in")
        lw_in = sem("lw_in")
        lw_split = sem("lw_split")
        x2T_mm = sem("x2T_mm")
        x2T_hi = sem("x2T_hi")
        x2T_lo = sem("x2T_lo")
        down_mm = sem("down_mm")
        z_act = sem("z_act")
        z_hi = sem("z_hi")
        z_lo = sem("z_lo")
        up_mm = sem("up_mm")
        y_add = sem("y_add")
        ln_mv = sem("ln_mv")
        ln_p = sem("ln_p")
        ln_rs = sem("ln_rs")
        ln_w = sem("ln_w")
        x3_done = sem("x3_done")
        x3T_mm = sem("x3T_mm")
        x3T_hi = sem("x3T_hi")
        x3T_lo = sem("x3T_lo")
        residual = sem("residual")
        n1_mm = sem("n1_mm")
        n1_act = sem("n1_act")
        mod_mm = sem("mod_mm")
        mod_sig = sem("mod_sig")
        mod_add = sem("mod_add")
        pre_mm = sem("pre_mm")
        ctx_mm = sem("ctx_mm")
        ctx_scan = sem("ctx_scan")
        pre_add = sem("pre_add")
        ctx_kept = sem("ctx_kept")
        wg_act = sem("wg_act")
        xsum_done = sem("xsum_done")
        gated = sem("gated")
        tr_in = sem("tr_in")
        tr_scan = sem("tr_scan")
        carried = sem("carried")
        blended = sem("blended")
        t_hi = sem("t_hi")
        t_lo = sem("t_lo")
        soma_mm = sem("soma_mm")
        soma_act = sem("soma_act")
        temp_mm = sem("temp_mm")
        gate_act = sem("gate_act")
        prod = sem("prod")
        prod_hi = sem("prod_hi")
        prod_lo = sem("prod_lo")
        out_mm = sem("out_mm")
        o_mv = sem("o_mv")
        o_p = sem("o_p")
        o_rs = sem("o_rs")
        out_free = sem("out_free")
        o_done = sem("o_done")
        o_out = sem("o_out")
        p2_v = sem("p2_v")
        cols_set = sem("cols_set")

        N1, PRE, CTX, MOD = 4, (5, 0, 2, 5), (6, 1, 3, 6), (7, 4)
        SOMA, X2T, DOWN, UP = (7, 3, 5, 7), (4, 0, 1, 2), 6, (4, 0, 1, 2)
        TEMP, OUT, X3T = (3, 5, 6, 7), (0, 1, 2, 3), (4, 5, 6, 7)

        with nc.Block() as block:

            @block.sync
            def _(sp):
                sp.sem_inc(o_out, START)
                x2_v = x2_dram.rearrange("(u c p) e -> p u c e", p=P, c=GT)
                out_v = out.rearrange("b (u c p) e -> p (b u) c e", p=P, c=GT)

                def load(q):
                    sp.dma_start(xa[:], x2_v[:, bass.ds(q, 1)].rearrange("p u c e -> p (u c) e"))\
                      .then_inc(x2_in, 16)

                def load_w(q):
                    pid = sp.value_load(ids[0:1, bass.ds(q // NG, 1)], min_val=0, max_val=7)
                    one = bass.ds(pid, 1)
                    sp.dma_start(dw_f[:], down_w[one].rearrange("o (k p) a -> p (o k) a", p=P))\
                      .then_inc(lw_in, 16)
                    sp.dma_start(uw_f[:], up_w[one].rearrange("o a e -> (o a) e")).then_inc(lw_in, 16)

                def store(g):
                    sp.wait_ge(o_done, START + GT * g + GT)
                    sp.dma_start(out_v[:, bass.ds(g, 1)].rearrange("p u c e -> p (u c) e"), res[:])\
                      .then_inc(o_out, 16)

                load(0)
                load_w(0)
                with sp.Fori(0, GROUPS - 1) as g:
                    sp.wait_ge(x3T_mm, KE * g + KE)
                    sp.wait_ge(residual, GT * g + GT)
                    load(g + 1)
                    sp.wait_ge(lw_split, 4 * g + 4)
                    load_w(g + 1)
                    store(g)
                store(GROUPS - 1)
                sp.wait_ge(o_out, START + 16 * GROUPS)

            @block.tensor
            def _(pe):
                pe.sem_inc(temp_mm, START)
                pe.sem_inc(out_mm, START)
                def split3(acc, wh, wl, xh_, xl_, first=True, last=True):
                    n = len(wh)
                    for k in range(n):
                        pe.matmul(acc, wl[k], xh_[k], start=(first and k == 0), stop=False)
                        pe.matmul(acc, wh[k], xl_[k], start=False, stop=False)
                        ins = pe.matmul(acc, wh[k], xh_[k], start=False, stop=(last and k == n - 1))
                    return ins

                ks = range(KE)

                def x2_transposes(q, g):
                    pe.wait_ge(x2_in, 16 * (q + 1))
                    if g is not None:
                        pe.wait_ge(mod_sig, 2 * g + 2)
                        pe.wait_ge(pre_add, KE * g + 3)
                    for k in ks:
                        for c in range(GT):
                            last = pe.transpose(bank[X2T[k]][:, P * c:P * c + P],
                                                xa[:, c, P * k:P * k + P], ident[:])
                        last.then_inc(x2T_mm, 1)

                def down(q, g):
                    if g is not None:
                        pe.wait_ge(ctx_scan, KE * g + 4)
                    pe.wait_ge(lw_split, 4 * q + 4)
                    pe.wait_ge(x2T_lo, KE * q + KE)
                    split3(bank[DOWN][:], [dw_h[:, k] for k in ks], [dw_l[:, k] for k in ks],
                           [ph[:, k] for k in ks], [pl[:, k] for k in ks]).then_inc(down_mm, 1)

                def up(q):
                    pe.wait_ge(z_lo, q + 1)
                    bu = bu_hl[:, bass.ds(q // NG, 1)].rearrange("p o e -> p (o e)")
                    for c in range(GT):
                        t = slice(P * c, P * c + P)
                        acc = bank[UP[c]][:]
                        split3(acc, [zh[:, t]], [zl[:, t]], [uw_h[:]], [uw_l[:]], last=False)
                        pe.matmul(acc, ones2[:], bu, start=False, stop=True).then_inc(up_mm, 1)

                def x3_transposes(q):
                    pe.wait_ge(x3_done, GT * q + GT)
                    for k in ks:
                        for c in range(GT):
                            last = pe.transpose(bank[X3T[k]][:, P * c:P * c + P],
                                                xa[:, c, P * k:P * k + P], ident[:])
                        last.then_inc(x3T_mm, 1)

                def wx(w_h, w_l, off, k):
                    m = slice(P * k, P * k + P)
                    return ([w_h[:, off + i, m] for i in ks], [w_l[:, off + i, m] for i in ks],
                            [xh[:, i] for i in ks], [xl[:, i] for i in ks])

                def front(g):
                    pe.wait_ge(x3T_lo, KE * g + KE)
                    split3(bank[N1][:], [wn1_h[:, i] for i in ks], [wn1_l[:, i] for i in ks],
                           [xh[:, i] for i in ks], [xl[:, i] for i in ks]).then_inc(n1_mm, 1)
                    for k in ks:
                        if k == 1:
                            pe.wait_ge(out_free, START + GT * g)
                        if k == 3:
                            pe.wait_ge(pre_add, KE * g + 1)
                        split3(bank[PRE[k]][:], *wx(wg_h, wg_l, 0, k)).then_inc(pre_mm, 1)
                        if k == 3:
                            pe.wait_ge(ctx_scan, KE * g + 1)
                        split3(bank[CTX[k]][:], *wx(wg_h, wg_l, KE, k)).then_inc(ctx_mm, 1)
                        if k == 0:
                            pe.wait_ge(n1_act, g + 1)
                            for d in range(2):
                                pe.matmul(bank[MOD[d]][:], wn2_rep[:, d], narrow[:], start=True,
                                          stop=True).then_inc(mod_mm, 1)

                def soma_in(g, k):
                    if k == 0:
                        pe.wait_ge(mod_sig, 2 * g + 1)
                    elif k == 1:
                        pe.wait_ge(ctx_scan, KE * g + 3)
                    elif k == 2:
                        pe.wait_ge(pre_add, KE * g + 4)
                    else:
                        pe.wait_ge(soma_act, KE * g + 1)
                    split3(bank[SOMA[k]][:], *wx(ws_h, ws_l, 0, k)).then_inc(soma_mm, 1)

                def temporal(g):
                    pe.wait_ge(t_lo, KE * g + KE)
                    for k in ks:
                        if k < 2:
                            pe.wait_ge(soma_act, KE * g + k + 2)
                        elif k == 3:
                            pe.wait_ge(soma_act, KE * g + 4)
                        m = slice(P * k, P * k + P)
                        split3(bank[TEMP[k]][:], [wt_h[:, i, m] for i in ks],
                               [wt_l[:, i, m] for i in ks], [th[:, i] for i in ks],
                               [tl[:, i] for i in ks]).then_inc(temp_mm, 1)

                def output_part(c, ki, **flags):
                    t = slice(P * c, P * c + P)
                    return split3(bank[OUT[c]][:], [ph[:, i, t] for i in ki], [pl[:, i, t] for i in ki],
                                  [wo_h[:, i] for i in ki], [wo_l[:, i] for i in ki], **flags)

                def output(g, adapted=True):
                    if adapted:
                        pe.wait_ge(y_add, GT * (g + 1) + GT)
                    for k in range(KE - 1):
                        pe.wait_ge(prod_lo, START + KE * g + k + 1)
                        for c in range(GT - 1):
                            output_part(c, [k], first=(k == 0), last=False)
                    pe.wait_ge(prod_lo, START + KE * g + KE)
                    for c in range(GT - 1):
                        output_part(c, [KE - 1], first=False).then_inc(out_mm, 1)

                def output_rest():
                    output_part(GT - 1, ks).then_inc(out_mm, 1)

                x2_transposes(0, None)
                down(0, None)
                up(0)
                x3_transposes(0)
                with pe.Fori(0, LAST) as g:
                    front(g)
                    x2_transposes(g + 1, g)
                    soma_in(g, 0)
                    soma_in(g, 1)
                    soma_in(g, 2)
                    down(g + 1, g)
                    soma_in(g, 3)
                    up(g + 1)
                    temporal(g)
                    output(g)
                    x3_transposes(g + 1)
                    output_rest()
                front(LAST)
                for k in ks:
                    soma_in(LAST, k)
                temporal(LAST)
                output(LAST, adapted=False)
                output_rest()

            @block.scalar
            def _(act):
                def x2_halves(q, first=False):
                    if not first:
                        act.wait_ge(out_mm, START + GT * (q - 1))
                    for k in range(KE):
                        act.wait_ge(x2T_mm, KE * q + k + 1)
                        act.activation(ph[:, k], bank[X2T[k]][:], ACT.Copy).then_inc(x2T_hi, 1)

                def relu(q):
                    act.wait_ge(down_mm, q + 1)
                    act.wait_ge(cols_set, q + 1)
                    act.activation(narrow[:], bank[DOWN][:], ACT.Relu,
                                   bias=cols[:, 0:1]).then_inc(z_act, 1)
                    act.wait_ge(z_act, q + 1)
                    act.activation(zh[:], narrow[:], ACT.Copy).then_inc(z_hi, 1)

                def x3_halves(q):
                    act.wait_ge(gated, KE * q)
                    for k in range(KE):
                        act.wait_ge(x3T_mm, KE * q + k + 1)
                        act.activation(xh[:, k], bank[X3T[k]][:], ACT.Identity,
                                       bias=cols[:, 1 + k:2 + k]).then_inc(x3T_hi, 1)

                def sigmoid_gate(g, k):
                    act.wait_ge(pre_add, KE * g + k + 1)
                    act.activation(wgb[:, k % 2], wgb[:, k % 2], ACT.Sigmoid, bias=bias_g[:, k:k + 1])\
                       .then_inc(wg_act, 1)

                def trace_hi(g, k):
                    act.wait_ge(blended, KE * g + k + 1)
                    act.activation(th[:, k], tr[:, k % 2, 1], ACT.Copy).then_inc(t_hi, 1)

                def front(g, adapted=True):
                    act.wait_ge(n1_mm, g + 1)
                    act.activation(narrow[:], bank[N1][:], ACT.Gelu, bias=bias_n1[:]).then_inc(n1_act, 1)
                    sigmoid_gate(g, 0)
                    act.wait_ge(prod_lo, START + KE * g)
                    for d in range(2):
                        act.wait_ge(mod_mm, 2 * g + d + 1)
                        act.activation(wide[:, d], bank[MOD[d]][:], ACT.Sigmoid,
                                       bias=bias_n2[:, d:d + 1]).then_inc(mod_sig, 1)
                    sigmoid_gate(g, 1)
                    act.wait_ge(temp_mm, START + KE * g)
                    sigmoid_gate(g, 2)
                    trace_hi(g, 0)
                    if adapted:
                        x2_halves(g + 1)
                    sigmoid_gate(g, 3)
                    trace_hi(g, 1)
                    soma_gelu(g, 0)

                def soma_gelu(g, k):
                    act.wait_ge(soma_mm, KE * g + k + 1)
                    act.activation(soma[:, k], bank[SOMA[k]][:], ACT.Gelu,
                                   bias=bias_soma[:, k:k + 1]).then_inc(soma_act, 1)

                def gate(g):
                    for k in range(KE):
                        act.wait_ge(temp_mm, START + KE * g + k + 1)
                        if k >= 2:
                            act.wait_ge(prod_lo, START + KE * g + k - 1)
                        act.activation(wide[:, k % 2], bank[TEMP[k]][:], ACT.Sigmoid,
                                       bias=bias_temp[:, k:k + 1]).then_inc(gate_act, 1)
                        if k >= 1:
                            product_hi(g, k - 1)
                    product_hi(g, KE - 1)

                def product_hi(g, k):
                    act.wait_ge(prod, KE * g + k + 1)
                    act.activation(ph[:, k], wide[:, k % 2], ACT.Copy).then_inc(prod_hi, 1)

                x2_halves(0, first=True)
                relu(0)
                x3_halves(0)
                with act.Fori(0, LAST) as g:
                    front(g)
                    trace_hi(g, 2)
                    soma_gelu(g, 1)
                    soma_gelu(g, 2)
                    relu(g + 1)
                    trace_hi(g, 3)
                    soma_gelu(g, 3)
                    gate(g)
                    x3_halves(g + 1)
                front(LAST, adapted=False)
                trace_hi(LAST, 2)
                soma_gelu(LAST, 1)
                soma_gelu(LAST, 2)
                trace_hi(LAST, 3)
                soma_gelu(LAST, 3)
                act.wait_ge(out_mm, START + GT * LAST)
                gate(LAST)

            @block.gpsimd
            def _(po):
                def split_weights(q):
                    po.wait_ge(lw_in, 32 * (q + 1))
                    po.wait_ge(up_mm, GT * q)
                    po.tensor_tensor(dw_h[:].rearrange("p k a -> p (k a)"), dw_f[:].rearrange("p k a -> p (k a)"),
                                     ONE.broadcast_to([P, KE * A]), ALU.mult).then_inc(lw_split, 1)
                    po.tensor_tensor(uw_h[:], uw_f[:], ONE.broadcast_to([P, E]), ALU.mult).then_inc(lw_split, 1)
                    po.wait_ge(lw_split, 4 * q + 2)
                    po.tensor_tensor(dw_l[:], dw_f[:], f32(dw_h[:]), ALU.subtract).then_inc(lw_split, 1)
                    po.tensor_tensor(uw_l[:], uw_f[:], f32(uw_h[:]), ALU.subtract).then_inc(lw_split, 1)

                def rstd(mean_ready, mv, rs, n, chain, done, c):
                    po.wait_ge(mean_ready, n + 1)
                    po.tensor_tensor(rs[:, c:c + 1], mv[:, c, 1:2], EPSILON, ALU.add).then_inc(chain, 1)
                    po.wait_ge(chain, n + 1)
                    po.tensor_tensor(rs[:, c:c + 1], rs[:, c:c + 1], NEG_HALF, ALU.pow)\
                      .then_inc(done, 1)

                def resid(g):
                    po.wait_ge(x3_done, GT * g + GT)
                    po.wait_ge(o_out, START + 16 * g)
                    for c in range(GT):
                        po.tensor_tensor(res[:, c], xa[:, c],
                                         shift_row[:, bass.ds(g // NG, 1)].rearrange("p o e -> p (o e)"),
                                         ALU.add).then_inc(residual, 1)

                def front(g):
                    resid(g)
                    po.wait_ge(mod_sig, 2 * g + 2)
                    po.tensor_tensor(wide[:], wide[:], HALF.rearrange("p (o n) -> p o n", o=1).broadcast_to([P, 2, GN]),
                                     ALU.add).then_inc(mod_add, 1)
                    for k in range(KE):
                        po.wait_ge(x3T_lo, KE * g + KE)
                        po.tensor_tensor(soma[:, k], f32(xh[:, k]), f32(xl[:, k]), ALU.add)\
                          .then_inc(xsum_done, 1)
                        po.wait_ge(xsum_done, KE * g + k + 1)
                        po.wait_ge(wg_act, KE * g + k + 1)
                        po.tensor_tensor(wgb[:, k % 2], soma[:, k], wgb[:, k % 2], ALU.mult)\
                          .then_inc(gated, 1)

                def ln(q, c):
                    rstd(ln_mv, mv_a, rs_a, GT * q + c, ln_p, ln_rs, c)

                def product(g, k):
                    po.wait_ge(gate_act, KE * g + k + 1)
                    po.tensor_tensor(wide[:, k % 2], soma[:, k], wide[:, k % 2], ALU.mult)\
                      .then_inc(prod, 1)

                def out_ln(g):
                    for c in range(GT):
                        rstd(o_mv, mv_o, rs_o, GT * g + c, o_p, o_rs, c)

                split_weights(0)
                for c in range(GT):
                    ln(0, c)
                with po.Fori(0, LAST) as g:
                    front(g)
                    split_weights(g + 1)
                    ln(g + 1, 0)
                    ln(g + 1, 1)
                    ln(g + 1, 2)
                    product(g, 0)
                    ln(g + 1, 3)
                    product(g, 1)
                    product(g, 2)
                    product(g, 3)
                    out_ln(g)
                front(LAST)
                for k in range(KE):
                    product(LAST, k)
                out_ln(LAST)

            @block.vector
            def _(ve):
                ve.sem_inc(out_free, START)
                ve.sem_inc(prod_lo, START)
                ve.sem_inc(ctx_kept, START)
                ve.sem_inc(o_done, START)
                ve.memset(keep[:], 1.0).then_inc(p2_v, 1)
                ve.memset(carry[:], 0.0).then_inc(p2_v, 1)
                ve.wait_ge(p2_v, 2)
                for b in range(B):
                    last = (b + 1) * NG - 1
                    ve.memset(keep[:, last:last + 1], 0.0).then_inc(p2_v, 1)
                ve.wait_ge(p2_v, 2 + B)

                def set_cols(q):
                    ve.wait_ge(x3T_lo, KE * q)
                    ve.tensor_scalar(cols[:], cols_all[:, bass.ds(q // NG, 1)].rearrange("p o c -> p (o c)"),
                                     1.0, None, ALU.mult).then_inc(cols_set, 1)

                def x2_lo(q):
                    for k in range(KE):
                        ve.wait_ge(x2T_hi, KE * q + k + 1)
                        ve.tensor_tensor(pl[:, k], bank[X2T[k]][:], f32(ph[:, k]), ALU.subtract)\
                          .then_inc(x2T_lo, 1)

                def relu_lo(q):
                    ve.wait_ge(z_hi, q + 1)
                    ve.tensor_tensor(zl[:], narrow[:], f32(zh[:]), ALU.subtract).then_inc(z_lo, 1)

                def moments(acc, st, mv, c, done):
                    ve.bn_stats(st[:, c], acc)
                    ve.drain()
                    ve.bn_aggr(mv[:, c], st[:, c]).then_inc(done, 1)

                def ln_stats(q, c):
                    y = tr[:, c % 2, 0]
                    ve.wait_ge(up_mm, GT * q + c + 1)
                    if c >= 2:
                        ve.wait_ge(x3_done, GT * q + c - 1)
                    ve.tensor_tensor(y, bank[UP[c]][:], xa[:, c], ALU.add).then_inc(y_add, 1)
                    ve.wait_ge(y_add, GT * q + c + 1)
                    moments(y, st_a, mv_a, c, ln_mv)

                def ln_apply(q, c):
                    y = tr[:, c % 2, 0]
                    ve.wait_ge(ln_mv, GT * q + c + 1)
                    ve.scalar_tensor_tensor(
                        y, y, mv_a[:, c, 0:1],
                        ln_g_row[:, bass.ds(q // NG, 1)].rearrange("p o e -> p (o e)"),
                        ALU.subtract, ALU.mult).then_inc(ln_w, 1)
                    ve.wait_ge(ln_w, GT * q + c + 1)
                    ve.wait_ge(ln_rs, GT * q + c + 1)
                    ve.scalar_tensor_tensor(xa[:, c], y, rs_a[:, c:c + 1], xa[:, c], ALU.mult, ALU.add)\
                      .then_inc(x3_done, 1)

                def x3_lo(q):
                    for k in range(KE):
                        ve.wait_ge(x3T_hi, KE * q + k + 1)
                        ve.scalar_tensor_tensor(xl[:, k], bank[X3T[k]][:],
                                                cols[:, 1 + k:2 + k], f32(xh[:, k]),
                                                ALU.add, ALU.subtract).then_inc(x3T_lo, 1)

                def logits(g, k):
                    w = wgb[:, k % 2]
                    h = tr[:, k % 2, 0]
                    if k >= 2:
                        ve.wait_ge(blended, KE * g + k - 1)
                    else:
                        ve.wait_ge(o_done, START + GT * g)
                    ve.wait_ge(ctx_mm, KE * g + k + 1)
                    ve.wait_ge(ctx_kept, START + KE * g + k)
                    ve.tensor_tensor_scan(h, alpha[:, 0:1].broadcast_to([P, GN]), bank[CTX[k]][:],
                                          carry[:, k, 0:1], ALU.mult, ALU.add).then_inc(ctx_scan, 1)
                    ve.wait_ge(ctx_scan, KE * g + k + 1)
                    ve.tensor_scalar(carry[:, k, 0:1], h[:, GN - 1:GN], keep[:, bass.ds(g, 1)], None,
                                     ALU.mult).then_inc(ctx_kept, 1)
                    ve.wait_ge(pre_mm, KE * g + k + 1)
                    ve.tensor_tensor(w, bank[PRE[k]][:], h, ALU.add).then_inc(pre_add, 1)

                def traces(g, k):
                    t = tr[:, k % 2]
                    if k == 0:
                        ve.wait_ge(mod_add, g + 1)
                    if k >= 2:
                        ve.wait_ge(t_lo, KE * g + k - 1)
                    ve.wait_ge(ctx_kept, START + KE * g + k + 1)
                    ve.wait_ge(gated, KE * g + k + 1)
                    for d in range(2):
                        ve.scalar_tensor_tensor(t[:, d], wgb[:, k % 2], blend_w[:, d, k:k + 1],
                                                wide[:, d], ALU.mult, ALU.mult).then_inc(tr_in, 1)
                    for d in range(2):
                        ve.wait_ge(tr_in, 2 * (KE * g + k) + d + 1)
                        ve.tensor_tensor_scan(t[:, d], alpha[:, 1 + d:2 + d].broadcast_to([P, GN]),
                                              t[:, d], carry[:, k, 1 + d:2 + d], ALU.mult, ALU.add)\
                          .then_inc(tr_scan, 1)
                    ve.wait_ge(tr_scan, 2 * (KE * g + k + 1))
                    ve.tensor_scalar(carry[:, k, 1:3], t[:, :, GN - 1], keep[:, bass.ds(g, 1)], None,
                                     ALU.mult).then_inc(carried, 1)
                    ve.wait_ge(carried, KE * g + k + 1)
                    ve.tensor_tensor(t[:, 1], t[:, 0], t[:, 1], ALU.add).then_inc(blended, 1)

                def trace_lo(g, k):
                    ve.wait_ge(t_hi, KE * g + k + 1)
                    ve.tensor_tensor(tl[:, k], tr[:, k % 2, 1], f32(th[:, k]), ALU.subtract)\
                      .then_inc(t_lo, 1)

                def front(g, adapted=True):
                    logits(g, 0)
                    logits(g, 1)
                    traces(g, 0)
                    logits(g, 2)
                    traces(g, 1)
                    trace_lo(g, 0)
                    logits(g, 3)
                    traces(g, 2)
                    trace_lo(g, 1)
                    if adapted:
                        x2_lo(g + 1)
                    traces(g, 3)
                    trace_lo(g, 2)
                    if adapted:
                        relu_lo(g + 1)
                    trace_lo(g, 3)

                def product_lo(g, k):
                    ve.wait_ge(prod_hi, KE * g + k + 1)
                    ve.tensor_tensor(pl[:, k], wide[:, k % 2], f32(ph[:, k]), ALU.subtract)\
                      .then_inc(prod_lo, 1)

                def out_stats(g, c):
                    ve.wait_ge(out_mm, START + GT * g + c + 1)
                    moments(bank[OUT[c]][:], st_o, mv_o, c, o_mv)

                def out_apply(g, c):
                    t = tr[:, c % 2, 0]
                    ve.wait_ge(o_mv, GT * g + c + 1)
                    ve.scalar_tensor_tensor(t, bank[OUT[c]][:], mv_o[:, c, 0:1], gamma_row[:],
                                            ALU.subtract, ALU.mult).then_inc(out_free, 1)
                    ve.wait_ge(out_free, START + GT * g + c + 1)
                    ve.wait_ge(o_rs, GT * g + c + 1)
                    ve.scalar_tensor_tensor(res[:, c], t, rs_o[:, c:c + 1], res[:, c], ALU.mult,
                                            ALU.add).then_inc(o_done, 1)

                def output(g, adapted=True):
                    ve.wait_ge(residual, GT * g + GT)
                    if adapted:
                        ve.wait_ge(x3_done, GT * (g + 1) + GT)
                    out_stats(g, 0)
                    out_stats(g, 1)
                    if adapted:
                        x3_lo(g + 1)
                    out_stats(g, 2)
                    out_apply(g, 0)
                    out_apply(g, 1)
                    out_stats(g, 3)
                    out_apply(g, 2)
                    out_apply(g, 3)

                set_cols(0)
                x2_lo(0)
                relu_lo(0)
                ln_stats(0, 0)
                for c in range(1, GT):
                    ln_stats(0, c)
                    ln_apply(0, c - 1)
                ln_apply(0, GT - 1)
                x3_lo(0)
                with ve.Fori(0, LAST) as g:
                    set_cols(g + 1)
                    front(g)
                    ln_stats(g + 1, 0)
                    ln_stats(g + 1, 1)
                    ln_apply(g + 1, 0)
                    ln_stats(g + 1, 2)
                    ln_apply(g + 1, 1)
                    ln_stats(g + 1, 3)
                    ln_apply(g + 1, 2)
                    product_lo(g, 0)
                    ln_apply(g + 1, 3)
                    for k in range(1, KE):
                        product_lo(g, k)
                    output(g)
                front(LAST, adapted=False)
                for k in range(KE):
                    product_lo(LAST, k)
                output(LAST, adapted=False)


def kernel(**inputs):
    import numpy as np
    import concourse.bacc as bacc
    from concourse.bass_utils import run_bass_kernel_spmd

    i = {k: np.asarray(a) for k, a in inputs.items()}
    flip = lambda a: np.ascontiguousarray(a.T)
    arrays = {
        "x": i["x"],
        "xT": np.ascontiguousarray(i["x"].transpose(0, 2, 1)),
        "ptype": i["itok_B_0_2"],
        "zx": i["condB_zX"],
        "zy": i["condB_zY"],
        "zr": i["condB_zR"],
        "profile": i["itok_B_0_6"],
        "tau_raws": i["condB_tauraws"],
        "wn2": i["cond_256"],
        "bn2": i["condB_bn2"],
        "blend": i["cond_1024"],
        "w1": i["L0_cond_W1"],
        "b1": i["L0_cond_b1"],
        "v": i["L0_cond_v"],
        "down_w": i["L2_cond_down_w"],
        "down_b": i["L2_cond_down_b"],
        "up_w": i["L2_cond_up_w"],
        "up_b": i["L2_cond_up_b"],
        "ln_g": i["L2_cond_ln_g"],
        "ln_b": i["L2_cond_ln_b"],
        "tau_ctx": i["L3_cond_tau_ctx"].reshape(1),
        "wg": flip(i["L3_cond_Wg"]),
        "bg": i["L3_cond_bg"],
        "wn1": flip(i["L3_cond_Wn1"]),
        "bn1": i["L3_cond_bn1"],
        "wsoma": flip(i["L3_cond_Wsoma"]),
        "bsoma": i["L3_cond_bsoma"],
        "wtemp": flip(i["L3_cond_Wtemp"]),
        "btemp": i["L3_cond_btemp"],
        "wout": flip(i["L3_cond_Wout"]),
        "gamma": i["L3_cond_gamma"],
        "beta": i["L3_cond_beta"],
    }
    arrays = {k: np.ascontiguousarray(a) for k, a in arrays.items()}
    nc = bacc.Bacc("TRN2", target_bir_lowering=False, num_devices=1)
    args = {k: nc.dram_tensor(f"in_{k}", a.shape, mybir.dt.from_np(a.dtype), kind="ExternalInput").ap()
            for k, a in arrays.items()}
    args["out"] = nc.dram_tensor("result", (B, T, E), F32, kind="ExternalOutput").ap()
    build_program(nc, **args)
    r = run_bass_kernel_spmd(nc, [{f"in_{k}": a for k, a in arrays.items()}], core_ids=[0])
    return r.results[0]["result"]
```

```python
from contextlib import ExitStack

import concourse.bass as bass
from concourse import mybir

F32 = mybir.dt.float32
F32R = mybir.dt.float32r
I32 = mybir.dt.int32
ALU = mybir.AluOpType
ACT = mybir.ActivationFunctionType
AX = mybir.AxisListType

P = 128
B, T, E = 2, 2048, 512
A = 128
KE = E // P
NT = T // P
GT = 4
SLOT = (1, 0, 1, 0)
GN = GT * P
NG = NT // GT
GROUPS = B * NG
LAST = GROUPS - 1
NEG = -1e30
EPS = 1e-5

N_COEF = 16 * 4
N_PARAMS = 16 * 11
POOL_CONST = 17
SETUP_V = 31
BLEND_SHIFTED = SETUP_V + 3
BIAS_LO = SETUP_V + 14
S_WLOG, S_BLOG, S_PROB, STAT = 14, 18, 19, 27
START = 1
Q_CHAIN = 2 + 3 * NG
NBR = [5, 4, 4 + 5, 5 + 4]


def build_program(nc, x, xT, ptype, zx, zy, zr, profile, tau_raws, wn2, bn2, blend, w1, b1, v,
                  down_w, down_b, up_w, up_b, ln_g, ln_b, tau_ctx, wg, bg, wn1, bn1, wsoma, bsoma,
                  wtemp, btemp, wout, gamma, beta, out):
    ctx = ExitStack()
    with ctx:
        def sb(name, shape, dt=F32, stack=ctx):
            return stack.enter_context(nc.sbuf_tensor(name, shape, dt))

        def sem(name):
            return ctx.enter_context(nc.semaphore(name))

        x2_dram = nc.dram_tensor("x2_scratch", (B * T, E), F32, kind="Internal").ap()

        ident = sb("ident", [P, P])
        consts = sb("consts", [P, 4])
        taus = sb("taus", [P, 3])
        alpha = sb("alpha", [P, 3])
        blend_sb = sb("blend_sb", [P, 2, KE])
        blend_w = sb("blend_w", [P, 2, KE])
        blend_t = sb("blend_t", [P, 3, KE])
        bias_g = sb("bias_g", [P, KE])
        bias_soma = sb("bias_soma", [P, KE])
        bias_temp = sb("bias_temp", [P, KE])
        bias_n1 = sb("bias_n1", [P, 1])
        bias_n2 = sb("bias_n2", [P, 2])
        cols_all = sb("cols_all", [P, B, 1 + KE])
        cols = sb("cols", [P, 1 + KE])
        ids = sb("ids", [1, B], I32)
        wn2_rep = sb("wn2_rep", [P, 2, P])
        wn2_col = sb("wn2_col", [P, 2])
        gamma_row = sb("gamma_row", [P, E])
        ln_g_row = sb("ln_g_row", [P, B, E])
        shift_row = sb("shift_row", [P, B, E])
        bu_hl = sb("bu_hl", [2, B, E], F32R)
        ones2 = sb("ones2", [2, P], F32R)
        wg_h = sb("wg_h", [P, 2 * KE, E], F32R)
        wg_l = sb("wg_l", [P, 2 * KE, E], F32R)
        wn1_h = sb("wn1_h", [P, KE, A], F32R)
        wn1_l = sb("wn1_l", [P, KE, A], F32R)
        ws_h = sb("ws_h", [P, KE, E], F32R)
        ws_l = sb("ws_l", [P, KE, E], F32R)
        wt_h = sb("wt_h", [P, KE, E], F32R)
        wt_l = sb("wt_l", [P, KE, E], F32R)
        wo_h = sb("wo_h", [P, KE, E], F32R)
        wo_l = sb("wo_l", [P, KE, E], F32R)

        dw_f = sb("dw_f", [P, KE, A])
        uw_f = sb("uw_f", [P, E])
        xa = sb("xa", [P, GT, E])

        bank = [ctx.enter_context(nc.psum_tensor(f"bank{i}", [P, 512], F32)) for i in range(8)]

        params_in = sem("params_in")

        x2_in = sem("x2_in")
        lw_in = sem("lw_in")

        def load_group(sp, q):
            src = x2_dram.rearrange("(u c p) e -> p u c e", p=P, c=GT)
            sp.dma_start(xa[:], src[:, bass.ds(q, 1)].rearrange("p u c e -> p (u c) e")).then_inc(x2_in, 16)

        def load_adapter(sp, q):
            pid = sp.value_load(ids[0:1, bass.ds(q // NG, 1)], min_val=0, max_val=7)
            one = bass.ds(pid, 1)
            sp.dma_start(dw_f[:], down_w[one].rearrange("o (k p) a -> p (o k) a", p=P)).then_inc(lw_in, 16)
            sp.dma_start(uw_f[:], up_w[one].rearrange("o a e -> (o a) e")).then_inc(lw_in, 16)

        NEG_HALF, HALF, EPSILON, ONE = (consts[:, i:i + 1] for i in range(4))

        def f32(t):
            return t.bitcast(F32)

        s1 = ExitStack()
        with s1:
            def sb1(name, shape, dt=F32):
                return sb(name, shape, dt, s1)

            xb = sb1("xb", [P, NT, E])
            xt = sb1("xt", [P, 2, KE, GN])
            w1_sb = sb1("w1_sb", [P, KE, A])
            b1_sb = sb1("b1_sb", [P, 1])
            v_sb = sb1("v_sb", [P, 1])
            v_rep = sb1("v_rep", [P, P])
            ones = sb1("ones", [P, P])
            hid = sb1("hid", [P, 2, GN])
            s_row = sb1("s_row", [P, NT, P])
            prob = sb1("prob", [P, NT, P])
            bmax = sb1("bmax", [P, NT])
            imax = sb1("imax", [P, NT])
            omax = sb1("omax", [P, NT])
            rmax = sb1("rmax", [P, NT])
            wlog = sb1("wlog", [P, NT])
            wcol = sb1("wcol", [P, NT])
            blog = sb1("blog", [P, NT, NT])
            bexp = sb1("bexp", [P, NT, 32])
            bwT = sb1("bwT", [P, GT, P])
            zin = sb1("zin", [P, NT])
            zout = sb1("zout", [P, NT])
            zblk = sb1("zblk", [P, NT])
            rnorm = sb1("rnorm", [P, NT])
            g4 = sb1("g4", [P, E])
            upb = sb1("upb", [P, GT, E])
            dnb = sb1("dnb", [P, GT, E])
            dbuf = s_row[:].rearrange("p (g c) l -> p g (c l)", g=GT)
            probT = hid[:].rearrange("p i (g q) -> p i g q", g=GT)
            bwz = blog
            tmask = uw_f[:, 0:B * P].rearrange("p (b l) -> p b l", b=B)
            bmask = dw_f[:].rearrange("p k a -> p (k a)").rearrange("p (b c d) -> p b c d", b=B, c=NT)
            qbuf = [xa[:], prob[:].rearrange("p (g c) l -> p g (c l)", g=GT)]
            before = [xt[:, 0], upb[:]]
            after = [xt[:, 1], dnb[:]]
            wsel = upb[:].rearrange("p g (u q) -> p (g u) q", q=P)
            wsel_flat = upb[:].rearrange("p g e -> p (g e)")
            beta_row = g4
            bu_f = hid[0:1]
            flat_prob = prob[:].rearrange("p c l -> p (c l)")
            hidden_m = flat_prob[:, 0:3 * P].rearrange("p (m l) -> p m l", m=3)
            hidden_b = flat_prob[:, 3 * P:9 * P].rearrange("p (m c d) -> p m c d", m=3, c=NT)
            counts = flat_prob[:, 9 * P:9 * P + 3 * NT].rearrange("p (m c) -> p m c", m=3)
            typ_i = sb1("typ_i", [P, B], I32)
            typ = sb1("typ", [P, B])
            sel = sb1("sel", [P, 3, B])
            coef_b = sb1("coef_b", [P, 5])
            coef = sb1("coef", [P, 5, B])
            cnt = sb1("cnt", [P, B, NT])

            ids_in = sem("ids_in")
            coef_in = sem("coef_in")
            late_in = sem("late_in")
            rows_in = sem("rows_in")
            x_in = [sem(f"x_in{j}") for j in range(NG)]
            xt_in = [sem(f"xt_in{i}") for i in range(2)]
            w_in = [sem(f"w_in{i}") for i in range(6)]
            w_split = sem("w_split")
            bu_out = sem("bu_out")
            pool_const = sem("pool_const")
            setup_v = sem("setup_v")
            setup_a = sem("setup_a")
            hid_mm = sem("hid_mm")
            hid_act = sem("hid_act")
            score_mm = sem("score_mm")
            score_cp = sem("score_cp")
            stat = sem("stat")
            wcol_act = sem("wcol_act")
            bexp_act = sem("bexp_act")
            prob_act = sem("prob_act")
            wsel_zero = sem("wsel_zero")
            wsel_act = sem("wsel_act")
            zsum_mm = sem("zsum_mm")
            w1_in = sem("w1_in")
            v_set = sem("v_set")
            mixed = sem("mixed")
            bwT_mm = sem("bwT_mm")
            bwT_cp = sem("bwT_cp")
            g4_mm = sem("g4_mm")
            g4_cp = sem("g4_cp")
            probT_mm = sem("probT_mm")
            probT_cp = sem("probT_cp")
            pool_mm = sem("pool_mm")
            x1_done = sem("x1_done")
            nbr_in = [sem(f"nbr_in{i}") for i in range(2)]
            nbr_sum = sem("nbr_sum")
            d_act = sem("d_act")
            d_mul = sem("d_mul")
            q_chain = sem("q_chain")
            x2_done = sem("x2_done")
            x2_out = [sem(f"x2_out{i}") for i in range(2)]

            col = lambda a: a.rearrange("(k p) -> p k", p=P)
            row = lambda a, n: a.rearrange("(o n) -> o n", o=1).broadcast_to([n, a.shape[0]])
            n_params = [0]

            with nc.Block() as block:

                x2_v = x2_dram.rearrange("(u c p) e -> p u c e", p=P, c=GT)

                def store_x2(sp, b, j):
                    sp.wait_ge(x2_done, START + NG * b + j + 1)
                    sp.dma_start(x2_v[:, bass.ds(NG * b + j, 1)].rearrange("p u c e -> p (u c) e"),
                                 qbuf[j % 2]).then_inc(x2_out[j % 2], 16)

                def stencil_coef(act, b, j):
                    act.wait_ge(x1_done, START + NT * b + GT * (j + 1))
                    act.wait_ge(mixed, START + NG * b + j)
                    act.activation(dbuf, xb[:, GT * j:GT * j + GT], ACT.Identity,
                                   bias=coef_b[:, 4:5], scale=coef_b[:, 3:4])\
                       .then_inc(d_act, 1)

                @block.sync
                def _(sp):
                    for i in range(2):
                        sp.sem_inc(x2_out[i], START)

                    def load_xt(b, j):
                        xT_b = xT[bass.ds(b, 1)].rearrange("o (k p) t -> p (o k) t", p=P)
                        sp.dma_start(xt[:, SLOT[j]], xT_b[:, :, GN * j:GN * j + GN]).then_inc(xt_in[j % 2], 16)

                    def load_x(b, j):
                        x_b = x[bass.ds(b, 1)].rearrange("o (c p) e -> p (o c) e", p=P)
                        sp.dma_start(xb[:, GT * j:GT * j + GT], x_b[:, GT * j:GT * j + GT])\
                          .then_inc(x_in[j], 16)

                    with nc.allow_non_contiguous_dma(reason="small parameters"):
                        sp.dma_start(w1_sb[:], w1.rearrange("(k p) a -> p k a", p=P)).then_inc(w1_in, 16)
                        load_xt(0, 0)
                        sp.dma_start(b1_sb[:], col(b1)).then_inc(w1_in, 16)
                        sp.dma_start(v_sb[:], col(v)).then_inc(w1_in, 16)
                        for dst, src in ((typ_i[:], ptype), (coef[:, 0], zx), (coef[:, 1], zy),
                                         (coef[:, 2], zr)):
                            sp.dma_start(dst, row(src, P)).then_inc(coef_in, 16)
                        sp.dma_start(ids[:], profile.rearrange("(o n) -> o n", o=1)).then_inc(ids_in, 16)
                        load_xt(0, 1)
                        load_x(0, 0)
                        load_x(0, 1)
                        sp.wait_ge(ids_in, 16)
                        for b in range(B):
                            pid = sp.value_load(ids[0:1, b:b + 1], min_val=0, max_val=7)
                            one = bass.ds(pid, 1)
                            for dst, src in (
                                (cols_all[:, b, 0:1], down_b[one, :].rearrange("o p -> p o")),
                                (cols_all[:, b, 1:], ln_b[one, :].rearrange("o (k p) -> p (o k)", p=P)),
                                (ln_g_row[:, b], ln_g[one, :].broadcast_to([P, E])),
                                (shift_row[:, b], ln_b[one, :].broadcast_to([P, E])),
                            ):
                                sp.dma_start(dst, src).then_inc(rows_in, 16)

                    def before_x1(b, j):
                        c0 = GT * j
                        up = before[j % 2]
                        if j < 2:
                            sp.wait_ge(x1_done, START + NT * b + c0 + GT)
                        else:
                            sp.wait_ge(x2_done, START + NG * b + j - 1)
                        sp.dma_start(up[1:P], xb[0:P - 1, c0:c0 + GT]).then_inc(nbr_in[j % 2], 16)
                        if j == 0:
                            sp.dma_start(up[0:1, 1:GT], xb[P - 1:P, c0:c0 + GT - 1]).then_inc(nbr_in[j % 2], 16)
                            sp.dma_start(up[0:1, 0:1], xb[1:2, 0:1]).then_inc(nbr_in[j % 2], 16)
                        else:
                            sp.dma_start(up[0:1], xb[P - 1:P, c0 - 1:c0 + GT - 1]).then_inc(nbr_in[j % 2], 16)

                    def after_x1(b, j):
                        c0 = GT * j
                        dn = after[j % 2]
                        if j >= 2:
                            sp.wait_ge(nbr_sum, NG * b + j - 1)
                        elif j == 1:
                            sp.wait_ge(w_split, 12)
                        sp.wait_ge(x1_done, START + NT * b + min(NT, c0 + GT + 1))
                        sp.dma_start(dn[0:P - 1], xb[1:P, c0:c0 + GT]).then_inc(nbr_in[j % 2], 16)
                        if j == NG - 1:
                            sp.dma_start(dn[P - 1:P, 0:GT - 1], xb[0:1, c0 + 1:c0 + GT]).then_inc(nbr_in[j % 2], 16)
                            sp.dma_start(dn[P - 1:P, GT - 1:GT], xb[P - 2:P - 1, NT - 1:NT])\
                              .then_inc(nbr_in[j % 2], 16)
                        else:
                            sp.dma_start(dn[P - 1:P], xb[0:1, c0 + 1:c0 + GT + 1]).then_inc(nbr_in[j % 2], 16)

                    def batch(b, more):
                        for j in range(2, NG):
                            sp.wait_ge(hid_mm, NG * b + j - 1)
                            load_xt(b, j)
                        for j in range(2, NG):
                            sp.wait_ge(w_split, 2 * j)
                            load_x(b, j)
                        before_x1(b, 0)
                        after_x1(b, 0)
                        before_x1(b, 1)
                        after_x1(b, 1)
                        after_x1(b, 2)
                        before_x1(b, 2)
                        store_x2(sp, b, 0)
                        after_x1(b, 3)
                        before_x1(b, 3)
                        store_x2(sp, b, 1)
                        if more:
                            sp.wait_ge(nbr_sum, NG * b + 3)
                            load_xt(b + 1, 0)
                        else:
                            for i in range(B):
                                pid = sp.value_load(ids[0:1, i:i + 1], min_val=0, max_val=7)
                                sp.dma_start(bu_f[:, i], up_b[bass.ds(pid, 1), :]).then_inc(late_in, 16)
                            sp.dma_start(beta_row[:], row(beta, P)).then_inc(late_in, 16)
                            load_adapter(sp, 0)
                        store_x2(sp, b, 2)
                        if more:
                            load_xt(b + 1, 1)
                            load_x(b + 1, 0)
                        store_x2(sp, b, 3)
                        if more:
                            load_x(b + 1, 1)
                        else:
                            sp.wait_ge(x2_out[0], START + 16 * B * NG // 2)
                            load_group(sp, 0)

                    with sp.Fori(0, B - 1) as b:
                        batch(b, True)
                    batch(B - 1, False)
                    for i in range(2):
                        sp.wait_ge(x2_out[i], START + 16 * B * NG // 2)
                        sp.wait_ge(xt_in[i], 16 * B * NG // 2)

                @block.gpsimd
                def _(po):
                    n = [0]

                    def step(ins):
                        n[0] += 1
                        ins.then_inc(pool_const, 1)

                    step(po.memset(ident[:], 0.0))
                    step(po.memset(hidden_m, 0.0))
                    step(po.memset(hidden_b, 0.0))
                    po.wait_ge(pool_const, 3)
                    diag = dict(compare_op=ALU.not_equal, fill=1.0)
                    step(po.affine_select(out=ident[:], in_=ident[:], base=0, pattern=[[-1, P]],
                                          channel_multiplier=1, **diag))
                    step(po.affine_select(out=hidden_m[:, 0], in_=hidden_m[:, 0], compare_op=ALU.is_ge,
                                          fill=1.0, base=0, pattern=[[-1, P]], channel_multiplier=1))
                    step(po.affine_select(out=hidden_m[:, 1], in_=hidden_m[:, 1], compare_op=ALU.is_ge,
                                          fill=1.0, base=0, pattern=[[1, P]], channel_multiplier=-1))
                    step(po.affine_select(out=hidden_m[:, 2], in_=hidden_m[:, 2], base=0,
                                          pattern=[[-1, P]], channel_multiplier=1, **diag))
                    step(po.affine_select(out=hidden_b[:, 0], in_=hidden_b[:, 0], compare_op=ALU.is_gt,
                                          fill=1.0, base=0, pattern=[[1, NT], [-1, NT]], channel_multiplier=0))
                    step(po.affine_select(out=hidden_b[:, 1], in_=hidden_b[:, 1], compare_op=ALU.is_gt,
                                          fill=1.0, base=0, pattern=[[-1, NT], [1, NT]], channel_multiplier=0))
                    step(po.affine_select(out=hidden_b[:, 2], in_=hidden_b[:, 2], base=0,
                                          pattern=[[1, NT], [-1, NT]], channel_multiplier=0, **diag))
                    step(po.iota(counts[:, 0], pattern=[[P, NT]], base=1, channel_multiplier=1,
                                 allow_small_or_imprecise_dtypes=True))
                    step(po.iota(counts[:, 1], pattern=[[-P, NT]], base=T, channel_multiplier=-1,
                                 allow_small_or_imprecise_dtypes=True))
                    step(po.memset(counts[:, 2], float(T - 1)))
                    for i, value in enumerate((-0.5, 0.5, EPS, 1.0)):
                        step(po.memset(consts[:, i:i + 1], value))
                    assert n[0] == POOL_CONST
                    chunks = lambda w: w.rearrange("(k p) n -> p k n", p=P)
                    pieces = [
                        (dnb[:], chunks(wg[0:E]), wg_h[:, 0:KE], wg_l[:, 0:KE]),
                        (xb[:, 2 * GT:3 * GT], chunks(wg[E:2 * E]), wg_h[:, KE:], wg_l[:, KE:]),
                        (xb[:, 3 * GT:], chunks(wsoma), ws_h[:], ws_l[:]),
                        (dnb[:], chunks(wtemp), wt_h[:], wt_l[:]),
                        (dnb[:], chunks(wout), wo_h[:], wo_l[:]),
                        (dnb[:, :, 0:A], chunks(wn1), wn1_h[:], wn1_l[:]),
                    ]
                    po.wait_ge(pool_const, POOL_CONST)

                    def load_piece(i):
                        po.dma_start(pieces[i][0], pieces[i][1]).then_inc(w_in[i], 16)

                    for i in range(3):
                        load_piece(i)
                    for i, (st, src, hi, lo) in enumerate(pieces):
                        if i > 3:
                            po.wait_ge(w_split, 2 * i)
                            load_piece(i)
                        po.wait_ge(w_in[i], 16)
                        po.tensor_tensor(hi, st, ONE.rearrange("p (o n) -> p o n", o=1)
                                         .broadcast_to(list(st.shape)), ALU.mult).then_inc(w_split, 1)
                        po.wait_ge(w_split, 2 * i + 1)
                        po.tensor_tensor(lo, st, f32(hi), ALU.subtract).then_inc(w_split, 1)
                        if i == 0:
                            po.wait_ge(w_split, 2)
                            load_piece(3)
                    with po.Fori(0, B) as b:
                        def local(j):
                            po.wait_ge(d_act, NG * b + j + 1)
                            po.tensor_tensor(dbuf, dbuf, xb[:, GT * j:GT * j + GT], ALU.mult)\
                              .then_inc(d_mul, 1)

                        def time_sum(j):
                            po.wait_ge(nbr_in[j % 2], 16 * (NBR[NG - 1] * b + NBR[j]))
                            po.tensor_tensor(before[j % 2], before[j % 2], after[j % 2], ALU.add)\
                              .then_inc(nbr_sum, 1)

                        local(0)
                        time_sum(0)
                        for j in range(1, NG):
                            time_sum(j)
                            local(j)
                    po.wait_ge(setup_v, BIAS_LO)
                    po.dma_start(bu_hl[1:2], bu_f.bitcast(F32R)).then_inc(bu_out, 16)
                    po.wait_ge(bu_out, 16)

                @block.scalar
                def _(act):
                    def load(dst, src):
                        act.dma_start(dst, src).then_inc(params_in, 16)
                        n_params[0] += 16

                    with nc.allow_non_contiguous_dma(reason="small parameters"):
                        load(taus[:, 0:1], row(tau_ctx, P))
                        load(taus[:, 1:3], row(tau_raws, P))
                        load(wn2_col[:], wn2.rearrange("d p -> p d"))
                        load(bias_n2[:], row(bn2, P))
                        for d in range(2):
                            load(blend_sb[:, d], col(blend[d]))
                        load(bias_g[:], col(bg))
                        load(bias_soma[:], col(bsoma))
                        load(bias_temp[:], col(btemp))
                        load(bias_n1[:], col(bn1))
                        load(gamma_row[:], row(gamma, P))
                    assert n_params[0] == N_PARAMS
                    act.wait_ge(w1_in, 48)
                    with act.Fori(0, B) as b:
                        for j in range(NG):
                            act.wait_ge(hid_mm, NG * b + j + 1)
                            if j >= 2:
                                act.wait_ge(score_mm, NG * b + j - 1)
                            act.activation(hid[:, j % 2], bank[j % 2][:], ACT.Tanh, bias=b1_sb[:])\
                               .then_inc(hid_act, 1)
                        act.wait_ge(stat, STAT * b + S_WLOG)
                        act.activation(wcol[:], wlog[:], ACT.Exp).then_inc(wcol_act, 1)
                        act.wait_ge(wsel_zero, b + 1)
                        for r in range(P // 32):
                            at = 32 * r
                            act.activation(wsel_flat[:, at:at + (NT - 1) * (P + 1) + 1:P + 1], wlog[:],
                                           ACT.Exp).then_inc(wsel_act, 1)
                        act.wait_ge(stat, STAT * b + S_BLOG)
                        act.activation(bexp[:, :, 0:NT], blog[:], ACT.Exp).then_inc(bexp_act, 1)
                        for j in range(NG):
                            act.wait_ge(stat, STAT * b + S_PROB + j)
                            p = prob[:, GT * j:GT * j + GT]
                            act.activation(p, p, ACT.Exp).then_inc(prob_act, 1)
                        act.wait_ge(g4_mm, b + 1)
                        act.activation(g4[:], bank[5][:], ACT.Copy).then_inc(g4_cp, 1)
                        act.wait_ge(bwT_mm, b + 1)
                        act.activation(bwT[:].rearrange("p g q -> p (g q)"), bank[4][:], ACT.Copy)\
                           .then_inc(bwT_cp, 1)
                        for j in range(NG):
                            act.wait_ge(probT_mm, NG * b + j + 1)
                            if j >= 2:
                                act.wait_ge(pool_mm, NT * b + GT * (j - 1))
                            act.activation(probT[:, j % 2].rearrange("p g q -> p (g q)"), bank[j % 2][:],
                                           ACT.Copy).then_inc(probT_cp, 1)
                            if j == 1:
                                stencil_coef(act, b, 0)
                        for j in range(1, NG):
                            stencil_coef(act, b, j)
                    act.wait_ge(params_in, N_PARAMS)
                    act.activation(alpha[:], taus[:], ACT.Exp).then_inc(setup_a, 1)
                    act.wait_ge(setup_v, BLEND_SHIFTED)
                    act.activation(blend_w[:], blend_t[:, 0:2], ACT.Exp).then_inc(setup_a, 1)

                @block.tensor
                def _(pe):
                    pe.wait_ge(w1_in, 48)
                    pe.wait_ge(v_set, 1)
                    with pe.Fori(0, B) as b:
                        def hidden(j):
                            pe.wait_ge(xt_in[j % 2], 16 * (2 * b + j // 2 + 1))
                            if j >= 2:
                                pe.wait_ge(hid_act, NG * b + j - 1)
                            for k in range(KE):
                                last = pe.matmul(bank[j % 2][:], w1_sb[:, k], xt[:, SLOT[j], k],
                                                 start=(k == 0), stop=(k == KE - 1))
                            last.then_inc(hid_mm, 1)

                        def scores(j):
                            pe.wait_ge(hid_act, NG * b + j + 1)
                            if j >= 2:
                                pe.wait_ge(score_cp, NG * b + j - 1)
                            pe.matmul(bank[2 + j % 2][:], v_rep[:], hid[:, j % 2], start=True, stop=True)
                            for i in range(GT):
                                c = GT * j + i
                                last = pe.matmul(bank[6][:, c:c + 1], hid[:, j % 2, P * i:P * i + P],
                                                 v_sb[:], start=True, stop=True)
                            last.then_inc(score_mm, 1)

                        pe.wait_ge(x1_done, START + NT * b)
                        hidden(0)
                        for j in range(1, NG):
                            hidden(j)
                            scores(j - 1)
                        scores(NG - 1)
                        pe.wait_ge(setup_v, SETUP_V)
                        pe.wait_ge(pool_const, POOL_CONST)
                        pe.wait_ge(wcol_act, b + 1)
                        pe.matmul(bank[7][:, 0:NT], ones[:], wcol[:], start=True, stop=True)\
                          .then_inc(zsum_mm, 1)
                        pe.wait_ge(wsel_act, GT * (b + 1))
                        for c in range(NT):
                            if c % GT == 0:
                                pe.wait_ge(x_in[c // GT], 16 * (b + 1))
                            last = pe.matmul(bank[5][:], wsel[:, c], xb[:, c], start=(c == 0),
                                             stop=(c == NT - 1))
                        last.then_inc(g4_mm, 1)
                        pe.wait_ge(bexp_act, b + 1)
                        for u in range(GT):
                            last = pe.transpose(bank[4][:, P * u:P * u + P],
                                                bexp[:, GT * u:GT * u + GT].rearrange("p c d -> p (c d)"),
                                                ident[:])
                        last.then_inc(bwT_mm, 1)

                        def transposed(j):
                            pe.wait_ge(prob_act, NG * b + j + 1)
                            if j >= 2:
                                pe.wait_ge(probT_cp, NG * b + j - 1)
                            for i in range(GT):
                                last = pe.transpose(bank[j % 2][:, P * i:P * i + P], prob[:, GT * j + i],
                                                    ident[:])
                            last.then_inc(probT_mm, 1)

                        def pooled(j):
                            pe.wait_ge(probT_cp, NG * b + j + 1)
                            for i in range(GT):
                                c = GT * j + i
                                if c >= 4:
                                    pe.wait_ge(x1_done, START + NT * b + c - 3)
                                acc = bank[2 + c % 4][:]
                                pe.matmul(acc, probT[:, j % 2, i], xb[:, c], start=True, stop=False)
                                q = 32 * i
                                pe.matmul(acc, bwT[q:q + 32, j], g4[q:q + 32], start=False, stop=True)\
                                  .then_inc(pool_mm, 1)

                        transposed(0)
                        transposed(1)
                        pe.wait_ge(bwT_cp, b + 1)
                        pe.wait_ge(g4_cp, b + 1)
                        for j in range(NG):
                            pooled(j)
                            if j + 2 < NG:
                                transposed(j + 2)

                @block.vector
                def _(ve):
                    ve.sem_inc(x1_done, START)
                    ve.sem_inc(x2_done, START)
                    ve.sem_inc(mixed, START)
                    n = [0]

                    def step(ins):
                        n[0] += 1
                        ins.then_inc(setup_v, 1)

                    def settle():
                        ve.wait_ge(setup_v, n[0])

                    step(ve.memset(bexp[:], 0.0))
                    step(ve.memset(ones[:], 1.0))
                    ve.wait_ge(w1_in, 48)
                    ve.tensor_copy(v_rep[:], v_sb[:].broadcast_to([P, P])).then_inc(v_set, 1)
                    ve.wait_ge(coef_in, N_COEF)
                    step(ve.tensor_copy(typ[:], typ_i[:]))
                    step(ve.tensor_scalar(coef[:, 3], coef[:, 2], -1.0, None, ALU.mult))
                    step(ve.tensor_tensor(coef[:, 4], coef[:, 0], coef[:, 1], ALU.add))
                    settle()
                    step(ve.tensor_scalar(coef[:, 4], coef[:, 4], -2.0, 1.0, ALU.mult, ALU.add))
                    settle()
                    step(ve.tensor_tensor(coef[:, 4], coef[:, 4], coef[:, 2], ALU.add))
                    step(ve.tensor_scalar(sel[:, 0], typ[:], 0.0, None, ALU.is_equal))
                    step(ve.tensor_scalar(sel[:, 1], typ[:], 1.0, None, ALU.is_equal))
                    settle()
                    step(ve.tensor_tensor(sel[:, 2], sel[:, 0], sel[:, 1], ALU.add))
                    settle()
                    step(ve.tensor_scalar(sel[:, 2], sel[:, 2], -1.0, 1.0, ALU.mult, ALU.add))
                    settle()
                    ve.wait_ge(pool_const, POOL_CONST)
                    for b in range(B):
                        for dst, src in ((tmask[:, b], lambda m: hidden_m[:, m]),
                                         (bmask[:, b], lambda m: hidden_b[:, m]),
                                         (cnt[:, b], lambda m: counts[:, m])):
                            step(ve.tensor_scalar(dst, src(0), sel[:, 0, b:b + 1], None, ALU.mult))
                            settle()
                            step(ve.scalar_tensor_tensor(dst, src(1), sel[:, 1, b:b + 1], dst,
                                                         ALU.mult, ALU.add))
                            settle()
                            step(ve.scalar_tensor_tensor(dst, src(2), sel[:, 2, b:b + 1], dst,
                                                         ALU.mult, ALU.add))
                            settle()
                    step(ve.tensor_scalar(tmask, tmask, NEG, None, ALU.mult))
                    step(ve.tensor_scalar(bmask, bmask, NEG, None, ALU.mult))
                    settle()
                    assert n[0] == SETUP_V, n[0]

                    with ve.Fori(0, B) as b:
                        m = [0]

                        def link(ins, wait=True):
                            m[0] += 1
                            ins.then_inc(stat, 1)
                            if wait:
                                ve.wait_ge(stat, STAT * b + m[0])

                        one = bass.ds(b, 1)
                        ve.wait_ge(x2_done, START + NG * b)
                        link(ve.tensor_scalar(coef_b[:], coef[:, :, one].rearrange("p m o -> p (m o)"), 1.0,
                                              None, ALU.mult), False)
                        ve.memset(wsel_flat, 0.0).then_inc(wsel_zero, 1)
                        ve.wait_ge(x2_out[1], START + 16 * NG // 2 * b)
                        for j in range(NG):
                            g = slice(GT * j, GT * j + GT)
                            ve.wait_ge(score_mm, NG * b + j + 1)
                            ve.tensor_copy(s_row[:, g].rearrange("p c l -> p (c l)"),
                                           bank[2 + j % 2][:]).then_inc(score_cp, 1)
                            ve.wait_ge(score_cp, NG * b + j + 1)
                            link(ve.tensor_reduce(bmax[:, g], s_row[:, g], AX.X, ALU.max), False)
                            link(ve.tensor_tensor(prob[:, g], s_row[:, g],
                                                  tmask[:, one].broadcast_to([P, GT, P]), ALU.add))
                            link(ve.tensor_reduce(imax[:, g], prob[:, g], AX.X, ALU.max), False)
                        ve.wait_ge(stat, STAT * b + m[0])
                        link(ve.tensor_tensor(wlog[:], bank[6][:, 0:NT], bmax[:], ALU.subtract), False)
                        assert m[0] == S_WLOG
                        link(ve.tensor_tensor(
                            blog[:], bmask[:, one].rearrange("p o c d -> p (o c) d"),
                            bmax[:].rearrange("p (o c) -> p o c", o=1).broadcast_to([P, NT, NT]), ALU.add))
                        link(ve.tensor_reduce(omax[:], blog[:], AX.X, ALU.max))
                        link(ve.tensor_tensor(rmax[:], imax[:], omax[:], ALU.max))
                        link(ve.tensor_tensor(
                            blog[:], blog[:],
                            rmax[:].rearrange("p (c o) -> p c o", o=1).broadcast_to([P, NT, NT]),
                            ALU.subtract), False)
                        assert m[0] == S_BLOG
                        for j in range(NG):
                            g = slice(GT * j, GT * j + GT)
                            link(ve.tensor_tensor(
                                prob[:, g], prob[:, g],
                                rmax[:, g].rearrange("p (c o) -> p c o", o=1).broadcast_to([P, GT, P]),
                                ALU.subtract), False)
                            assert m[0] == S_PROB + j
                        ve.wait_ge(zsum_mm, b + 1)
                        link(ve.tensor_copy(zblk[:], bank[7][:, 0:NT]), False)
                        ve.wait_ge(bexp_act, b + 1)
                        ve.wait_ge(stat, STAT * b + m[0])
                        link(ve.tensor_tensor(
                            bwz[:], bexp[:, :, 0:NT],
                            zblk[:].rearrange("p (o c) -> p o c", o=1).broadcast_to([P, NT, NT]), ALU.mult))
                        link(ve.tensor_reduce(zout[:], bwz[:], AX.X, ALU.add), False)
                        ve.wait_ge(prob_act, NG * (b + 1))
                        link(ve.tensor_reduce(zin[:], prob[:], AX.X, ALU.add))
                        link(ve.tensor_tensor(zin[:], zin[:], zout[:], ALU.add))
                        assert m[0] == STAT, m[0]
                        ve.tensor_tensor(rnorm[:], zin[:], cnt[:, one].rearrange("p o c -> p (o c)"),
                                         ALU.mult).then_inc(q_chain, 1)
                        ve.wait_ge(q_chain, Q_CHAIN * b + 1)
                        ve.reciprocal(rnorm[:], rnorm[:]).then_inc(q_chain, 1)
                        ve.wait_ge(q_chain, Q_CHAIN * b + 2)

                        def stencil(j):
                            xg = xb[:, GT * j:GT * j + GT]
                            flat = lambda a: a.rearrange("p c e -> p (c e)")
                            ve.wait_ge(d_mul, NG * b + j + 1)
                            ve.wait_ge(nbr_sum, NG * b + j + 1)
                            ve.scalar_tensor_tensor(flat(before[j % 2]), flat(before[j % 2]),
                                                    coef_b[:, 1:2], flat(dbuf), ALU.mult, ALU.add)\
                              .then_inc(mixed, 1)
                            if j == 1:
                                ve.wait_ge(probT_mm, NG * (b + 1))
                            else:
                                ve.wait_ge(x2_out[j % 2], START + 16 * (NG // 2 * b + j // 2))
                            q = qbuf[j % 2]
                            ve.tensor_tensor(q[:, :, 1:E - 1], xg[:, :, 0:E - 2], xg[:, :, 2:E],
                                             ALU.add).then_inc(q_chain, 1)
                            ve.tensor_scalar(q[:, :, 0:1], xg[:, :, 1:2], 2.0, None, ALU.mult)\
                              .then_inc(q_chain, 1)
                            ve.tensor_scalar(q[:, :, E - 1:E], xg[:, :, E - 2:E - 1], 2.0, None,
                                             ALU.mult).then_inc(q_chain, 1)
                            ve.wait_ge(q_chain, Q_CHAIN * b + 2 + 3 * (j + 1))
                            ve.wait_ge(mixed, START + NG * b + j + 1)
                            ve.scalar_tensor_tensor(flat(q), flat(q), coef_b[:, 0:1],
                                                    flat(before[j % 2]), ALU.mult, ALU.add)\
                              .then_inc(x2_done, 1)

                        for c in range(NT):
                            ve.wait_ge(pool_mm, NT * b + c + 1)
                            ve.scalar_tensor_tensor(xb[:, c], bank[2 + c % 4][:], rnorm[:, c:c + 1],
                                                    xb[:, c], ALU.mult, ALU.add).then_inc(x1_done, 1)
                            if c == 3 * GT:
                                stencil(0)
                        for j in range(1, NG):
                            stencil(j)
                    ve.wait_ge(params_in, N_PARAMS)
                    step(ve.tensor_tensor(blend_t[:, 2], blend_sb[:, 0], blend_sb[:, 1], ALU.max))
                    settle()
                    for d in range(2):
                        step(ve.tensor_tensor(blend_t[:, d], blend_sb[:, d], blend_t[:, 2], ALU.subtract))
                    assert n[0] == BLEND_SHIFTED, n[0]
                    for d in range(2):
                        step(ve.tensor_copy(wn2_rep[:, d], wn2_col[:, d:d + 1].broadcast_to([P, P])))
                    step(ve.tensor_copy(ones2[:], ones[0:2, :]))
                    ve.wait_ge(setup_a, 1)
                    step(ve.tensor_scalar(alpha[:], alpha[:], 1.0, None, ALU.add))
                    settle()
                    step(ve.reciprocal(alpha[:], alpha[:]))
                    ve.wait_ge(setup_a, 2)
                    step(ve.tensor_tensor(blend_t[:, 2], blend_w[:, 0], blend_w[:, 1], ALU.add))
                    settle()
                    step(ve.reciprocal(blend_t[:, 2], blend_t[:, 2]))
                    settle()
                    for d in range(2):
                        step(ve.tensor_tensor(blend_w[:, d], blend_w[:, d], blend_t[:, 2], ALU.mult))
                    ve.wait_ge(rows_in, 16 * 4 * B)
                    ve.wait_ge(late_in, 16 * (B + 1))
                    step(ve.tensor_copy(bu_hl[0:1], bu_f))
                    settle()
                    step(ve.tensor_tensor(bu_f.bitcast(F32R), bu_f, f32(bu_hl[0:1]), ALU.subtract))
                    assert n[0] == BIAS_LO, n[0]
                    for b in range(B):
                        step(ve.tensor_tensor(shift_row[:, b], shift_row[:, b], beta_row[:], ALU.add))
                    settle()

        dw_h = sb("dw_h", [P, KE, A], F32R)
        dw_l = sb("dw_l", [P, KE, A], F32R)
        uw_h = sb("uw_h", [P, E], F32R)
        uw_l = sb("uw_l", [P, E], F32R)
        res = sb("res", [P, GT, E])
        ph = sb("ph", [P, KE, GN], F32R)
        pl = sb("pl", [P, KE, GN], F32R)
        xh = sb("xh", [P, KE, GN], F32R)
        xl = sb("xl", [P, KE, GN], F32R)
        th = sb("th", [P, KE, GN], F32R)
        tl = sb("tl", [P, KE, GN], F32R)
        narrow = sb("narrow", [P, GN])
        zh = sb("zh", [P, GN], F32R)
        zl = sb("zl", [P, GN], F32R)
        wide = sb("wide", [P, 2, GN])
        wgb = sb("wgb", [P, 2, GN])
        tr = sb("tr", [P, 2, 2, GN])
        soma = sb("soma", [P, KE, GN])
        carry = sb("carry", [P, KE, 3])
        keep = sb("keep", [P, GROUPS])
        st_a = sb("st_a", [P, GT, 6])
        mv_a = sb("mv_a", [P, GT, 2])
        rs_a = sb("rs_a", [P, GT])
        st_o = sb("st_o", [P, GT, 6])
        mv_o = sb("mv_o", [P, GT, 2])
        rs_o = sb("rs_o", [P, GT])

        lw_split = sem("lw_split")
        x2T_mm = sem("x2T_mm")
        x2T_hi = sem("x2T_hi")
        x2T_lo = sem("x2T_lo")
        down_mm = sem("down_mm")
        z_act = sem("z_act")
        z_hi = sem("z_hi")
        z_lo = sem("z_lo")
        up_mm = sem("up_mm")
        y_add = sem("y_add")
        ln_mv = sem("ln_mv")
        ln_p = sem("ln_p")
        ln_rs = sem("ln_rs")
        ln_w = sem("ln_w")
        x3_done = sem("x3_done")
        x3T_mm = sem("x3T_mm")
        x3T_hi = sem("x3T_hi")
        x3T_lo = sem("x3T_lo")
        residual = sem("residual")
        n1_mm = sem("n1_mm")
        n1_act = sem("n1_act")
        mod_mm = sem("mod_mm")
        mod_sig = sem("mod_sig")
        mod_add = sem("mod_add")
        pre_mm = sem("pre_mm")
        ctx_mm = sem("ctx_mm")
        ctx_scan = sem("ctx_scan")
        pre_add = sem("pre_add")
        ctx_kept = sem("ctx_kept")
        wg_act = sem("wg_act")
        xsum_done = sem("xsum_done")
        gated = sem("gated")
        tr_in = sem("tr_in")
        tr_scan = sem("tr_scan")
        carried = sem("carried")
        blended = sem("blended")
        t_hi = sem("t_hi")
        t_lo = sem("t_lo")
        soma_mm = sem("soma_mm")
        soma_act = sem("soma_act")
        temp_mm = sem("temp_mm")
        gate_act = sem("gate_act")
        prod = sem("prod")
        prod_hi = sem("prod_hi")
        prod_lo = sem("prod_lo")
        out_mm = sem("out_mm")
        o_mv = sem("o_mv")
        o_p = sem("o_p")
        o_rs = sem("o_rs")
        out_free = sem("out_free")
        o_done = sem("o_done")
        o_out = sem("o_out")
        p2_v = sem("p2_v")
        cols_set = sem("cols_set")

        N1, PRE, CTX, MOD = 4, (5, 0, 2, 5), (6, 1, 3, 6), (7, 4)
        X2T, SOMA, DOWN, UP = (4, 7, 0, 1), (2, 3, 5, 2), 6, (4, 7, 0, 1)
        TEMP, OUT, X3T = (3, 5, 6, 2), (0, 1, 3, 2), (4, 5, 6, 7)

        with nc.Block() as block:

            @block.sync
            def _(sp):
                sp.sem_inc(o_out, START)
                out_v = out.rearrange("b (u c p) e -> p (b u) c e", p=P, c=GT)

                def store(g):
                    sp.wait_ge(o_done, START + GT * g + GT)
                    sp.dma_start(out_v[:, bass.ds(g, 1)].rearrange("p u c e -> p (u c) e"), res[:])\
                      .then_inc(o_out, 16)

                with sp.Fori(0, GROUPS - 1) as g:
                    sp.wait_ge(x3T_mm, KE * g + KE)
                    sp.wait_ge(residual, GT * g + GT)
                    load_group(sp, g + 1)
                    sp.wait_ge(lw_split, 4 * g + 4)
                    load_adapter(sp, g + 1)
                    store(g)
                store(GROUPS - 1)
                sp.wait_ge(o_out, START + 16 * GROUPS)

            @block.tensor
            def _(pe):
                pe.sem_inc(temp_mm, START)
                pe.sem_inc(out_mm, START)
                def split3(acc, wh, wl, xh_, xl_, first=True, last=True):
                    n = len(wh)
                    for k in range(n):
                        pe.matmul(acc, wl[k], xh_[k], start=(first and k == 0), stop=False)
                        pe.matmul(acc, wh[k], xl_[k], start=False, stop=False)
                        ins = pe.matmul(acc, wh[k], xh_[k], start=False, stop=(last and k == n - 1))
                    return ins

                ks = range(KE)

                def x2_transposes(q, g):
                    pe.wait_ge(x2_in, 16 * (q + 1))
                    if g is not None:
                        pe.wait_ge(mod_sig, 2 * g + 2)
                        pe.wait_ge(pre_add, KE * g + 2)
                    for k in ks:
                        for c in range(GT):
                            last = pe.transpose(bank[X2T[k]][:, P * c:P * c + P],
                                                xa[:, c, P * k:P * k + P], ident[:])
                        last.then_inc(x2T_mm, 1)

                def down(q, g):
                    if g is not None:
                        pe.wait_ge(ctx_scan, KE * g + 4)
                    pe.wait_ge(lw_split, 4 * q + 4)
                    pe.wait_ge(x2T_lo, KE * q + KE)
                    split3(bank[DOWN][:], [dw_h[:, k] for k in ks], [dw_l[:, k] for k in ks],
                           [ph[:, k] for k in ks], [pl[:, k] for k in ks]).then_inc(down_mm, 1)

                def up(q):
                    pe.wait_ge(z_lo, q + 1)
                    bu = bu_hl[:, bass.ds(q // NG, 1)].rearrange("p o e -> p (o e)")
                    for c in range(GT):
                        t = slice(P * c, P * c + P)
                        acc = bank[UP[c]][:]
                        split3(acc, [zh[:, t]], [zl[:, t]], [uw_h[:]], [uw_l[:]], last=False)
                        pe.matmul(acc, ones2[:], bu, start=False, stop=True).then_inc(up_mm, 1)

                def x3_transposes(q):
                    pe.wait_ge(x3_done, GT * q + GT)
                    for k in ks:
                        for c in range(GT):
                            last = pe.transpose(bank[X3T[k]][:, P * c:P * c + P],
                                                xa[:, c, P * k:P * k + P], ident[:])
                        last.then_inc(x3T_mm, 1)

                def wx(w_h, w_l, off, k):
                    m = slice(P * k, P * k + P)
                    return ([w_h[:, off + i, m] for i in ks], [w_l[:, off + i, m] for i in ks],
                            [xh[:, i] for i in ks], [xl[:, i] for i in ks])

                def front(g):
                    pe.wait_ge(x3T_lo, KE * g + KE)
                    split3(bank[N1][:], [wn1_h[:, i] for i in ks], [wn1_l[:, i] for i in ks],
                           [xh[:, i] for i in ks], [xl[:, i] for i in ks]).then_inc(n1_mm, 1)
                    for k in ks:
                        if k == 1:
                            pe.wait_ge(out_free, START + GT * g)
                        if k == 3:
                            pe.wait_ge(pre_add, KE * g + 1)
                        split3(bank[PRE[k]][:], *wx(wg_h, wg_l, 0, k)).then_inc(pre_mm, 1)
                        if k == 3:
                            pe.wait_ge(ctx_scan, KE * g + 1)
                        split3(bank[CTX[k]][:], *wx(wg_h, wg_l, KE, k)).then_inc(ctx_mm, 1)
                        if k == 0:
                            pe.wait_ge(n1_act, g + 1)
                            for d in range(2):
                                pe.matmul(bank[MOD[d]][:], wn2_rep[:, d], narrow[:], start=True,
                                          stop=True).then_inc(mod_mm, 1)

                def soma_in(g, k):
                    if k == 0:
                        pe.wait_ge(pre_add, KE * g + 3)
                    elif k == 1:
                        pe.wait_ge(ctx_scan, KE * g + 3)
                    elif k == 2:
                        pe.wait_ge(pre_add, KE * g + 4)
                    else:
                        pe.wait_ge(soma_act, KE * g + 1)
                    split3(bank[SOMA[k]][:], *wx(ws_h, ws_l, 0, k)).then_inc(soma_mm, 1)

                def temporal(g):
                    pe.wait_ge(t_lo, KE * g + KE)
                    for k in ks:
                        if k < 2:
                            pe.wait_ge(soma_act, KE * g + k + 2)
                        elif k == 3:
                            pe.wait_ge(soma_act, KE * g + 4)
                        m = slice(P * k, P * k + P)
                        split3(bank[TEMP[k]][:], [wt_h[:, i, m] for i in ks],
                               [wt_l[:, i, m] for i in ks], [th[:, i] for i in ks],
                               [tl[:, i] for i in ks]).then_inc(temp_mm, 1)

                def output_part(c, ki, **flags):
                    t = slice(P * c, P * c + P)
                    return split3(bank[OUT[c]][:], [ph[:, i, t] for i in ki], [pl[:, i, t] for i in ki],
                                  [wo_h[:, i] for i in ki], [wo_l[:, i] for i in ki], **flags)

                def output(g, adapted=True):
                    if adapted:
                        pe.wait_ge(y_add, GT * (g + 1) + GT)
                    for k in range(KE - 1):
                        pe.wait_ge(prod_lo, START + KE * g + k + 1)
                        for c in range(GT - 1):
                            output_part(c, [k], first=(k == 0), last=False)
                    pe.wait_ge(prod_lo, START + KE * g + KE)
                    for c in range(GT - 1):
                        output_part(c, [KE - 1], first=False).then_inc(out_mm, 1)

                def output_rest():
                    output_part(GT - 1, ks).then_inc(out_mm, 1)

                x2_transposes(0, None)
                down(0, None)
                up(0)
                x3_transposes(0)
                with pe.Fori(0, LAST) as g:
                    front(g)
                    x2_transposes(g + 1, g)
                    soma_in(g, 0)
                    soma_in(g, 1)
                    soma_in(g, 2)
                    down(g + 1, g)
                    soma_in(g, 3)
                    up(g + 1)
                    temporal(g)
                    output(g)
                    x3_transposes(g + 1)
                    output_rest()
                front(LAST)
                for k in ks:
                    soma_in(LAST, k)
                temporal(LAST)
                output(LAST, adapted=False)
                output_rest()

            @block.scalar
            def _(act):
                def x2_halves(q, first=False):
                    if not first:
                        act.wait_ge(out_mm, START + GT * (q - 1))
                    for k in range(KE):
                        act.wait_ge(x2T_mm, KE * q + k + 1)
                        act.activation(ph[:, k], bank[X2T[k]][:], ACT.Copy).then_inc(x2T_hi, 1)

                def relu(q):
                    act.wait_ge(down_mm, q + 1)
                    act.wait_ge(cols_set, q + 1)
                    act.activation(narrow[:], bank[DOWN][:], ACT.Relu,
                                   bias=cols[:, 0:1]).then_inc(z_act, 1)
                    act.wait_ge(z_act, q + 1)
                    act.activation(zh[:], narrow[:], ACT.Copy).then_inc(z_hi, 1)

                def x3_halves(q):
                    act.wait_ge(gated, KE * q)
                    for k in range(KE):
                        act.wait_ge(x3T_mm, KE * q + k + 1)
                        act.activation(xh[:, k], bank[X3T[k]][:], ACT.Identity,
                                       bias=cols[:, 1 + k:2 + k]).then_inc(x3T_hi, 1)

                def sigmoid_gate(g, k):
                    act.wait_ge(pre_add, KE * g + k + 1)
                    act.activation(wgb[:, k % 2], wgb[:, k % 2], ACT.Sigmoid, bias=bias_g[:, k:k + 1])\
                       .then_inc(wg_act, 1)

                def trace_hi(g, k):
                    act.wait_ge(blended, KE * g + k + 1)
                    act.activation(th[:, k], tr[:, k % 2, 1], ACT.Copy).then_inc(t_hi, 1)

                def front(g, adapted=True):
                    act.wait_ge(n1_mm, g + 1)
                    act.activation(narrow[:], bank[N1][:], ACT.Gelu, bias=bias_n1[:]).then_inc(n1_act, 1)
                    sigmoid_gate(g, 0)
                    act.wait_ge(prod_lo, START + KE * g)
                    for d in range(2):
                        act.wait_ge(mod_mm, 2 * g + d + 1)
                        act.activation(wide[:, d], bank[MOD[d]][:], ACT.Sigmoid,
                                       bias=bias_n2[:, d:d + 1]).then_inc(mod_sig, 1)
                    sigmoid_gate(g, 1)
                    act.wait_ge(temp_mm, START + KE * g)
                    sigmoid_gate(g, 2)
                    trace_hi(g, 0)
                    if adapted:
                        x2_halves(g + 1)
                    sigmoid_gate(g, 3)
                    trace_hi(g, 1)
                    soma_gelu(g, 0)

                def soma_gelu(g, k):
                    act.wait_ge(soma_mm, KE * g + k + 1)
                    act.activation(soma[:, k], bank[SOMA[k]][:], ACT.Gelu,
                                   bias=bias_soma[:, k:k + 1]).then_inc(soma_act, 1)

                def gate(g):
                    for k in range(KE):
                        act.wait_ge(temp_mm, START + KE * g + k + 1)
                        if k >= 2:
                            act.wait_ge(prod_lo, START + KE * g + k - 1)
                        act.activation(wide[:, k % 2], bank[TEMP[k]][:], ACT.Sigmoid,
                                       bias=bias_temp[:, k:k + 1]).then_inc(gate_act, 1)
                        if k >= 1:
                            product_hi(g, k - 1)
                    product_hi(g, KE - 1)

                def product_hi(g, k):
                    act.wait_ge(prod, KE * g + k + 1)
                    act.activation(ph[:, k], wide[:, k % 2], ACT.Copy).then_inc(prod_hi, 1)

                x2_halves(0, first=True)
                relu(0)
                x3_halves(0)
                with act.Fori(0, LAST) as g:
                    front(g)
                    trace_hi(g, 2)
                    soma_gelu(g, 1)
                    soma_gelu(g, 2)
                    relu(g + 1)
                    trace_hi(g, 3)
                    soma_gelu(g, 3)
                    gate(g)
                    x3_halves(g + 1)
                front(LAST, adapted=False)
                trace_hi(LAST, 2)
                soma_gelu(LAST, 1)
                soma_gelu(LAST, 2)
                trace_hi(LAST, 3)
                soma_gelu(LAST, 3)
                act.wait_ge(out_mm, START + GT * LAST)
                gate(LAST)

            @block.gpsimd
            def _(po):
                def split_weights(q):
                    po.wait_ge(lw_in, 32 * (q + 1))
                    po.wait_ge(up_mm, GT * q)
                    po.tensor_tensor(dw_h[:].rearrange("p k a -> p (k a)"), dw_f[:].rearrange("p k a -> p (k a)"),
                                     ONE.broadcast_to([P, KE * A]), ALU.mult).then_inc(lw_split, 1)
                    po.tensor_tensor(uw_h[:], uw_f[:], ONE.broadcast_to([P, E]), ALU.mult).then_inc(lw_split, 1)
                    po.wait_ge(lw_split, 4 * q + 2)
                    po.tensor_tensor(dw_l[:], dw_f[:], f32(dw_h[:]), ALU.subtract).then_inc(lw_split, 1)
                    po.tensor_tensor(uw_l[:], uw_f[:], f32(uw_h[:]), ALU.subtract).then_inc(lw_split, 1)

                def rstd(mean_ready, mv, rs, n, chain, done, c):
                    po.wait_ge(mean_ready, n + 1)
                    po.tensor_tensor(rs[:, c:c + 1], mv[:, c, 1:2], EPSILON, ALU.add).then_inc(chain, 1)
                    po.wait_ge(chain, n + 1)
                    po.tensor_tensor(rs[:, c:c + 1], rs[:, c:c + 1], NEG_HALF, ALU.pow)\
                      .then_inc(done, 1)

                def resid(g):
                    po.wait_ge(x3_done, GT * g + GT)
                    po.wait_ge(o_out, START + 16 * g)
                    for c in range(GT):
                        po.tensor_tensor(res[:, c], xa[:, c],
                                         shift_row[:, bass.ds(g // NG, 1)].rearrange("p o e -> p (o e)"),
                                         ALU.add).then_inc(residual, 1)

                def front(g):
                    po.wait_ge(mod_sig, 2 * g + 2)
                    po.tensor_tensor(wide[:], wide[:], HALF.rearrange("p (o n) -> p o n", o=1).broadcast_to([P, 2, GN]),
                                     ALU.add).then_inc(mod_add, 1)
                    for k in range(KE):
                        po.wait_ge(x3T_lo, KE * g + KE)
                        po.tensor_tensor(soma[:, k], f32(xh[:, k]), f32(xl[:, k]), ALU.add)\
                          .then_inc(xsum_done, 1)
                        po.wait_ge(xsum_done, KE * g + k + 1)
                        po.wait_ge(wg_act, KE * g + k + 1)
                        po.tensor_tensor(wgb[:, k % 2], soma[:, k], wgb[:, k % 2], ALU.mult)\
                          .then_inc(gated, 1)
                        if k == 0:
                            resid(g)

                def ln(q, c):
                    rstd(ln_mv, mv_a, rs_a, GT * q + c, ln_p, ln_rs, c)

                def product(g, k):
                    po.wait_ge(gate_act, KE * g + k + 1)
                    po.tensor_tensor(wide[:, k % 2], soma[:, k], wide[:, k % 2], ALU.mult)\
                      .then_inc(prod, 1)

                def out_ln(g):
                    for c in range(GT):
                        rstd(o_mv, mv_o, rs_o, GT * g + c, o_p, o_rs, c)

                split_weights(0)
                for c in range(GT):
                    ln(0, c)
                with po.Fori(0, LAST) as g:
                    front(g)
                    split_weights(g + 1)
                    ln(g + 1, 0)
                    ln(g + 1, 1)
                    ln(g + 1, 2)
                    product(g, 0)
                    ln(g + 1, 3)
                    product(g, 1)
                    product(g, 2)
                    product(g, 3)
                    out_ln(g)
                front(LAST)
                for k in range(KE):
                    product(LAST, k)
                out_ln(LAST)

            @block.vector
            def _(ve):
                ve.sem_inc(out_free, START)
                ve.sem_inc(prod_lo, START)
                ve.sem_inc(ctx_kept, START)
                ve.sem_inc(o_done, START)
                ve.memset(keep[:], 1.0).then_inc(p2_v, 1)
                ve.memset(carry[:], 0.0).then_inc(p2_v, 1)
                ve.wait_ge(p2_v, 2)
                for b in range(B):
                    last = (b + 1) * NG - 1
                    ve.memset(keep[:, last:last + 1], 0.0).then_inc(p2_v, 1)
                ve.wait_ge(p2_v, 2 + B)

                def set_cols(q):
                    ve.wait_ge(x3T_lo, KE * q)
                    ve.tensor_scalar(cols[:], cols_all[:, bass.ds(q // NG, 1)].rearrange("p o c -> p (o c)"),
                                     1.0, None, ALU.mult).then_inc(cols_set, 1)

                def x2_lo(q):
                    for k in range(KE):
                        ve.wait_ge(x2T_hi, KE * q + k + 1)
                        ve.tensor_tensor(pl[:, k], bank[X2T[k]][:], f32(ph[:, k]), ALU.subtract)\
                          .then_inc(x2T_lo, 1)

                def relu_lo(q):
                    ve.wait_ge(z_hi, q + 1)
                    ve.tensor_tensor(zl[:], narrow[:], f32(zh[:]), ALU.subtract).then_inc(z_lo, 1)

                def moments(acc, st, mv, c, done):
                    ve.bn_stats(st[:, c], acc)
                    ve.drain()
                    ve.bn_aggr(mv[:, c], st[:, c]).then_inc(done, 1)

                def ln_stats(q, c):
                    y = tr[:, c % 2, 0]
                    ve.wait_ge(up_mm, GT * q + c + 1)
                    if c >= 2:
                        ve.wait_ge(x3_done, GT * q + c - 1)
                    ve.tensor_tensor(y, bank[UP[c]][:], xa[:, c], ALU.add).then_inc(y_add, 1)
                    ve.wait_ge(y_add, GT * q + c + 1)
                    moments(y, st_a, mv_a, c, ln_mv)

                def ln_apply(q, c):
                    y = tr[:, c % 2, 0]
                    ve.wait_ge(ln_mv, GT * q + c + 1)
                    ve.scalar_tensor_tensor(
                        y, y, mv_a[:, c, 0:1],
                        ln_g_row[:, bass.ds(q // NG, 1)].rearrange("p o e -> p (o e)"),
                        ALU.subtract, ALU.mult).then_inc(ln_w, 1)
                    ve.wait_ge(ln_w, GT * q + c + 1)
                    ve.wait_ge(ln_rs, GT * q + c + 1)
                    ve.scalar_tensor_tensor(xa[:, c], y, rs_a[:, c:c + 1], xa[:, c], ALU.mult, ALU.add)\
                      .then_inc(x3_done, 1)

                def x3_lo(q):
                    for k in range(KE):
                        ve.wait_ge(x3T_hi, KE * q + k + 1)
                        ve.scalar_tensor_tensor(xl[:, k], bank[X3T[k]][:],
                                                cols[:, 1 + k:2 + k], f32(xh[:, k]),
                                                ALU.add, ALU.subtract).then_inc(x3T_lo, 1)

                def logits(g, k):
                    w = wgb[:, k % 2]
                    h = tr[:, k % 2, 0]
                    if k >= 2:
                        ve.wait_ge(blended, KE * g + k - 1)
                    else:
                        ve.wait_ge(o_done, START + GT * g)
                    ve.wait_ge(ctx_mm, KE * g + k + 1)
                    ve.wait_ge(ctx_kept, START + KE * g + k)
                    ve.tensor_tensor_scan(h, alpha[:, 0:1].broadcast_to([P, GN]), bank[CTX[k]][:],
                                          carry[:, k, 0:1], ALU.mult, ALU.add).then_inc(ctx_scan, 1)
                    ve.wait_ge(ctx_scan, KE * g + k + 1)
                    ve.tensor_scalar(carry[:, k, 0:1], h[:, GN - 1:GN], keep[:, bass.ds(g, 1)], None,
                                     ALU.mult).then_inc(ctx_kept, 1)
                    ve.wait_ge(pre_mm, KE * g + k + 1)
                    ve.tensor_tensor(w, bank[PRE[k]][:], h, ALU.add).then_inc(pre_add, 1)

                def traces(g, k):
                    t = tr[:, k % 2]
                    if k == 0:
                        ve.wait_ge(mod_add, g + 1)
                    if k >= 2:
                        ve.wait_ge(t_lo, KE * g + k - 1)
                    ve.wait_ge(ctx_kept, START + KE * g + k + 1)
                    ve.wait_ge(gated, KE * g + k + 1)
                    for d in range(2):
                        ve.scalar_tensor_tensor(t[:, d], wgb[:, k % 2], blend_w[:, d, k:k + 1],
                                                wide[:, d], ALU.mult, ALU.mult).then_inc(tr_in, 1)
                    for d in range(2):
                        ve.wait_ge(tr_in, 2 * (KE * g + k) + d + 1)
                        ve.tensor_tensor_scan(t[:, d], alpha[:, 1 + d:2 + d].broadcast_to([P, GN]),
                                              t[:, d], carry[:, k, 1 + d:2 + d], ALU.mult, ALU.add)\
                          .then_inc(tr_scan, 1)
                    ve.wait_ge(tr_scan, 2 * (KE * g + k + 1))
                    ve.tensor_scalar(carry[:, k, 1:3], t[:, :, GN - 1], keep[:, bass.ds(g, 1)], None,
                                     ALU.mult).then_inc(carried, 1)
                    ve.wait_ge(carried, KE * g + k + 1)
                    ve.tensor_tensor(t[:, 1], t[:, 0], t[:, 1], ALU.add).then_inc(blended, 1)

                def trace_lo(g, k):
                    ve.wait_ge(t_hi, KE * g + k + 1)
                    ve.tensor_tensor(tl[:, k], tr[:, k % 2, 1], f32(th[:, k]), ALU.subtract)\
                      .then_inc(t_lo, 1)

                def front(g, adapted=True):
                    logits(g, 0)
                    logits(g, 1)
                    traces(g, 0)
                    logits(g, 2)
                    traces(g, 1)
                    trace_lo(g, 0)
                    logits(g, 3)
                    traces(g, 2)
                    trace_lo(g, 1)
                    if adapted:
                        x2_lo(g + 1)
                    traces(g, 3)
                    trace_lo(g, 2)
                    if adapted:
                        relu_lo(g + 1)
                    trace_lo(g, 3)

                def product_lo(g, k):
                    ve.wait_ge(prod_hi, KE * g + k + 1)
                    ve.tensor_tensor(pl[:, k], wide[:, k % 2], f32(ph[:, k]), ALU.subtract)\
                      .then_inc(prod_lo, 1)

                def out_stats(g, c):
                    ve.wait_ge(out_mm, START + GT * g + c + 1)
                    moments(bank[OUT[c]][:], st_o, mv_o, c, o_mv)

                def out_apply(g, c):
                    t = tr[:, c % 2, 0]
                    ve.wait_ge(o_mv, GT * g + c + 1)
                    ve.scalar_tensor_tensor(t, bank[OUT[c]][:], mv_o[:, c, 0:1], gamma_row[:],
                                            ALU.subtract, ALU.mult).then_inc(out_free, 1)
                    ve.wait_ge(out_free, START + GT * g + c + 1)
                    ve.wait_ge(o_rs, GT * g + c + 1)
                    ve.scalar_tensor_tensor(res[:, c], t, rs_o[:, c:c + 1], res[:, c], ALU.mult,
                                            ALU.add).then_inc(o_done, 1)

                def output(g, adapted=True):
                    ve.wait_ge(residual, GT * g + GT)
                    if adapted:
                        ve.wait_ge(x3_done, GT * (g + 1) + GT)
                    out_stats(g, 0)
                    out_stats(g, 1)
                    if adapted:
                        x3_lo(g + 1)
                    out_stats(g, 2)
                    out_apply(g, 0)
                    out_apply(g, 1)
                    out_stats(g, 3)
                    out_apply(g, 2)
                    out_apply(g, 3)

                set_cols(0)
                x2_lo(0)
                relu_lo(0)
                ln_stats(0, 0)
                for c in range(1, GT):
                    ln_stats(0, c)
                    ln_apply(0, c - 1)
                ln_apply(0, GT - 1)
                x3_lo(0)
                with ve.Fori(0, LAST) as g:
                    set_cols(g + 1)
                    front(g)
                    ln_stats(g + 1, 0)
                    ln_stats(g + 1, 1)
                    ln_apply(g + 1, 0)
                    ln_stats(g + 1, 2)
                    ln_apply(g + 1, 1)
                    ln_stats(g + 1, 3)
                    ln_apply(g + 1, 2)
                    product_lo(g, 0)
                    ln_apply(g + 1, 3)
                    for k in range(1, KE):
                        product_lo(g, k)
                    output(g)
                front(LAST, adapted=False)
                for k in range(KE):
                    product_lo(LAST, k)
                output(LAST, adapted=False)


def kernel(**inputs):
    import numpy as np
    import concourse.bacc as bacc
    from concourse.bass_utils import run_bass_kernel_spmd

    i = {k: np.asarray(a) for k, a in inputs.items()}
    flip = lambda a: np.ascontiguousarray(a.T)
    arrays = {
        "x": i["x"],
        "xT": np.ascontiguousarray(i["x"].transpose(0, 2, 1)),
        "ptype": i["itok_B_0_2"],
        "zx": i["condB_zX"],
        "zy": i["condB_zY"],
        "zr": i["condB_zR"],
        "profile": i["itok_B_0_6"],
        "tau_raws": i["condB_tauraws"],
        "wn2": i["cond_256"],
        "bn2": i["condB_bn2"],
        "blend": i["cond_1024"],
        "w1": i["L0_cond_W1"],
        "b1": i["L0_cond_b1"],
        "v": i["L0_cond_v"],
        "down_w": i["L2_cond_down_w"],
        "down_b": i["L2_cond_down_b"],
        "up_w": i["L2_cond_up_w"],
        "up_b": i["L2_cond_up_b"],
        "ln_g": i["L2_cond_ln_g"],
        "ln_b": i["L2_cond_ln_b"],
        "tau_ctx": i["L3_cond_tau_ctx"].reshape(1),
        "wg": flip(i["L3_cond_Wg"]),
        "bg": i["L3_cond_bg"],
        "wn1": flip(i["L3_cond_Wn1"]),
        "bn1": i["L3_cond_bn1"],
        "wsoma": flip(i["L3_cond_Wsoma"]),
        "bsoma": i["L3_cond_bsoma"],
        "wtemp": flip(i["L3_cond_Wtemp"]),
        "btemp": i["L3_cond_btemp"],
        "wout": flip(i["L3_cond_Wout"]),
        "gamma": i["L3_cond_gamma"],
        "beta": i["L3_cond_beta"],
    }
    arrays = {k: np.ascontiguousarray(a) for k, a in arrays.items()}
    nc = bacc.Bacc("TRN2", target_bir_lowering=False, num_devices=1)
    args = {k: nc.dram_tensor(f"in_{k}", a.shape, mybir.dt.from_np(a.dtype), kind="ExternalInput").ap()
            for k, a in arrays.items()}
    args["out"] = nc.dram_tensor("result", (B, T, E), F32, kind="ExternalOutput").ap()
    build_program(nc, **args)
    r = run_bass_kernel_spmd(nc, [{f"in_{k}": a for k, a in arrays.items()}], core_ids=[0])
    return r.results[0]["result"]
```

```python
from contextlib import ExitStack

import concourse.bass as bass
from concourse import mybir

F32 = mybir.dt.float32
F32R = mybir.dt.float32r
I32 = mybir.dt.int32
ALU = mybir.AluOpType
ACT = mybir.ActivationFunctionType
AX = mybir.AxisListType

P = 128
B, T, E = 2, 2048, 512
A = 128
KE = E // P
NT = T // P
GT = 4
GN = GT * P
NG = NT // GT
GROUPS = B * NG
LAST = GROUPS - 1
NEG = -1e30
EPS = 1e-5

N_COEF = 16 * 4
N_PARAMS = 16 * 10
POOL_CONST = 24
SETUP_V = 31
BLEND_SHIFTED = SETUP_V + 3
S_WLOG, S_BLOG, S_PROB, STAT = 12, 18, 19, 27
BY_ACT = 2
START = 1
Q_CHAIN = 2 + 3 * (NG - 1)
NBR = [5, 4]
DS = 2


def build_program(nc, x, xT, ptype, zx, zy, zr, profile, tau_raws, wn2, bn2, blend, w1, b1, v,
                  down_w, down_b, up_w, up_b, ln_g, ln_b, tau_ctx, wg, bg, wn1, bn1, wsoma, bsoma,
                  wtemp, btemp, wout, gamma, beta, out):
    ctx = ExitStack()
    with ctx:
        def sb(name, shape, dt=F32, stack=ctx):
            return stack.enter_context(nc.sbuf_tensor(name, shape, dt))

        def sem(name):
            return ctx.enter_context(nc.semaphore(name))

        x2_dram = nc.dram_tensor("x2_scratch", (B * T, E), F32, kind="Internal").ap()

        ident = sb("ident", [P, P])
        consts = sb("consts", [P, 4])
        taus = sb("taus", [P, 3])
        alpha = sb("alpha", [P, 3])
        blend_sb = sb("blend_sb", [P, 2, KE])
        blend_w = sb("blend_w", [P, 2, KE])
        blend_t = sb("blend_t", [P, 3, KE])
        bias_g = sb("bias_g", [P, KE])
        bias_soma = sb("bias_soma", [P, KE])
        bias_temp = sb("bias_temp", [P, KE])
        bias_n1 = sb("bias_n1", [P, 1])
        bias_n2 = sb("bias_n2", [P, 2])
        cols_all = sb("cols_all", [P, B, 1 + KE])
        cols = sb("cols", [P, 1 + KE])
        ids = sb("ids", [1, B], I32)
        wn2_rep = sb("wn2_rep", [P, 2, P])
        wn2_col = sb("wn2_col", [P, 2])
        wg_h = sb("wg_h", [P, 2 * KE, E], F32R)
        wg_l = sb("wg_l", [P, 2 * KE, E], F32R)
        wn1_h = sb("wn1_h", [P, KE, A], F32R)
        wn1_l = sb("wn1_l", [P, KE, A], F32R)
        ws_h = sb("ws_h", [P, KE, E], F32R)
        ws_l = sb("ws_l", [P, KE, E], F32R)
        wt_h = sb("wt_h", [P, KE, E], F32R)
        wt_l = sb("wt_l", [P, KE, E], F32R)
        wo_h = sb("wo_h", [P, KE, E], F32R)
        wo_l = sb("wo_l", [P, KE, E], F32R)

        res = sb("res", [P, GT, E])
        dw_f = sb("dw_f", [P, KE, A])
        uw_f = sb("uw_f", [P, E])
        xa = sb("xa", [P, GT, E])

        bank = [ctx.enter_context(nc.psum_tensor(f"bank{i}", [P, 512], F32)) for i in range(8)]

        params_in = sem("params_in")

        x2_in = sem("x2_in")
        lw_in = sem("lw_in")

        def load_group(sp, q):
            src = x2_dram.rearrange("(u c p) e -> p u c e", p=P, c=GT)
            sp.dma_start(xa[:], src[:, bass.ds(q, 1)].rearrange("p u c e -> p (u c) e")).then_inc(x2_in, 16)

        def load_adapter(sp, q):
            pid = sp.value_load(ids[0:1, bass.ds(q // NG, 1)], min_val=0, max_val=7)
            one = bass.ds(pid, 1)
            sp.dma_start(dw_f[:], down_w[one].rearrange("o (k p) a -> p (o k) a", p=P)).then_inc(lw_in, 16)
            sp.dma_start(uw_f[:], up_w[one].rearrange("o a e -> (o a) e")).then_inc(lw_in, 16)

        NEG_HALF, HALF, EPSILON, ONE = (consts[:, i:i + 1] for i in range(4))

        def f32(t):
            return t.bitcast(F32)

        s1 = ExitStack()
        with s1:
            def sb1(name, shape, dt=F32):
                return sb(name, shape, dt, s1)

            xb = sb1("xb", [P, NT, E])
            xt = sb1("xt", [P, 2, KE, GN])
            w1_sb = sb1("w1_sb", [P, KE, A])
            b1_sb = sb1("b1_sb", [P, 1])
            v_sb = sb1("v_sb", [P, 1])
            v_rep = sb1("v_rep", [P, P])
            ones = sb1("ones", [P, P])
            prob = res[:].rearrange("p g (u q) -> p (g u) q", q=P)
            hid = sb1("hid", [P, 2, GN])
            s_row = sb1("s_row", [P, NT, P])
            bmax = sb1("bmax", [P, NT])
            imax = sb1("imax", [P, NT])
            omax = sb1("omax", [P, NT])
            rmax = sb1("rmax", [P, NT])
            wlog = sb1("wlog", [P, NT])
            wcol = sb1("wcol", [P, NT])
            blog = sb1("blog", [P, NT, NT])
            bexp = sb1("bexp", [P, NT, 32])
            bexp_h = sb1("bexp_h", [P, NT, 32], F32R)
            bexp_l = sb1("bexp_l", [P, NT, 32])
            bw_hl = sb1("bw_hl", [3 * 32, NT, P], F32R)
            g_hl = sb1("g_hl", [3 * 32, E], F32R)
            zin = sb1("zin", [P, NT])
            zout = sb1("zout", [P, NT])
            zblk = sb1("zblk", [P, NT])
            rnorm = sb1("rnorm", [P, NT])
            upb = sb1("upb", [P, GT, E])
            dnb = sb1("dnb", [P, GT, E])
            xt_slot = [xt[:, 1], xt[:, 0], dnb[:], xt[:, 1]]
            probT = hid[:].rearrange("p i (g q) -> p i g q", g=GT)
            bwz = blog
            shift_m, last_m = wn2_rep[:, 0], wn2_rep[:, 1]
            next_m, mirror_m = uw_f[:, 2 * P:3 * P], uw_f[:, 3 * P:4 * P]
            SUM = {2: (0, 1, 6, 7), 3: (2, 3, 4, 5)}
            tmask = uw_f[:, 0:B * P].rearrange("p (b l) -> p b l", b=B)
            bmask = dw_f[:].rearrange("p k a -> p (k a)").rearrange("p (b c d) -> p b c d", b=B, c=NT)
            qbuf = [xa[:], prob.rearrange("p (g c) l -> p g (c l)", g=GT)]
            before = [xt[:, 0], upb[:]]
            after = [xt[:, 1], dnb[:]]
            dbuf = [s_row[:].rearrange("p (g c) l -> p g (c l)", g=GT)] * NG
            dbuf[1] = after[0]
            dbuf[2] = after[1]
            wsel = upb[:].rearrange("p g (u q) -> p (g u) q", q=P)
            wsel_flat = upb[:].rearrange("p g e -> p (g e)")
            bu_cols = sb1("bu_cols", [P, B, KE])
            flat_prob = prob.rearrange("p c l -> p (c l)")
            hidden_m = flat_prob[:, 0:3 * P].rearrange("p (m l) -> p m l", m=3)
            hidden_b = flat_prob[:, 3 * P:9 * P].rearrange("p (m c d) -> p m c d", m=3, c=NT)
            counts = flat_prob[:, 9 * P:9 * P + 3 * NT].rearrange("p (m c) -> p m c", m=3)
            typ_i = sb1("typ_i", [P, B], I32)
            typ = sb1("typ", [P, B])
            sel = sb1("sel", [P, 3, B])
            coef_b = sb1("coef_b", [P, 5])
            coef = sb1("coef", [P, 5, B])
            cnt = sb1("cnt", [P, B, NT])

            ids_in = sem("ids_in")
            coef_in = sem("coef_in")
            rows_in = sem("rows_in")
            x_in = [sem(f"x_in{j}") for j in range(NG)]
            xt_in = [sem(f"xt_in{j}") for j in range(NG)]
            w_in = [sem(f"w_in{i}") for i in range(6)]
            w_split = sem("w_split")
            w_hi = sem("w_hi")
            pool_const = sem("pool_const")
            setup_v = sem("setup_v")
            setup_a = sem("setup_a")
            hid_mm = sem("hid_mm")
            hid_act = sem("hid_act")
            score_mm = sem("score_mm")
            score_cp = sem("score_cp")
            stat = sem("stat")
            wcol_act = sem("wcol_act")
            bexp_act = sem("bexp_act")
            prob_act = sem("prob_act")
            wsel_zero = sem("wsel_zero")
            wsel_act = sem("wsel_act")
            zsum_mm = sem("zsum_mm")
            w1_in = sem("w1_in")
            v_set = sem("v_set")
            mixed = sem("mixed")
            bwT_mm = sem("bwT_mm")
            bexp_split = sem("bexp_split")
            bw_hi = sem("bw_hi")
            bw_lo = sem("bw_lo")
            g4_mm = sem("g4_mm")
            g_hi = sem("g_hi")
            g_lo = sem("g_lo")
            probT_mm = sem("probT_mm")
            probT_cp = sem("probT_cp")
            pool_mm = sem("pool_mm")
            x1_done = sem("x1_done")
            nbr_in = [sem(f"nbr_in{i}") for i in range(2)]
            nbr_sum = sem("nbr_sum")
            d_act = sem("d_act")
            d_mul = sem("d_mul")
            q_chain = sem("q_chain")
            q_last = sem("q_last")
            tsum_mm = sem("tsum_mm")
            tmixed = {j: sem(f"tmixed{j}") for j in (2, 3)}
            x2_done = sem("x2_done")
            x2_out = [sem(f"x2_out{i}") for i in range(2)]

            col = lambda a: a.rearrange("(k p) -> p k", p=P)
            row = lambda a, n: a.rearrange("(o n) -> o n", o=1).broadcast_to([n, a.shape[0]])
            n_params = [0]

            with nc.Block() as block:

                x2_v = x2_dram.rearrange("(u c p) e -> p u c e", p=P, c=GT)

                def store_x2(sp, b, j):
                    sp.wait_ge(x2_done, START + NG * b + j + 1)
                    sp.dma_start(x2_v[:, bass.ds(NG * b + j, 1)].rearrange("p u c e -> p (u c) e"),
                                 qbuf[j % 2]).then_inc(x2_out[j % 2], 16)

                def stencil_coef(act, b, j):
                    act.wait_ge(x1_done, START + NT * b + GT * (j + 1))
                    if j in (1, 2):
                        act.wait_ge(nbr_sum, DS * b + j)
                    else:
                        act.wait_ge(mixed, START + DS * b + min(j, 1))
                    act.activation(dbuf[j], xb[:, GT * j:GT * j + GT], ACT.Identity,
                                   bias=coef_b[:, 4:5], scale=coef_b[:, 3:4])\
                       .then_inc(d_act, 1)

                @block.sync
                def _(sp):
                    for i in range(2):
                        sp.sem_inc(x2_out[i], START)

                    def load_xt(b, j):
                        xT_b = xT[bass.ds(b, 1)].rearrange("o (k p) t -> p (o k) t", p=P)
                        sp.dma_start(xt_slot[j], xT_b[:, :, GN * j:GN * j + GN]).then_inc(xt_in[j], 16)

                    def load_x(b, j):
                        x_b = x[bass.ds(b, 1)].rearrange("o (c p) e -> p (o c) e", p=P)
                        sp.dma_start(xb[:, GT * j:GT * j + GT], x_b[:, GT * j:GT * j + GT])\
                          .then_inc(x_in[j], 16)

                    with nc.allow_non_contiguous_dma(reason="small parameters"):
                        sp.dma_start(w1_sb[:], w1.rearrange("(k p) a -> p k a", p=P)).then_inc(w1_in, 16)
                        load_xt(0, 0)
                        sp.dma_start(b1_sb[:], col(b1)).then_inc(w1_in, 16)
                        sp.dma_start(v_sb[:], col(v)).then_inc(w1_in, 16)
                        for dst, src in ((typ_i[:], ptype), (coef[:, 0], zx), (coef[:, 1], zy),
                                         (coef[:, 2], zr)):
                            sp.dma_start(dst, row(src, P)).then_inc(coef_in, 16)
                        sp.dma_start(ids[:], profile.rearrange("(o n) -> o n", o=1)).then_inc(ids_in, 16)
                        load_xt(0, 1)
                        load_xt(0, 2)
                        sp.wait_ge(ids_in, 16)
                        for b in range(B):
                            pid = sp.value_load(ids[0:1, b:b + 1], min_val=0, max_val=7)
                            one = bass.ds(pid, 1)
                            for dst, src in (
                                (cols_all[:, b, 0:1], down_b[one, :].rearrange("o p -> p o")),
                                (cols_all[:, b, 1:], ln_b[one, :].rearrange("o (k p) -> p (o k)", p=P)),
                                (bu_cols[:, b], up_b[one, :].rearrange("o (k p) -> p (o k)", p=P)),
                            ):
                                sp.dma_start(dst, src).then_inc(rows_in, 16)

                    def before_x1(b, j):
                        c0 = GT * j
                        up = before[j % 2]
                        sp.wait_ge(x1_done, START + NT * b + c0 + GT)
                        sp.dma_start(up[1:P], xb[0:P - 1, c0:c0 + GT]).then_inc(nbr_in[j % 2], 16)
                        if j == 0:
                            sp.dma_start(up[0:1, 1:GT], xb[P - 1:P, c0:c0 + GT - 1]).then_inc(nbr_in[j % 2], 16)
                            sp.dma_start(up[0:1, 0:1], xb[1:2, 0:1]).then_inc(nbr_in[j % 2], 16)
                        else:
                            sp.dma_start(up[0:1], xb[P - 1:P, c0 - 1:c0 + GT - 1]).then_inc(nbr_in[j % 2], 16)

                    def after_x1(b, j):
                        c0 = GT * j
                        dn = after[j % 2]
                        if j == 1:
                            sp.wait_ge(w_split, 12)
                        sp.wait_ge(x1_done, START + NT * b + min(NT, c0 + GT + 1))
                        sp.dma_start(dn[0:P - 1], xb[1:P, c0:c0 + GT]).then_inc(nbr_in[j % 2], 16)
                        sp.dma_start(dn[P - 1:P], xb[0:1, c0 + 1:c0 + GT + 1]).then_inc(nbr_in[j % 2], 16)

                    def batch(b, more):
                        sp.wait_ge(hid_mm, NG * b + 1)
                        load_xt(b, 3)
                        sp.wait_ge(x2_done, START + NG * b)
                        for j in range(NG):
                            if j != 1:
                                sp.wait_ge(w_split, 2 * max(j, 1))
                            load_x(b, j)
                        before_x1(b, 0)
                        after_x1(b, 0)
                        before_x1(b, 1)
                        after_x1(b, 1)
                        store_x2(sp, b, 0)
                        if more:
                            load_xt(b + 1, 1)
                            sp.wait_ge(mixed, START + DS * (b + 1))
                            load_xt(b + 1, 0)
                        store_x2(sp, b, 1)
                        store_x2(sp, b, 2)
                        if not more:
                            sp.wait_ge(tsum_mm, (NT - GT * DS) * B)
                            load_adapter(sp, 0)
                        if more:
                            load_xt(b + 1, 2)
                        if not more:
                            sp.wait_ge(x2_out[0], START + 16 * NG // 2 * B)
                            load_group(sp, 0)
                        store_x2(sp, b, 3)

                    with sp.Fori(0, B - 1) as b:
                        batch(b, True)
                    batch(B - 1, False)
                    sp.wait_ge(x2_out[0], START + 16 * B * NG // 2)

                chunks = lambda w: w.rearrange("(k p) n -> p k n", p=P)
                pieces = [
                    (xb[:, 0:GT], chunks(wg[0:E]), wg_h[:, 0:KE], wg_l[:, 0:KE]),
                    (xb[:, 2 * GT:3 * GT], chunks(wg[E:2 * E]), wg_h[:, KE:], wg_l[:, KE:]),
                    (xb[:, 3 * GT:], chunks(wsoma), ws_h[:], ws_l[:]),
                    (dnb[:], chunks(wtemp), wt_h[:], wt_l[:]),
                    (dnb[:], chunks(wout), wo_h[:], wo_l[:]),
                    (dnb[:, :, 0:A], chunks(wn1), wn1_h[:], wn1_l[:]),
                ]

                @block.gpsimd
                def _(po):
                    n = [0]

                    def step(ins):
                        n[0] += 1
                        ins.then_inc(pool_const, 1)

                    step(po.memset(ident[:], 0.0))
                    step(po.memset(hidden_m, 0.0))
                    step(po.memset(hidden_b, 0.0))
                    po.wait_ge(pool_const, 3)
                    diag = dict(compare_op=ALU.not_equal, fill=1.0)
                    step(po.affine_select(out=ident[:], in_=ident[:], base=0, pattern=[[-1, P]],
                                          channel_multiplier=1, **diag))
                    step(po.affine_select(out=hidden_m[:, 0], in_=hidden_m[:, 0], compare_op=ALU.is_ge,
                                          fill=1.0, base=0, pattern=[[-1, P]], channel_multiplier=1))
                    step(po.affine_select(out=hidden_m[:, 1], in_=hidden_m[:, 1], compare_op=ALU.is_ge,
                                          fill=1.0, base=0, pattern=[[1, P]], channel_multiplier=-1))
                    step(po.affine_select(out=hidden_m[:, 2], in_=hidden_m[:, 2], base=0,
                                          pattern=[[-1, P]], channel_multiplier=1, **diag))
                    step(po.affine_select(out=hidden_b[:, 0], in_=hidden_b[:, 0], compare_op=ALU.is_gt,
                                          fill=1.0, base=0, pattern=[[1, NT], [-1, NT]], channel_multiplier=0))
                    step(po.affine_select(out=hidden_b[:, 1], in_=hidden_b[:, 1], compare_op=ALU.is_gt,
                                          fill=1.0, base=0, pattern=[[-1, NT], [1, NT]], channel_multiplier=0))
                    step(po.affine_select(out=hidden_b[:, 2], in_=hidden_b[:, 2], base=0,
                                          pattern=[[1, NT], [-1, NT]], channel_multiplier=0, **diag))
                    step(po.iota(counts[:, 0], pattern=[[P, NT]], base=1, channel_multiplier=1,
                                 allow_small_or_imprecise_dtypes=True))
                    step(po.iota(counts[:, 1], pattern=[[-P, NT]], base=T, channel_multiplier=-1,
                                 allow_small_or_imprecise_dtypes=True))
                    step(po.memset(counts[:, 2], float(T - 1)))
                    for i, value in enumerate((-0.5, 0.5, EPS, 1.0)):
                        step(po.memset(consts[:, i:i + 1], value))
                    step(po.memset(wn2_rep[:], 0.0))
                    step(po.memset(uw_f[:, 2 * P:4 * P], 0.0))
                    po.wait_ge(pool_const, n[0])
                    for dst, base, per_row, per_col in (
                        (shift_m, -1, 1, -1),
                        (last_m, P - 1, -1, P),
                        (next_m, P * (P - 1), 1, -P),
                        (mirror_m, -(P - 2) - P * (P - 1), 1, P),
                        (shift_m, 1, 1, -1),
                    ):
                        po.wait_ge(pool_const, n[0])
                        step(po.affine_select(out=dst, in_=dst, base=base, pattern=[[per_col, P]],
                                              channel_multiplier=per_row, **diag))
                    assert n[0] == POOL_CONST, n[0]
                    po.wait_ge(pool_const, POOL_CONST)

                    def load_piece(i):
                        po.dma_start(pieces[i][0], pieces[i][1]).then_inc(w_in[i], 16)

                    load_piece(0)
                    load_piece(1)
                    for i, (st, src, hi, lo) in enumerate(pieces):
                        if i > 3:
                            po.wait_ge(w_split, 2 * i)
                            load_piece(i)
                        po.wait_ge(w_in[i], 16)
                        if i == 0:
                            load_piece(2)
                        if i < BY_ACT:
                            po.wait_ge(w_hi, i + 1)
                            if i:
                                po.wait_ge(w_split, 2 * i)
                            po.sem_inc(w_split, 1)
                        else:
                            po.tensor_tensor(hi, st, ONE.rearrange("p (o n) -> p o n", o=1)
                                             .broadcast_to(list(st.shape)), ALU.mult).then_inc(w_split, 1)
                            po.wait_ge(w_split, 2 * i + 1)
                        po.tensor_tensor(lo, st, f32(hi), ALU.subtract).then_inc(w_split, 1)
                        if i == 1:
                            po.wait_ge(hid_mm, 3)
                            load_piece(3)
                    with po.Fori(0, B) as b:
                        def local(j):
                            po.wait_ge(d_act, NG * b + j + 1)
                            po.tensor_tensor(dbuf[j], dbuf[j], xb[:, GT * j:GT * j + GT], ALU.mult)\
                              .then_inc(d_mul, 1)

                        def time_sum(j):
                            po.wait_ge(nbr_in[j], 16 * NBR[j] * (b + 1))
                            po.tensor_tensor(before[j % 2], before[j % 2], after[j % 2], ALU.add)\
                              .then_inc(nbr_sum, 1)

                        local(0)
                        time_sum(0)
                        time_sum(1)
                        for j in range(1, NG):
                            local(j)
                        q, xg = qbuf[(NG - 1) % 2], xb[:, NT - GT:]
                        po.wait_ge(x2_out[1], START + 16 * (NG // 2 * b + 1))
                        for dst, one, other in ((slice(1, E - 1), slice(0, E - 2), slice(2, E)),
                                                (slice(0, 1), slice(1, 2), slice(1, 2)),
                                                (slice(E - 1, E), slice(E - 2, E - 1), slice(E - 2, E - 1))):
                            po.tensor_tensor(q[:, :, dst], xg[:, :, one], xg[:, :, other], ALU.add)\
                              .then_inc(q_last, 1)

                @block.scalar
                def _(act):
                    def load(dst, src):
                        act.dma_start(dst, src).then_inc(params_in, 16)
                        n_params[0] += 16

                    with nc.allow_non_contiguous_dma(reason="small parameters"):
                        load(taus[:, 0:1], row(tau_ctx, P))
                        load(taus[:, 1:3], row(tau_raws, P))
                        load(wn2_col[:], wn2.rearrange("d p -> p d"))
                        load(bias_n2[:], row(bn2, P))
                        for d in range(2):
                            load(blend_sb[:, d], col(blend[d]))
                        load(bias_g[:], col(bg))
                        load(bias_soma[:], col(bsoma))
                        load(bias_temp[:], col(btemp))
                        load(bias_n1[:], col(bn1))
                    assert n_params[0] == N_PARAMS
                    for i in range(BY_ACT):
                        act.wait_ge(w_in[i], 16)
                        act.activation(pieces[i][2], pieces[i][0], ACT.Copy).then_inc(w_hi, 1)
                    act.wait_ge(w1_in, 48)
                    with act.Fori(0, B) as b:
                        for j in range(NG):
                            act.wait_ge(hid_mm, NG * b + j + 1)
                            if j >= 2:
                                act.wait_ge(score_mm, NG * b + j - 1)
                            act.activation(hid[:, j % 2], bank[j % 2][:], ACT.Tanh, bias=b1_sb[:])\
                               .then_inc(hid_act, 1)
                        act.wait_ge(stat, STAT * b + S_WLOG)
                        act.activation(wcol[:], wlog[:], ACT.Exp).then_inc(wcol_act, 1)
                        act.wait_ge(wsel_zero, b + 1)
                        for r in range(P // 32):
                            at = 32 * r
                            act.activation(wsel_flat[:, at:at + (NT - 1) * (P + 1) + 1:P + 1], wlog[:],
                                           ACT.Exp).then_inc(wsel_act, 1)
                        act.wait_ge(stat, STAT * b + S_BLOG)
                        act.activation(bexp[:, :, 0:NT], blog[:], ACT.Exp).then_inc(bexp_act, 1)
                        for j in range(NG):
                            act.wait_ge(stat, STAT * b + S_PROB + j)
                            p = prob[:, GT * j:GT * j + GT]
                            act.activation(p, p, ACT.Exp).then_inc(prob_act, 1)
                        act.wait_ge(bwT_mm, 2 * b + 1)
                        for at in (32, 64):
                            for i in range(GT):
                                act.activation(bw_hl[at:at + 32].rearrange("d (u i) q -> d i u q", i=GT)[:, i],
                                               bank[4][32 * i:32 * i + 32].rearrange("d (u q) -> d u q", q=P),
                                               ACT.Copy).then_inc(bw_hi, 1)
                        act.wait_ge(g4_mm, b + 1)
                        act.activation(g_hl[:], bank[5][0:3 * 32], ACT.Copy).then_inc(g_hi, 1)
                        for j in range(NG):
                            act.wait_ge(probT_mm, NG * b + j + 1)
                            if j >= 2:
                                act.wait_ge(pool_mm, NT * b + GT * (j - 1))
                            act.activation(probT[:, j % 2].rearrange("p g q -> p (g q)"), bank[j % 2][:],
                                           ACT.Copy).then_inc(probT_cp, 1)
                            if j == 1:
                                stencil_coef(act, b, 0)
                        for j in range(1, NG):
                            stencil_coef(act, b, j)
                    act.wait_ge(params_in, N_PARAMS)
                    act.activation(alpha[:], taus[:], ACT.Exp).then_inc(setup_a, 1)
                    act.wait_ge(setup_v, BLEND_SHIFTED)
                    act.activation(blend_w[:], blend_t[:, 0:2], ACT.Exp).then_inc(setup_a, 1)

                @block.tensor
                def _(pe):
                    pe.wait_ge(w1_in, 48)
                    pe.wait_ge(v_set, 1)
                    with pe.Fori(0, B) as b:
                        def hidden(j):
                            pe.wait_ge(xt_in[j], 16 * (b + 1))
                            if j >= 2:
                                pe.wait_ge(hid_act, NG * b + j - 1)
                            for k in range(KE):
                                last = pe.matmul(bank[j % 2][:], w1_sb[:, k], xt_slot[j][:, k],
                                                 start=(k == 0), stop=(k == KE - 1))
                            last.then_inc(hid_mm, 1)

                        def scores(j):
                            pe.wait_ge(hid_act, NG * b + j + 1)
                            if j >= 2:
                                pe.wait_ge(score_cp, NG * b + j - 1)
                            pe.matmul(bank[2 + j % 2][:], v_rep[:], hid[:, j % 2], start=True, stop=True)
                            for i in range(GT):
                                c = GT * j + i
                                last = pe.matmul(bank[6][:, c:c + 1], hid[:, j % 2, P * i:P * i + P],
                                                 v_sb[:], start=True, stop=True)
                            last.then_inc(score_mm, 1)

                        pe.wait_ge(tmixed[2], START + GT * b)
                        hidden(0)
                        for j in range(1, NG):
                            hidden(j)
                            if j == 1:
                                pe.wait_ge(tmixed[3], START + GT * b)
                            scores(j - 1)
                        scores(NG - 1)
                        pe.wait_ge(setup_v, SETUP_V)
                        pe.wait_ge(pool_const, POOL_CONST)
                        pe.wait_ge(wcol_act, b + 1)
                        pe.matmul(bank[7][:, 0:NT], ones[:], wcol[:], start=True, stop=True)\
                          .then_inc(zsum_mm, 1)
                        pe.wait_ge(wsel_act, GT * (b + 1))
                        for c in range(NT):
                            if c % GT == 0:
                                pe.wait_ge(x_in[c // GT], 16 * (b + 1))
                            if c == NT // 4:
                                pe.wait_ge(bexp_split, 2 * (b + 1))
                                for half, acc in ((f32(bexp_h), bank[4]), (bexp_l, bank[3])):
                                    for u in range(GT):
                                        last = pe.transpose(
                                            acc[:, P * u:P * u + P],
                                            half[:, GT * u:GT * u + GT].rearrange("p c d -> p (c d)"), ident[:])
                                    last.then_inc(bwT_mm, 1)
                            last = pe.matmul(bank[5][:], wsel[:, c], xb[:, c], start=(c == 0),
                                             stop=(c == NT - 1))
                        last.then_inc(g4_mm, 1)

                        def transposed(j):
                            pe.wait_ge(prob_act, NG * b + j + 1)
                            if j >= 2:
                                pe.wait_ge(probT_cp, NG * b + j - 1)
                            for i in range(GT):
                                last = pe.transpose(bank[j % 2][:, P * i:P * i + P], prob[:, GT * j + i],
                                                    ident[:])
                            last.then_inc(probT_mm, 1)

                        def pooled(j):
                            pe.wait_ge(probT_cp, NG * b + j + 1)
                            for i in range(GT):
                                c = GT * j + i
                                if c >= 4:
                                    pe.wait_ge(x1_done, START + NT * b + c - 3)
                                acc = bank[2 + c % 4][:]
                                pe.matmul(acc, probT[:, j % 2, i], xb[:, c], start=True, stop=False)
                                pe.matmul(acc, bw_hl[:, c], g_hl[:], start=False, stop=True)\
                                  .then_inc(pool_mm, 1)

                        transposed(0)
                        transposed(1)
                        pe.wait_ge(bw_hi, 2 * GT * (b + 1))
                        pe.wait_ge(bw_lo, GT * (b + 1))
                        pe.wait_ge(g_lo, b + 1)
                        for j in range(NG):
                            pooled(j)
                            if j + 2 < NG:
                                transposed(j + 2)
                        for j in range(DS, NG):
                            for i in range(GT):
                                c = GT * j + i
                                pe.wait_ge(x1_done, START + NT * b + min(NT, c + 2))
                                acc = bank[SUM[j][i]][:]
                                pe.matmul(acc, shift_m, xb[:, c], start=True, stop=False)
                                pe.matmul(acc, last_m, xb[:, c - 1], start=False, stop=False)
                                if c < NT - 1:
                                    last = pe.matmul(acc, next_m, xb[:, c + 1], start=False, stop=True)
                                else:
                                    last = pe.matmul(acc, mirror_m, xb[:, c], start=False, stop=True)
                                last.then_inc(tsum_mm, 1)

                @block.vector
                def _(ve):
                    ve.sem_inc(x1_done, START)
                    ve.sem_inc(x2_done, START)
                    ve.sem_inc(mixed, START)
                    ve.sem_inc(tmixed[2], START)
                    ve.sem_inc(tmixed[3], START)
                    n = [0]

                    def step(ins):
                        n[0] += 1
                        ins.then_inc(setup_v, 1)

                    def settle():
                        ve.wait_ge(setup_v, n[0])

                    step(ve.memset(bexp[:], 0.0))
                    step(ve.memset(ones[:], 1.0))
                    ve.wait_ge(w1_in, 48)
                    ve.tensor_copy(v_rep[:], v_sb[:].broadcast_to([P, P])).then_inc(v_set, 1)
                    ve.wait_ge(coef_in, N_COEF)
                    step(ve.tensor_copy(typ[:], typ_i[:]))
                    step(ve.tensor_scalar(coef[:, 3], coef[:, 2], -1.0, None, ALU.mult))
                    step(ve.tensor_tensor(coef[:, 4], coef[:, 0], coef[:, 1], ALU.add))
                    settle()
                    step(ve.tensor_scalar(coef[:, 4], coef[:, 4], -2.0, 1.0, ALU.mult, ALU.add))
                    settle()
                    step(ve.tensor_tensor(coef[:, 4], coef[:, 4], coef[:, 2], ALU.add))
                    step(ve.tensor_scalar(sel[:, 0], typ[:], 0.0, None, ALU.is_equal))
                    step(ve.tensor_scalar(sel[:, 1], typ[:], 1.0, None, ALU.is_equal))
                    settle()
                    step(ve.tensor_tensor(sel[:, 2], sel[:, 0], sel[:, 1], ALU.add))
                    settle()
                    step(ve.tensor_scalar(sel[:, 2], sel[:, 2], -1.0, 1.0, ALU.mult, ALU.add))
                    settle()
                    ve.wait_ge(pool_const, POOL_CONST)
                    for b in range(B):
                        for dst, src in ((tmask[:, b], lambda m: hidden_m[:, m]),
                                         (bmask[:, b], lambda m: hidden_b[:, m]),
                                         (cnt[:, b], lambda m: counts[:, m])):
                            step(ve.tensor_scalar(dst, src(0), sel[:, 0, b:b + 1], None, ALU.mult))
                            settle()
                            step(ve.scalar_tensor_tensor(dst, src(1), sel[:, 1, b:b + 1], dst,
                                                         ALU.mult, ALU.add))
                            settle()
                            step(ve.scalar_tensor_tensor(dst, src(2), sel[:, 2, b:b + 1], dst,
                                                         ALU.mult, ALU.add))
                            settle()
                    step(ve.tensor_scalar(tmask, tmask, NEG, None, ALU.mult))
                    step(ve.tensor_scalar(bmask, bmask, NEG, None, ALU.mult))
                    settle()
                    assert n[0] == SETUP_V, n[0]

                    with ve.Fori(0, B) as b:
                        m = [0]

                        def link(ins, wait=True):
                            m[0] += 1
                            ins.then_inc(stat, 1)
                            if wait:
                                ve.wait_ge(stat, STAT * b + m[0])

                        one = bass.ds(b, 1)
                        ve.wait_ge(x2_done, START + NG * b)
                        link(ve.tensor_scalar(coef_b[:], coef[:, :, one].rearrange("p m o -> p (m o)"), 1.0,
                                              None, ALU.mult), False)
                        ve.memset(wsel_flat, 0.0).then_inc(wsel_zero, 1)
                        ve.wait_ge(x2_out[1], START + 16 * NG // 2 * b)
                        for j in range(NG):
                            g = slice(GT * j, GT * j + GT)
                            ve.wait_ge(score_mm, NG * b + j + 1)
                            ve.tensor_copy(s_row[:, g].rearrange("p c l -> p (c l)"),
                                           bank[2 + j % 2][:]).then_inc(score_cp, 1)
                            ve.wait_ge(score_cp, NG * b + j + 1)
                            link(ve.tensor_reduce(bmax[:, g], s_row[:, g], AX.X, ALU.max), j == NG - 1)
                            if j == NG - 1:
                                link(ve.tensor_tensor(wlog[:], bank[6][:, 0:NT], bmax[:], ALU.subtract), False)
                                assert m[0] == S_WLOG
                            link(ve.tensor_tensor(prob[:, g], s_row[:, g],
                                                  tmask[:, one].broadcast_to([P, GT, P]), ALU.add))
                            link(ve.tensor_reduce(imax[:, g], prob[:, g], AX.X, ALU.max), False)
                        ve.wait_ge(stat, STAT * b + m[0])
                        link(ve.tensor_tensor(
                            blog[:], bmask[:, one].rearrange("p o c d -> p (o c) d"),
                            bmax[:].rearrange("p (o c) -> p o c", o=1).broadcast_to([P, NT, NT]), ALU.add))
                        link(ve.tensor_reduce(omax[:], blog[:], AX.X, ALU.max))
                        link(ve.tensor_tensor(rmax[:], imax[:], omax[:], ALU.max))
                        link(ve.tensor_tensor(
                            blog[:], blog[:],
                            rmax[:].rearrange("p (c o) -> p c o", o=1).broadcast_to([P, NT, NT]),
                            ALU.subtract), False)
                        assert m[0] == S_BLOG
                        for j in range(NG):
                            g = slice(GT * j, GT * j + GT)
                            link(ve.tensor_tensor(
                                prob[:, g], prob[:, g],
                                rmax[:, g].rearrange("p (c o) -> p c o", o=1).broadcast_to([P, GT, P]),
                                ALU.subtract), False)
                            assert m[0] == S_PROB + j
                        ve.wait_ge(bexp_act, b + 1)
                        ve.tensor_copy(bexp_h[:], bexp[:]).then_inc(bexp_split, 1)
                        ve.wait_ge(bexp_split, 2 * b + 1)
                        ve.tensor_tensor(bexp_l[:], bexp[:], f32(bexp_h[:]), ALU.subtract)\
                          .then_inc(bexp_split, 1)
                        ve.wait_ge(zsum_mm, b + 1)
                        link(ve.tensor_copy(zblk[:], bank[7][:, 0:NT]), False)
                        ve.wait_ge(bexp_act, b + 1)
                        ve.wait_ge(stat, STAT * b + m[0])
                        link(ve.tensor_tensor(
                            bwz[:], bexp[:, :, 0:NT],
                            zblk[:].rearrange("p (o c) -> p o c", o=1).broadcast_to([P, NT, NT]), ALU.mult))
                        link(ve.tensor_reduce(zout[:], bwz[:], AX.X, ALU.add), False)
                        ve.wait_ge(prob_act, NG * (b + 1))
                        link(ve.tensor_reduce(zin[:], prob, AX.X, ALU.add))
                        link(ve.tensor_tensor(zin[:], zin[:], zout[:], ALU.add))
                        assert m[0] == STAT, m[0]
                        ve.tensor_tensor(rnorm[:], zin[:], cnt[:, one].rearrange("p o c -> p (o c)"),
                                         ALU.mult).then_inc(q_chain, 1)
                        ve.wait_ge(q_chain, Q_CHAIN * b + 1)
                        ve.reciprocal(rnorm[:], rnorm[:]).then_inc(q_chain, 1)
                        ve.wait_ge(q_chain, Q_CHAIN * b + 2)
                        for i in range(GT):
                            if i == 0:
                                ve.wait_ge(bwT_mm, 2 * (b + 1))
                            ve.tensor_copy(bw_hl[0:32].rearrange("d (u i) q -> d i u q", i=GT)[:, i],
                                           bank[3][32 * i:32 * i + 32].rearrange("d (u q) -> d u q", q=P))\
                              .then_inc(bw_lo, 1)
                        ve.wait_ge(g_hi, b + 1)
                        ve.tensor_tensor(g_hl[32:64], bank[5][32:64], f32(g_hl[32:64]), ALU.subtract)\
                          .then_inc(g_lo, 1)

                        flat = lambda a: a.rearrange("p c e -> p (c e)")

                        def channel_part(j):
                            q, xg = qbuf[j % 2], xb[:, GT * j:GT * j + GT]
                            if j == 1:
                                ve.wait_ge(probT_mm, NG * (b + 1))
                            else:
                                ve.wait_ge(x2_out[0], START + 16 * (NG // 2 * b + j // 2))
                            ve.wait_ge(x1_done, START + NT * b + GT * (j + 1))
                            ve.tensor_tensor(q[:, :, 1:E - 1], xg[:, :, 0:E - 2], xg[:, :, 2:E],
                                             ALU.add).then_inc(q_chain, 1)
                            ve.tensor_scalar(q[:, :, 0:1], xg[:, :, 1:2], 2.0, None, ALU.mult)\
                              .then_inc(q_chain, 1)
                            ve.tensor_scalar(q[:, :, E - 1:E], xg[:, :, E - 2:E - 1], 2.0, None,
                                             ALU.mult).then_inc(q_chain, 1)

                        def time_part(j):
                            d = dbuf[j]
                            ve.wait_ge(d_mul, NG * b + j + 1)
                            if j < DS:
                                ve.wait_ge(nbr_sum, DS * b + j + 1)
                                ve.scalar_tensor_tensor(flat(before[j]), flat(before[j]), coef_b[:, 1:2],
                                                        flat(d), ALU.mult, ALU.add).then_inc(mixed, 1)
                                return
                            for i in range(GT):
                                ve.wait_ge(tsum_mm, (NT - GT * DS) * b + GT * (j - DS) + i + 1)
                                ve.scalar_tensor_tensor(d[:, i], bank[SUM[j][i]][:], coef_b[:, 1:2],
                                                        d[:, i], ALU.mult, ALU.add).then_inc(tmixed[j], 1)

                        def stencil(j):
                            q = qbuf[j % 2]
                            if j < NG - 1:
                                ve.wait_ge(q_chain, Q_CHAIN * b + 2 + 3 * (j + 1))
                            else:
                                ve.wait_ge(q_last, 3 * (b + 1))
                            if j < DS:
                                ve.wait_ge(mixed, START + DS * b + j + 1)
                            else:
                                ve.wait_ge(tmixed[j], START + GT * (b + 1))
                            ve.scalar_tensor_tensor(flat(q), flat(q), coef_b[:, 0:1],
                                                    flat(before[j] if j < DS else dbuf[j]),
                                                    ALU.mult, ALU.add).then_inc(x2_done, 1)

                        for c in range(NT):
                            ve.wait_ge(pool_mm, NT * b + c + 1)
                            ve.scalar_tensor_tensor(xb[:, c], bank[2 + c % 4][:], rnorm[:, c:c + 1],
                                                    xb[:, c], ALU.mult, ALU.add).then_inc(x1_done, 1)
                            if c == GT + 1:
                                channel_part(0)
                            if c == 2 * GT + 2:
                                channel_part(1)
                            if c == 3 * GT - 1:
                                time_part(0)
                            if c == 3 * GT + 1:
                                stencil(0)
                        time_part(1)
                        stencil(1)
                        channel_part(2)
                        time_part(2)
                        stencil(2)
                        time_part(3)
                        stencil(3)
                    ve.wait_ge(params_in, N_PARAMS)
                    step(ve.tensor_tensor(blend_t[:, 2], blend_sb[:, 0], blend_sb[:, 1], ALU.max))
                    settle()
                    for d in range(2):
                        step(ve.tensor_tensor(blend_t[:, d], blend_sb[:, d], blend_t[:, 2], ALU.subtract))
                    assert n[0] == BLEND_SHIFTED, n[0]
                    for d in range(2):
                        step(ve.tensor_copy(wn2_rep[:, d], wn2_col[:, d:d + 1].broadcast_to([P, P])))
                    ve.wait_ge(setup_a, 1)
                    step(ve.tensor_scalar(alpha[:], alpha[:], 1.0, None, ALU.add))
                    settle()
                    step(ve.reciprocal(alpha[:], alpha[:]))
                    ve.wait_ge(setup_a, 2)
                    step(ve.tensor_tensor(blend_t[:, 2], blend_w[:, 0], blend_w[:, 1], ALU.add))
                    settle()
                    step(ve.reciprocal(blend_t[:, 2], blend_t[:, 2]))
                    settle()
                    for d in range(2):
                        step(ve.tensor_tensor(blend_w[:, d], blend_w[:, d], blend_t[:, 2], ALU.mult))
                    ve.wait_ge(rows_in, 16 * 3 * B)
                    step(ve.tensor_tensor(cols_all[:, :, 1:], cols_all[:, :, 1:], bu_cols[:], ALU.subtract))
                    settle()
                    settle()

        gamma_row = sb("gamma_row", [P, E])
        ln_g_row = sb("ln_g_row", [P, B, E])
        shift_row = sb("shift_row", [P, B, E])
        bu_row = sb("bu_row", [P, B, E])
        dw_h = sb("dw_h", [P, KE, A], F32R)
        dw_l = sb("dw_l", [P, KE, A], F32R)
        uw_h = sb("uw_h", [P, E], F32R)
        uw_l = sb("uw_l", [P, E], F32R)
        ph = sb("ph", [P, KE, GN], F32R)
        pl = sb("pl", [P, KE, GN], F32R)
        xh = sb("xh", [P, KE, GN], F32R)
        xl = sb("xl", [P, KE, GN], F32R)
        th = sb("th", [P, KE, GN], F32R)
        tl = sb("tl", [P, KE, GN], F32R)
        narrow = sb("narrow", [P, GN])
        zh = sb("zh", [P, GN], F32R)
        zl = sb("zl", [P, GN], F32R)
        wide = sb("wide", [P, 2, GN])
        wgb = sb("wgb", [P, 2, GN])
        tr = sb("tr", [P, 2, 2, GN])
        soma = sb("soma", [P, KE, GN])
        carry = sb("carry", [P, KE, 3])
        keep = sb("keep", [P, GROUPS])
        st_a = sb("st_a", [P, GT, 6])
        mv_a = sb("mv_a", [P, GT, 2])
        rs_a = sb("rs_a", [P, GT])
        st_o = sb("st_o", [P, GT, 6])
        mv_o = sb("mv_o", [P, GT, 2])
        rs_o = sb("rs_o", [P, GT])

        lw_split = sem("lw_split")
        x2T_mm = sem("x2T_mm")
        x2T_hi = sem("x2T_hi")
        x2T_lo = sem("x2T_lo")
        down_mm = sem("down_mm")
        z_act = sem("z_act")
        z_hi = sem("z_hi")
        z_lo = sem("z_lo")
        up_mm = sem("up_mm")
        y_add = sem("y_add")
        ln_mv = sem("ln_mv")
        ln_p = sem("ln_p")
        ln_rs = sem("ln_rs")
        ln_w = sem("ln_w")
        x3_done = sem("x3_done")
        x3T_mm = sem("x3T_mm")
        x3T_hi = sem("x3T_hi")
        x3T_lo = sem("x3T_lo")
        residual = sem("residual")
        n1_mm = sem("n1_mm")
        n1_act = sem("n1_act")
        mod_mm = sem("mod_mm")
        mod_sig = sem("mod_sig")
        mod_add = sem("mod_add")
        pre_mm = sem("pre_mm")
        ctx_mm = sem("ctx_mm")
        ctx_scan = sem("ctx_scan")
        pre_add = sem("pre_add")
        ctx_kept = sem("ctx_kept")
        wg_act = sem("wg_act")
        xsum_done = sem("xsum_done")
        gated = sem("gated")
        tr_in = sem("tr_in")
        tr_scan = sem("tr_scan")
        carried = sem("carried")
        blended = sem("blended")
        t_hi = sem("t_hi")
        t_lo = sem("t_lo")
        soma_mm = sem("soma_mm")
        soma_act = sem("soma_act")
        temp_mm = sem("temp_mm")
        gate_act = sem("gate_act")
        prod = sem("prod")
        prod_hi = sem("prod_hi")
        prod_lo = sem("prod_lo")
        out_mm = sem("out_mm")
        o_mv = sem("o_mv")
        o_p = sem("o_p")
        o_rs = sem("o_rs")
        out_free = sem("out_free")
        o_done = sem("o_done")
        o_out = sem("o_out")
        p2_v = sem("p2_v")
        bias_add = sem("bias_add")
        rows2_in = sem("rows2_in")
        cols_set = sem("cols_set")

        N1, PRE, CTX, MOD = 4, (5, 0, 2, 5), (6, 1, 3, 6), (7, 4)
        X2T, SOMA, DOWN, UP = (4, 7, 0, 1), (2, 3, 5, 2), 6, (4, 7, 0, 1)
        TEMP, OUT, X3T = (3, 5, 6, 2), (0, 1, 3, 2), (4, 5, 6, 7)

        with nc.Block() as block:

            @block.sync
            def _(sp):
                sp.dma_start(gamma_row[:], row(gamma, P)).then_inc(rows2_in, 16)
                sp.dma_start(wgb[:, 0], row(beta, P)).then_inc(rows2_in, 16)
                for b in range(B):
                    pid = sp.value_load(ids[0:1, b:b + 1], min_val=0, max_val=7)
                    one = bass.ds(pid, 1)
                    sp.dma_start(ln_g_row[:, b], ln_g[one, :].broadcast_to([P, E])).then_inc(rows2_in, 16)
                    sp.dma_start(shift_row[:, b], ln_b[one, :].broadcast_to([P, E])).then_inc(rows2_in, 16)
                    sp.dma_start(bu_row[:, b], up_b[one, :].broadcast_to([P, E])).then_inc(rows2_in, 16)
                out_v = out.rearrange("b (u c p) e -> p (b u) c e", p=P, c=GT)

                def store(g):
                    sp.wait_ge(o_done, START + GT * g + GT)
                    sp.dma_start(out_v[:, bass.ds(g, 1)].rearrange("p u c e -> p (u c) e"), res[:])\
                      .then_inc(o_out, 16)

                sp.wait_ge(x2_out[1], START + 16 * B * NG // 2)
                sp.sem_inc(o_out, START)
                with sp.Fori(0, GROUPS - 1) as g:
                    sp.wait_ge(x3T_mm, KE * g + KE)
                    sp.wait_ge(residual, GT * g + GT)
                    load_group(sp, g + 1)
                    sp.wait_ge(lw_split, 4 * g + 4)
                    load_adapter(sp, g + 1)
                    store(g)
                store(GROUPS - 1)
                sp.wait_ge(o_out, START + 16 * GROUPS)

            @block.tensor
            def _(pe):
                pe.sem_inc(temp_mm, START)
                pe.sem_inc(out_mm, START)
                def split3(acc, wh, wl, xh_, xl_, first=True, last=True):
                    n = len(wh)
                    for k in range(n):
                        pe.matmul(acc, wl[k], xh_[k], start=(first and k == 0), stop=False)
                        pe.matmul(acc, wh[k], xl_[k], start=False, stop=False)
                        ins = pe.matmul(acc, wh[k], xh_[k], start=False, stop=(last and k == n - 1))
                    return ins

                ks = range(KE)

                def x2_transposes(q, g):
                    pe.wait_ge(x2_in, 16 * (q + 1))
                    if g is not None:
                        pe.wait_ge(mod_sig, 2 * g + 2)
                        pe.wait_ge(pre_add, KE * g + 2)
                    for k in ks:
                        for c in range(GT):
                            last = pe.transpose(bank[X2T[k]][:, P * c:P * c + P],
                                                xa[:, c, P * k:P * k + P], ident[:])
                        last.then_inc(x2T_mm, 1)

                def down(q, g):
                    if g is not None:
                        pe.wait_ge(ctx_scan, KE * g + 4)
                    pe.wait_ge(lw_split, 4 * q + 4)
                    pe.wait_ge(x2T_lo, KE * q + KE)
                    split3(bank[DOWN][:], [dw_h[:, k] for k in ks], [dw_l[:, k] for k in ks],
                           [ph[:, k] for k in ks], [pl[:, k] for k in ks]).then_inc(down_mm, 1)

                def up(q):
                    pe.wait_ge(z_lo, q + 1)
                    for c in range(GT):
                        t = slice(P * c, P * c + P)
                        acc = bank[UP[c]][:]
                        split3(acc, [zh[:, t]], [zl[:, t]], [uw_h[:]], [uw_l[:]]).then_inc(up_mm, 1)

                def x3_transposes(q, by_tile=False):
                    if by_tile:
                        order = [(k, c) for c in range(GT) for k in ks]
                    else:
                        order = [(k, c) for k in ks for c in range(GT)]
                        pe.wait_ge(x3_done, GT * q + GT)
                    for k, c in order:
                        if by_tile and k == 0:
                            pe.wait_ge(x3_done, GT * q + c + 1)
                        last = pe.transpose(bank[X3T[k]][:, P * c:P * c + P],
                                            xa[:, c, P * k:P * k + P], ident[:])
                        if c == GT - 1:
                            last.then_inc(x3T_mm, 1)

                def wx(w_h, w_l, off, k):
                    m = slice(P * k, P * k + P)
                    return ([w_h[:, off + i, m] for i in ks], [w_l[:, off + i, m] for i in ks],
                            [xh[:, i] for i in ks], [xl[:, i] for i in ks])

                def front(g):
                    pe.wait_ge(x3T_lo, KE * g + KE)
                    split3(bank[N1][:], [wn1_h[:, i] for i in ks], [wn1_l[:, i] for i in ks],
                           [xh[:, i] for i in ks], [xl[:, i] for i in ks]).then_inc(n1_mm, 1)
                    for k in ks:
                        if k == 1:
                            pe.wait_ge(out_free, START + GT * g)
                        if k == 3:
                            pe.wait_ge(pre_add, KE * g + 1)
                        split3(bank[PRE[k]][:], *wx(wg_h, wg_l, 0, k)).then_inc(pre_mm, 1)
                        if k == 3:
                            pe.wait_ge(ctx_scan, KE * g + 1)
                        split3(bank[CTX[k]][:], *wx(wg_h, wg_l, KE, k)).then_inc(ctx_mm, 1)
                        if k == 0:
                            pe.wait_ge(n1_act, g + 1)
                            for d in range(2):
                                pe.matmul(bank[MOD[d]][:], wn2_rep[:, d], narrow[:], start=True,
                                          stop=True).then_inc(mod_mm, 1)

                def soma_in(g, k):
                    if k == 0:
                        pe.wait_ge(pre_add, KE * g + 3)
                    elif k == 1:
                        pe.wait_ge(ctx_scan, KE * g + 3)
                    elif k == 2:
                        pe.wait_ge(pre_add, KE * g + 4)
                    else:
                        pe.wait_ge(soma_act, KE * g + 1)
                    split3(bank[SOMA[k]][:], *wx(ws_h, ws_l, 0, k)).then_inc(soma_mm, 1)

                def temporal(g):
                    pe.wait_ge(t_lo, KE * g + KE)
                    for k in ks:
                        if k < 2:
                            pe.wait_ge(soma_act, KE * g + k + 2)
                        elif k == 3:
                            pe.wait_ge(soma_act, KE * g + 4)
                        m = slice(P * k, P * k + P)
                        split3(bank[TEMP[k]][:], [wt_h[:, i, m] for i in ks],
                               [wt_l[:, i, m] for i in ks], [th[:, i] for i in ks],
                               [tl[:, i] for i in ks]).then_inc(temp_mm, 1)

                def output_part(c, ki, **flags):
                    t = slice(P * c, P * c + P)
                    return split3(bank[OUT[c]][:], [ph[:, i, t] for i in ki], [pl[:, i, t] for i in ki],
                                  [wo_h[:, i] for i in ki], [wo_l[:, i] for i in ki], **flags)

                def output(g, adapted=True):
                    if adapted:
                        pe.wait_ge(y_add, GT * (g + 1) + GT)
                    for k in range(KE - 1):
                        pe.wait_ge(prod_lo, START + KE * g + k + 1)
                        for c in range(GT - 1):
                            output_part(c, [k], first=(k == 0), last=False)
                    pe.wait_ge(prod_lo, START + KE * g + KE)
                    for c in range(GT - 1):
                        output_part(c, [KE - 1], first=False).then_inc(out_mm, 1)

                def output_rest():
                    output_part(GT - 1, ks).then_inc(out_mm, 1)

                x2_transposes(0, None)
                down(0, None)
                up(0)
                x3_transposes(0, by_tile=True)
                with pe.Fori(0, LAST) as g:
                    front(g)
                    x2_transposes(g + 1, g)
                    soma_in(g, 0)
                    soma_in(g, 1)
                    soma_in(g, 2)
                    down(g + 1, g)
                    soma_in(g, 3)
                    up(g + 1)
                    temporal(g)
                    output(g)
                    x3_transposes(g + 1)
                    output_rest()
                front(LAST)
                for k in ks:
                    soma_in(LAST, k)
                temporal(LAST)
                output(LAST, adapted=False)
                output_rest()

            @block.scalar
            def _(act):
                def x2_halves(q, first=False):
                    if not first:
                        act.wait_ge(out_mm, START + GT * (q - 1))
                    for k in range(KE):
                        act.wait_ge(x2T_mm, KE * q + k + 1)
                        act.activation(ph[:, k], bank[X2T[k]][:], ACT.Copy).then_inc(x2T_hi, 1)

                def relu(q):
                    act.wait_ge(down_mm, q + 1)
                    act.wait_ge(cols_set, q + 1)
                    act.activation(narrow[:], bank[DOWN][:], ACT.Relu,
                                   bias=cols[:, 0:1]).then_inc(z_act, 1)
                    act.wait_ge(z_act, q + 1)
                    act.activation(zh[:], narrow[:], ACT.Copy).then_inc(z_hi, 1)

                def x3_halves(q):
                    act.wait_ge(gated, KE * q)
                    for k in range(KE):
                        act.wait_ge(x3T_mm, KE * q + k + 1)
                        act.activation(xh[:, k], bank[X3T[k]][:], ACT.Identity,
                                       bias=cols[:, 1 + k:2 + k]).then_inc(x3T_hi, 1)

                def sigmoid_gate(g, k):
                    act.wait_ge(pre_add, KE * g + k + 1)
                    act.activation(wgb[:, k % 2], wgb[:, k % 2], ACT.Sigmoid, bias=bias_g[:, k:k + 1])\
                       .then_inc(wg_act, 1)

                def trace_hi(g, k):
                    act.wait_ge(blended, KE * g + k + 1)
                    act.activation(th[:, k], tr[:, k % 2, 1], ACT.Copy).then_inc(t_hi, 1)

                def front(g, adapted=True):
                    act.wait_ge(n1_mm, g + 1)
                    act.activation(narrow[:], bank[N1][:], ACT.Gelu, bias=bias_n1[:]).then_inc(n1_act, 1)
                    sigmoid_gate(g, 0)
                    act.wait_ge(prod_lo, START + KE * g)
                    for d in range(2):
                        act.wait_ge(mod_mm, 2 * g + d + 1)
                        act.activation(wide[:, d], bank[MOD[d]][:], ACT.Sigmoid,
                                       bias=bias_n2[:, d:d + 1]).then_inc(mod_sig, 1)
                    sigmoid_gate(g, 1)
                    act.wait_ge(temp_mm, START + KE * g)
                    sigmoid_gate(g, 2)
                    trace_hi(g, 0)
                    if adapted:
                        x2_halves(g + 1)
                    sigmoid_gate(g, 3)
                    trace_hi(g, 1)
                    soma_gelu(g, 0)

                def soma_gelu(g, k):
                    act.wait_ge(soma_mm, KE * g + k + 1)
                    act.activation(soma[:, k], bank[SOMA[k]][:], ACT.Gelu,
                                   bias=bias_soma[:, k:k + 1]).then_inc(soma_act, 1)

                def gate(g):
                    for k in range(KE):
                        act.wait_ge(temp_mm, START + KE * g + k + 1)
                        if k >= 2:
                            act.wait_ge(prod_lo, START + KE * g + k - 1)
                        act.activation(wide[:, k % 2], bank[TEMP[k]][:], ACT.Sigmoid,
                                       bias=bias_temp[:, k:k + 1]).then_inc(gate_act, 1)
                        if k >= 1:
                            product_hi(g, k - 1)
                    product_hi(g, KE - 1)

                def product_hi(g, k):
                    act.wait_ge(prod, KE * g + k + 1)
                    act.activation(ph[:, k], wide[:, k % 2], ACT.Copy).then_inc(prod_hi, 1)

                x2_halves(0, first=True)
                relu(0)
                x3_halves(0)
                with act.Fori(0, LAST) as g:
                    front(g)
                    trace_hi(g, 2)
                    soma_gelu(g, 1)
                    soma_gelu(g, 2)
                    relu(g + 1)
                    trace_hi(g, 3)
                    soma_gelu(g, 3)
                    gate(g)
                    x3_halves(g + 1)
                front(LAST, adapted=False)
                trace_hi(LAST, 2)
                soma_gelu(LAST, 1)
                soma_gelu(LAST, 2)
                trace_hi(LAST, 3)
                soma_gelu(LAST, 3)
                act.wait_ge(out_mm, START + GT * LAST)
                gate(LAST)

            @block.gpsimd
            def _(po):
                def weights_hi(q):
                    po.wait_ge(lw_in, 32 * (q + 1))
                    po.wait_ge(up_mm, GT * q)
                    po.tensor_tensor(dw_h[:].rearrange("p k a -> p (k a)"), dw_f[:].rearrange("p k a -> p (k a)"),
                                     ONE.broadcast_to([P, KE * A]), ALU.mult).then_inc(lw_split, 1)
                    po.tensor_tensor(uw_h[:], uw_f[:], ONE.broadcast_to([P, E]), ALU.mult).then_inc(lw_split, 1)

                def weights_lo(q):
                    po.wait_ge(lw_split, 4 * q + 2)
                    po.tensor_tensor(dw_l[:], dw_f[:], f32(dw_h[:]), ALU.subtract).then_inc(lw_split, 1)
                    po.tensor_tensor(uw_l[:], uw_f[:], f32(uw_h[:]), ALU.subtract).then_inc(lw_split, 1)

                def add_bias(q):
                    po.wait_ge(x2T_mm, KE * q + KE)
                    for c in range(GT):
                        po.tensor_tensor(xa[:, c], xa[:, c],
                                         bu_row[:, bass.ds(q // NG, 1)].rearrange("p o e -> p (o e)"),
                                         ALU.add).then_inc(bias_add, 1)

                def rstd(mean_ready, mv, rs, n, chain, done, c):
                    po.wait_ge(mean_ready, n + 1)
                    po.tensor_tensor(rs[:, c:c + 1], mv[:, c, 1:2], EPSILON, ALU.add).then_inc(chain, 1)
                    po.wait_ge(chain, n + 1)
                    po.tensor_tensor(rs[:, c:c + 1], rs[:, c:c + 1], NEG_HALF, ALU.pow)\
                      .then_inc(done, 1)

                def resid(g):
                    po.wait_ge(x3_done, GT * g + GT)
                    po.wait_ge(o_out, START + 16 * g)
                    for c in range(GT):
                        po.tensor_tensor(res[:, c], xa[:, c],
                                         shift_row[:, bass.ds(g // NG, 1)].rearrange("p o e -> p (o e)"),
                                         ALU.add).then_inc(residual, 1)

                def front(g, adapted=False):
                    po.wait_ge(x3T_lo, KE * g + KE)
                    for k in range(KE):
                        po.tensor_tensor(soma[:, k], f32(xh[:, k]), f32(xl[:, k]), ALU.add)\
                          .then_inc(xsum_done, 1)
                    po.wait_ge(mod_sig, 2 * g + 2)
                    po.tensor_tensor(wide[:], wide[:], HALF.rearrange("p (o n) -> p o n", o=1).broadcast_to([P, 2, GN]),
                                     ALU.add).then_inc(mod_add, 1)
                    for k in range(KE):
                        if adapted and k == KE - 1:
                            weights_hi(g + 1)
                        po.wait_ge(xsum_done, KE * g + k + 1)
                        po.wait_ge(wg_act, KE * g + k + 1)
                        po.tensor_tensor(wgb[:, k % 2], soma[:, k], wgb[:, k % 2], ALU.mult)\
                          .then_inc(gated, 1)
                        if k == 0:
                            resid(g)
                    if adapted:
                        weights_lo(g + 1)
                        add_bias(g + 1)

                def ln(q, c):
                    rstd(ln_mv, mv_a, rs_a, GT * q + c, ln_p, ln_rs, c)

                def product(g, k):
                    po.wait_ge(gate_act, KE * g + k + 1)
                    po.tensor_tensor(wide[:, k % 2], soma[:, k], wide[:, k % 2], ALU.mult)\
                      .then_inc(prod, 1)

                def out_ln(g):
                    for c in range(GT):
                        rstd(o_mv, mv_o, rs_o, GT * g + c, o_p, o_rs, c)

                weights_hi(0)
                weights_lo(0)
                po.wait_ge(rows2_in, 16 * (2 + 3 * B))
                add_bias(0)
                for c in range(GT):
                    ln(0, c)
                with po.Fori(0, LAST) as g:
                    front(g, adapted=True)
                    ln(g + 1, 0)
                    ln(g + 1, 1)
                    ln(g + 1, 2)
                    product(g, 0)
                    ln(g + 1, 3)
                    product(g, 1)
                    product(g, 2)
                    product(g, 3)
                    out_ln(g)
                front(LAST)
                for k in range(KE):
                    product(LAST, k)
                out_ln(LAST)

            @block.vector
            def _(ve):
                ve.sem_inc(out_free, START)
                ve.sem_inc(prod_lo, START)
                ve.sem_inc(ctx_kept, START)
                ve.sem_inc(o_done, START)
                ve.memset(keep[:], 1.0).then_inc(p2_v, 1)
                ve.memset(carry[:], 0.0).then_inc(p2_v, 1)
                ve.wait_ge(p2_v, 2)
                for b in range(B):
                    last = (b + 1) * NG - 1
                    ve.memset(keep[:, last:last + 1], 0.0).then_inc(p2_v, 1)
                ve.wait_ge(p2_v, 2 + B)

                def set_cols(q):
                    ve.wait_ge(x3T_lo, KE * q)
                    ve.tensor_scalar(cols[:], cols_all[:, bass.ds(q // NG, 1)].rearrange("p o c -> p (o c)"),
                                     1.0, None, ALU.mult).then_inc(cols_set, 1)

                def x2_lo(q):
                    for k in range(KE):
                        ve.wait_ge(x2T_hi, KE * q + k + 1)
                        ve.tensor_tensor(pl[:, k], bank[X2T[k]][:], f32(ph[:, k]), ALU.subtract)\
                          .then_inc(x2T_lo, 1)

                def relu_lo(q):
                    ve.wait_ge(z_hi, q + 1)
                    ve.tensor_tensor(zl[:], narrow[:], f32(zh[:]), ALU.subtract).then_inc(z_lo, 1)

                def moments(acc, st, mv, c, done):
                    ve.bn_stats(st[:, c], acc)
                    ve.drain()
                    ve.bn_aggr(mv[:, c], st[:, c]).then_inc(done, 1)

                def ln_stats(q, c):
                    ve.wait_ge(bias_add, GT * q + c + 1)
                    y = tr[:, c % 2, 0]
                    ve.wait_ge(up_mm, GT * q + c + 1)
                    if c >= 2:
                        ve.wait_ge(x3_done, GT * q + c - 1)
                    ve.tensor_tensor(y, bank[UP[c]][:], xa[:, c], ALU.add).then_inc(y_add, 1)
                    ve.wait_ge(y_add, GT * q + c + 1)
                    moments(y, st_a, mv_a, c, ln_mv)

                def ln_apply(q, c):
                    y = tr[:, c % 2, 0]
                    ve.wait_ge(ln_mv, GT * q + c + 1)
                    ve.scalar_tensor_tensor(
                        y, y, mv_a[:, c, 0:1],
                        ln_g_row[:, bass.ds(q // NG, 1)].rearrange("p o e -> p (o e)"),
                        ALU.subtract, ALU.mult).then_inc(ln_w, 1)
                    ve.wait_ge(ln_w, GT * q + c + 1)
                    ve.wait_ge(ln_rs, GT * q + c + 1)
                    ve.scalar_tensor_tensor(xa[:, c], y, rs_a[:, c:c + 1], xa[:, c], ALU.mult, ALU.add)\
                      .then_inc(x3_done, 1)

                def x3_lo(q):
                    for k in range(KE):
                        ve.wait_ge(x3T_hi, KE * q + k + 1)
                        ve.scalar_tensor_tensor(xl[:, k], bank[X3T[k]][:],
                                                cols[:, 1 + k:2 + k], f32(xh[:, k]),
                                                ALU.add, ALU.subtract).then_inc(x3T_lo, 1)

                def logits(g, k):
                    w = wgb[:, k % 2]
                    h = tr[:, k % 2, 0]
                    if k >= 2:
                        ve.wait_ge(blended, KE * g + k - 1)
                    else:
                        ve.wait_ge(o_done, START + GT * g)
                    ve.wait_ge(ctx_mm, KE * g + k + 1)
                    ve.wait_ge(ctx_kept, START + KE * g + k)
                    ve.tensor_tensor_scan(h, alpha[:, 0:1].broadcast_to([P, GN]), bank[CTX[k]][:],
                                          carry[:, k, 0:1], ALU.mult, ALU.add).then_inc(ctx_scan, 1)
                    ve.wait_ge(ctx_scan, KE * g + k + 1)
                    ve.tensor_scalar(carry[:, k, 0:1], h[:, GN - 1:GN], keep[:, bass.ds(g, 1)], None,
                                     ALU.mult).then_inc(ctx_kept, 1)
                    ve.wait_ge(pre_mm, KE * g + k + 1)
                    ve.tensor_tensor(w, bank[PRE[k]][:], h, ALU.add).then_inc(pre_add, 1)

                def traces(g, k):
                    t = tr[:, k % 2]
                    if k == 0:
                        ve.wait_ge(mod_add, g + 1)
                    if k >= 2:
                        ve.wait_ge(t_lo, KE * g + k - 1)
                    ve.wait_ge(ctx_kept, START + KE * g + k + 1)
                    ve.wait_ge(gated, KE * g + k + 1)
                    for d in range(2):
                        ve.scalar_tensor_tensor(t[:, d], wgb[:, k % 2], blend_w[:, d, k:k + 1],
                                                wide[:, d], ALU.mult, ALU.mult).then_inc(tr_in, 1)
                    for d in range(2):
                        ve.wait_ge(tr_in, 2 * (KE * g + k) + d + 1)
                        ve.tensor_tensor_scan(t[:, d], alpha[:, 1 + d:2 + d].broadcast_to([P, GN]),
                                              t[:, d], carry[:, k, 1 + d:2 + d], ALU.mult, ALU.add)\
                          .then_inc(tr_scan, 1)
                    ve.wait_ge(tr_scan, 2 * (KE * g + k + 1))
                    ve.tensor_scalar(carry[:, k, 1:3], t[:, :, GN - 1], keep[:, bass.ds(g, 1)], None,
                                     ALU.mult).then_inc(carried, 1)
                    ve.wait_ge(carried, KE * g + k + 1)
                    ve.tensor_tensor(t[:, 1], t[:, 0], t[:, 1], ALU.add).then_inc(blended, 1)

                def trace_lo(g, k):
                    ve.wait_ge(t_hi, KE * g + k + 1)
                    ve.tensor_tensor(tl[:, k], tr[:, k % 2, 1], f32(th[:, k]), ALU.subtract)\
                      .then_inc(t_lo, 1)

                def front(g, adapted=True):
                    logits(g, 0)
                    logits(g, 1)
                    traces(g, 0)
                    logits(g, 2)
                    traces(g, 1)
                    trace_lo(g, 0)
                    logits(g, 3)
                    traces(g, 2)
                    trace_lo(g, 1)
                    if adapted:
                        x2_lo(g + 1)
                    traces(g, 3)
                    trace_lo(g, 2)
                    if adapted:
                        relu_lo(g + 1)
                    trace_lo(g, 3)

                def product_lo(g, k):
                    ve.wait_ge(prod_hi, KE * g + k + 1)
                    ve.tensor_tensor(pl[:, k], wide[:, k % 2], f32(ph[:, k]), ALU.subtract)\
                      .then_inc(prod_lo, 1)

                def out_stats(g, c):
                    ve.wait_ge(out_mm, START + GT * g + c + 1)
                    moments(bank[OUT[c]][:], st_o, mv_o, c, o_mv)

                def out_apply(g, c):
                    t = tr[:, c % 2, 0]
                    ve.wait_ge(o_mv, GT * g + c + 1)
                    ve.scalar_tensor_tensor(t, bank[OUT[c]][:], mv_o[:, c, 0:1], gamma_row[:],
                                            ALU.subtract, ALU.mult).then_inc(out_free, 1)
                    ve.wait_ge(out_free, START + GT * g + c + 1)
                    ve.wait_ge(o_rs, GT * g + c + 1)
                    ve.scalar_tensor_tensor(res[:, c], t, rs_o[:, c:c + 1], res[:, c], ALU.mult,
                                            ALU.add).then_inc(o_done, 1)

                def output(g, adapted=True):
                    ve.wait_ge(residual, GT * g + GT)
                    if adapted:
                        ve.wait_ge(x3_done, GT * (g + 1) + GT)
                    out_stats(g, 0)
                    out_stats(g, 1)
                    if adapted:
                        x3_lo(g + 1)
                    out_stats(g, 2)
                    out_apply(g, 0)
                    out_apply(g, 1)
                    out_stats(g, 3)
                    out_apply(g, 2)
                    out_apply(g, 3)

                set_cols(0)
                x2_lo(0)
                ve.wait_ge(rows2_in, 16 * (2 + 3 * B))
                for b in range(B):
                    ve.tensor_tensor(shift_row[:, b], shift_row[:, b], bu_row[:, b], ALU.subtract)\
                      .then_inc(p2_v, 1)
                ve.wait_ge(p2_v, 2 + 2 * B)
                for b in range(B):
                    ve.tensor_tensor(shift_row[:, b], shift_row[:, b], wgb[:, 0], ALU.add).then_inc(p2_v, 1)
                ve.wait_ge(p2_v, 2 + 3 * B)
                relu_lo(0)
                ln_stats(0, 0)
                for c in range(1, GT):
                    ln_stats(0, c)
                    ln_apply(0, c - 1)
                ln_apply(0, GT - 1)
                x3_lo(0)
                with ve.Fori(0, LAST) as g:
                    set_cols(g + 1)
                    front(g)
                    ln_stats(g + 1, 0)
                    ln_stats(g + 1, 1)
                    ln_apply(g + 1, 0)
                    ln_stats(g + 1, 2)
                    ln_apply(g + 1, 1)
                    ln_stats(g + 1, 3)
                    ln_apply(g + 1, 2)
                    product_lo(g, 0)
                    ln_apply(g + 1, 3)
                    for k in range(1, KE):
                        product_lo(g, k)
                    output(g)
                front(LAST, adapted=False)
                for k in range(KE):
                    product_lo(LAST, k)
                output(LAST, adapted=False)


def kernel(**inputs):
    import numpy as np
    import concourse.bacc as bacc
    from concourse.bass_utils import run_bass_kernel_spmd

    i = {k: np.asarray(a) for k, a in inputs.items()}
    flip = lambda a: np.ascontiguousarray(a.T)
    arrays = {
        "x": i["x"],
        "xT": np.ascontiguousarray(i["x"].transpose(0, 2, 1)),
        "ptype": i["itok_B_0_2"],
        "zx": i["condB_zX"],
        "zy": i["condB_zY"],
        "zr": i["condB_zR"],
        "profile": i["itok_B_0_6"],
        "tau_raws": i["condB_tauraws"],
        "wn2": i["cond_256"],
        "bn2": i["condB_bn2"],
        "blend": i["cond_1024"],
        "w1": i["L0_cond_W1"],
        "b1": i["L0_cond_b1"],
        "v": i["L0_cond_v"],
        "down_w": i["L2_cond_down_w"],
        "down_b": i["L2_cond_down_b"],
        "up_w": i["L2_cond_up_w"],
        "up_b": i["L2_cond_up_b"],
        "ln_g": i["L2_cond_ln_g"],
        "ln_b": i["L2_cond_ln_b"],
        "tau_ctx": i["L3_cond_tau_ctx"].reshape(1),
        "wg": flip(i["L3_cond_Wg"]),
        "bg": i["L3_cond_bg"],
        "wn1": flip(i["L3_cond_Wn1"]),
        "bn1": i["L3_cond_bn1"],
        "wsoma": flip(i["L3_cond_Wsoma"]),
        "bsoma": i["L3_cond_bsoma"],
        "wtemp": flip(i["L3_cond_Wtemp"]),
        "btemp": i["L3_cond_btemp"],
        "wout": flip(i["L3_cond_Wout"]),
        "gamma": i["L3_cond_gamma"],
        "beta": i["L3_cond_beta"],
    }
    arrays = {k: np.ascontiguousarray(a) for k, a in arrays.items()}
    nc = bacc.Bacc("TRN2", target_bir_lowering=False, num_devices=1)
    args = {k: nc.dram_tensor(f"in_{k}", a.shape, mybir.dt.from_np(a.dtype), kind="ExternalInput").ap()
            for k, a in arrays.items()}
    args["out"] = nc.dram_tensor("result", (B, T, E), F32, kind="ExternalOutput").ap()
    build_program(nc, **args)
    r = run_bass_kernel_spmd(nc, [{f"in_{k}": a for k, a in arrays.items()}], core_ids=[0])
    return r.results[0]["result"]
```
